# Optimizing a Trainium2 kernel written in Bass

```python
import numpy as np
import jax
import jax.numpy as jnp

def _softmax(x, axis=-1):
    return jax.nn.softmax(x, axis=axis)

def _gelu(x):
    return jax.nn.gelu(x, approximate=True)

def _silu(x):
    return jax.nn.silu(x)

def _sigmoid(x):
    return jax.nn.sigmoid(x)

def _layernorm(x, axis=-1, eps=1e-05):
    m = jnp.mean(x, axis=axis, keepdims=True)
    v = jnp.var(x, axis=axis, keepdims=True)
    return (x - m) / jnp.sqrt(v + eps)

def _scatter_add(tgt, idx, src, axis=0):
    return tgt.at[idx].add(src)

def _segment_sum(src, seg, n):
    return jax.ops.segment_sum(src, seg, n)
kernel_name = 'mk_gps_d1_gnn_r32_4b149e'

def setup_inputs(seed: int=0):
    np.random.seed(seed)
    _w = jnp.asarray

    def _rec_inputs():
        import jax
        import jax.numpy as jnp
        _gk = jax.random.key(seed)
        x = -0.0003713 + 1 * jax.random.normal(jax.random.fold_in(_gk, 1), (3125, 256), jnp.float32)
        _s = jax.random.randint(jax.random.fold_in(_gk, 2), (25000,), 0, 3125, jnp.int32)
        _d = jax.random.randint(jax.random.fold_in(_gk, 3), (25000,), 0, 3125, jnp.int32)
        _loop = jnp.arange(3125, dtype=jnp.int32)
        src = jnp.concatenate([_s, _d, _loop])
        dst = jnp.concatenate([_d, _s, _loop])
        _o = jnp.argsort(dst, stable=True)
        src = src[_o]
        dst = dst[_o]
        edge_type_400 = jax.random.randint(jax.random.fold_in(_gk, 12), (53125,), 0, 400, jnp.int32)
        return (x, src, dst, edge_type_400)
    x, src, dst, edge_type_400 = _rec_inputs()

    def _L0_gnn_setup():
        import jax, jax.numpy as jnp
        import numpy as np
        N = 50000
        D = 256
        E = 10000
        R = 400

        def _mgcn_conv(x, edge_index, edge_type, rel, W_in, W_out, W_loop, b, n):
            src, dst = (edge_index[0], edge_index[1])
            e = edge_index.shape[1]
            half = e // 2
            m = x[src] * rel[edge_type]
            m = jnp.concatenate([m[:half] @ W_in, m[half:] @ W_out], 0)
            deg = jax.ops.segment_sum(jnp.ones((e,), x.dtype), dst, num_segments=n)
            norm = 1.0 / jnp.maximum(deg, 1.0)
            agg = jax.ops.segment_sum(m * norm[dst][:, None], dst, num_segments=n)
            return jnp.tanh(agg + x @ W_loop + b)
        key = jax.random.key(seed)
        ks = jax.random.split(key, 12)
        s = 0.05
        w = lambda k, shp: jax.random.normal(k, shp, jnp.float32) * s
        return {'emb': jax.random.normal(ks[0], (N, D), jnp.float32), 'edge_index': jax.random.randint(ks[1], (2, E), 0, N), 'edge_type': jax.random.randint(ks[2], (E,), 0, R), 'rel1': w(ks[3], (R, D)), 'W_in1': w(ks[4], (D, D)), 'W_out1': w(ks[5], (D, D)), 'W_loop1': w(ks[6], (D, D)), 'b1': jnp.zeros((D,), jnp.float32), 'rel2': w(ks[7], (R, D)), 'W_in2': w(ks[8], (D, D)), 'W_out2': w(ks[9], (D, D)), 'W_loop2': w(ks[10], (D, D)), 'b2': jnp.zeros((D,), jnp.float32), 'res': jnp.array([0.1], jnp.float32), 'mu_w': w(ks[11], (D, D)), 'mu_b': jnp.zeros((D,), jnp.float32), 'num_nodes': N}
    _L0_gnn_all = _L0_gnn_setup()
    _L0_gnn_in = {k: v for k, v in _L0_gnn_all.items() if k in ('rel1', 'W_in1', 'W_out1', 'W_loop1', 'b1', 'rel2', 'W_in2', 'W_out2', 'W_loop2', 'b2', 'res', 'mu_w', 'mu_b')}
    del _L0_gnn_all

    def _L0_mix_setup():
        import jax, jax.numpy as jnp
        import numpy as np
        EMB, HEADS, DEPTH, SEQ, BATCH = (256, 8, 4, 256, 4)
        DH = EMB // HEADS
        FF = 4 * EMB
        EPS = 1e-05

        def _layernorm(x, g, b):
            mu = x.mean(-1, keepdims=True)
            var = ((x - mu) ** 2).mean(-1, keepdims=True)
            return (x - mu) * jax.lax.rsqrt(var + EPS) * g + b

        def _linear_attn(x, Wq, Wk, Wv, Wo, bo):
            b, n, dm = x.shape
            split = lambda t: t.reshape(b, n, HEADS, DH).transpose(0, 2, 1, 3)
            scale = DH ** (-0.25)
            q = jax.nn.softmax(split(x @ Wq) * scale, axis=-1)
            k = jax.nn.softmax(split(x @ Wk) * scale, axis=-2)
            v = split(x @ Wv)
            context = jnp.einsum('bhnd,bhne->bhde', k, v)
            out = jnp.einsum('bhnd,bhde->bhne', q, context)
            out = out.transpose(0, 2, 1, 3).reshape(b, n, dm)
            return out @ Wo + bo

        def _forward(x, Wq, Wk, Wv, Wo, bo, ln1_g, ln1_b, W1, b1, W2, b2, ln2_g, ln2_b):
            for i in range(DEPTH):
                h = _layernorm(x, ln1_g[i], ln1_b[i])
                x = x + _linear_attn(h, Wq[i], Wk[i], Wv[i], Wo[i], bo[i])
                h = _layernorm(x, ln2_g[i], ln2_b[i])
                x = x + (jax.nn.gelu(h @ W1[i] + b1[i], approximate=False) @ W2[i] + b2[i])
            return x
        key = jax.random.key(seed)
        ks = jax.random.split(key, 8)
        w = lambda k, shape: jax.random.normal(k, shape, dtype=jnp.float32) * 0.02
        D = DEPTH
        return {'x': jax.random.normal(ks[0], (BATCH, SEQ, EMB), dtype=jnp.float32), 'Wq': w(ks[1], (D, EMB, EMB)), 'Wk': w(ks[2], (D, EMB, EMB)), 'Wv': w(ks[3], (D, EMB, EMB)), 'Wo': w(ks[4], (D, EMB, EMB)), 'bo': jnp.zeros((D, EMB), jnp.float32), 'ln1_g': jnp.ones((D, EMB), jnp.float32), 'ln1_b': jnp.zeros((D, EMB), jnp.float32), 'W1': w(ks[5], (D, EMB, FF)), 'b1': jnp.zeros((D, FF), jnp.float32), 'W2': w(ks[6], (D, FF, EMB)), 'b2': jnp.zeros((D, EMB), jnp.float32), 'ln2_g': jnp.ones((D, EMB), jnp.float32), 'ln2_b': jnp.zeros((D, EMB), jnp.float32)}
    _L0_mix_all = _L0_mix_setup()
    _L0_mix_in = {k: v for k, v in _L0_mix_all.items() if k in ('Wq', 'Wk', 'Wv', 'Wo', 'bo', 'ln1_g', 'ln1_b', 'W1', 'b1', 'W2', 'b2', 'ln2_g', 'ln2_b')}
    del _L0_mix_all

    def _L0_ffn_setup():
        import jax, jax.numpy as jnp
        import numpy as np
        B, A = (128, 8)
        IN, OUT = (256, 256)
        SH1, SH2 = (256, 128)
        EH1, EH2 = (128, 64)
        E, TOPK = (4, 2)

        def _shared_mlp(x, W1, b1, W2, b2, W3, b3):
            h = jax.nn.relu(x @ W1 + b1)
            h = jax.nn.relu(h @ W2 + b2)
            return h @ W3 + b3

        def _experts_mlp(x, eW1, eb1, eW2, eb2, eW3, eb3):
            h = jax.nn.relu(jnp.einsum('baf,efh->ebah', x, eW1) + eb1[:, None, None, :])
            h = jax.nn.relu(jnp.einsum('ebah,ehg->ebag', h, eW2) + eb2[:, None, None, :])
            o = jnp.einsum('ebag,ego->ebao', h, eW3) + eb3[:, None, None, :]
            return jnp.moveaxis(o, 0, -1)
        key = jax.random.key(seed)
        ks = jax.random.split(key, 16)
        s = 0.05
        return {'x': jax.random.normal(ks[0], (B, A, IN), jnp.float32), 'sW1': jax.random.normal(ks[1], (IN, SH1), jnp.float32) * s, 'sb1': jnp.zeros((SH1,), jnp.float32), 'sW2': jax.random.normal(ks[2], (SH1, SH2), jnp.float32) * s, 'sb2': jnp.zeros((SH2,), jnp.float32), 'sW3': jax.random.normal(ks[3], (SH2, OUT), jnp.float32) * s, 'sb3': jnp.zeros((OUT,), jnp.float32), 'eW1': jax.random.normal(ks[4], (E, IN, EH1), jnp.float32) * s, 'eb1': jnp.zeros((E, EH1), jnp.float32), 'eW2': jax.random.normal(ks[5], (E, EH1, EH2), jnp.float32) * s, 'eb2': jnp.zeros((E, EH2), jnp.float32), 'eW3': jax.random.normal(ks[6], (E, EH2, OUT), jnp.float32) * s, 'eb3': jnp.zeros((E, OUT), jnp.float32), 'gW': jax.random.normal(ks[7], (IN, E), jnp.float32) * s, 'gb': jnp.zeros((E,), jnp.float32)}
    _L0_ffn_all = _L0_ffn_setup()
    _L0_ffn_in = {k: v for k, v in _L0_ffn_all.items() if k in ('sW1', 'sb1', 'sW2', 'sb2', 'sW3', 'sb3', 'eW1', 'eb1', 'eW2', 'eb2', 'eW3', 'eb3', 'gW', 'gb')}
    del _L0_ffn_all
    return {'x': x, 'src': src, 'dst': dst, 'edge_type_400': edge_type_400, 'L0_gnn_rel1': _L0_gnn_in['rel1'], 'L0_gnn_W_in1': _L0_gnn_in['W_in1'], 'L0_gnn_W_out1': _L0_gnn_in['W_out1'], 'L0_gnn_W_loop1': _L0_gnn_in['W_loop1'], 'L0_gnn_b1': _L0_gnn_in['b1'], 'L0_gnn_rel2': _L0_gnn_in['rel2'], 'L0_gnn_W_in2': _L0_gnn_in['W_in2'], 'L0_gnn_W_out2': _L0_gnn_in['W_out2'], 'L0_gnn_W_loop2': _L0_gnn_in['W_loop2'], 'L0_gnn_b2': _L0_gnn_in['b2'], 'L0_gnn_res': _L0_gnn_in['res'], 'L0_gnn_mu_w': _L0_gnn_in['mu_w'], 'L0_gnn_mu_b': _L0_gnn_in['mu_b'], 'L0_mix_Wq': _L0_mix_in['Wq'], 'L0_mix_Wk': _L0_mix_in['Wk'], 'L0_mix_Wv': _L0_mix_in['Wv'], 'L0_mix_Wo': _L0_mix_in['Wo'], 'L0_mix_bo': _L0_mix_in['bo'], 'L0_mix_ln1_g': _L0_mix_in['ln1_g'], 'L0_mix_ln1_b': _L0_mix_in['ln1_b'], 'L0_mix_W1': _L0_mix_in['W1'], 'L0_mix_b1': _L0_mix_in['b1'], 'L0_mix_W2': _L0_mix_in['W2'], 'L0_mix_b2': _L0_mix_in['b2'], 'L0_mix_ln2_g': _L0_mix_in['ln2_g'], 'L0_mix_ln2_b': _L0_mix_in['ln2_b'], 'L0_ffn_sW1': _L0_ffn_in['sW1'], 'L0_ffn_sb1': _L0_ffn_in['sb1'], 'L0_ffn_sW2': _L0_ffn_in['sW2'], 'L0_ffn_sb2': _L0_ffn_in['sb2'], 'L0_ffn_sW3': _L0_ffn_in['sW3'], 'L0_ffn_sb3': _L0_ffn_in['sb3'], 'L0_ffn_eW1': _L0_ffn_in['eW1'], 'L0_ffn_eb1': _L0_ffn_in['eb1'], 'L0_ffn_eW2': _L0_ffn_in['eW2'], 'L0_ffn_eb2': _L0_ffn_in['eb2'], 'L0_ffn_eW3': _L0_ffn_in['eW3'], 'L0_ffn_eb3': _L0_ffn_in['eb3'], 'L0_ffn_gW': _L0_ffn_in['gW'], 'L0_ffn_gb': _L0_ffn_in['gb']}

def reference(x, src, dst, edge_type_400, L0_gnn_rel1, L0_gnn_W_in1, L0_gnn_W_out1, L0_gnn_W_loop1, L0_gnn_b1, L0_gnn_rel2, L0_gnn_W_in2, L0_gnn_W_out2, L0_gnn_W_loop2, L0_gnn_b2, L0_gnn_res, L0_gnn_mu_w, L0_gnn_mu_b, L0_mix_Wq, L0_mix_Wk, L0_mix_Wv, L0_mix_Wo, L0_mix_bo, L0_mix_ln1_g, L0_mix_ln1_b, L0_mix_W1, L0_mix_b1, L0_mix_W2, L0_mix_b2, L0_mix_ln2_g, L0_mix_ln2_b, L0_ffn_sW1, L0_ffn_sb1, L0_ffn_sW2, L0_ffn_sb2, L0_ffn_sW3, L0_ffn_sb3, L0_ffn_eW1, L0_ffn_eb1, L0_ffn_eW2, L0_ffn_eb2, L0_ffn_eW3, L0_ffn_eb3, L0_ffn_gW, L0_ffn_gb):
    import jax
    import jax.numpy as jnp

    def _L0_gnn_ref(emb, edge_index, edge_type, rel1, W_in1, W_out1, W_loop1, b1, rel2, W_in2, W_out2, W_loop2, b2, res, mu_w, mu_b, num_nodes):
        import jax, jax.numpy as jnp
        import numpy as np
        N = 50000
        D = 256
        E = 10000
        R = 400

        def _mgcn_conv(x, edge_index, edge_type, rel, W_in, W_out, W_loop, b, n):
            src, dst = (edge_index[0], edge_index[1])
            e = edge_index.shape[1]
            half = e // 2
            m = x[src] * rel[edge_type]
            m = jnp.concatenate([m[:half] @ W_in, m[half:] @ W_out], 0)
            deg = jax.ops.segment_sum(jnp.ones((e,), x.dtype), dst, num_segments=n)
            norm = 1.0 / jnp.maximum(deg, 1.0)
            agg = jax.ops.segment_sum(m * norm[dst][:, None], dst, num_segments=n)
            return jnp.tanh(agg + x @ W_loop + b)
        h = emb + res * _mgcn_conv(emb, edge_index, edge_type, rel1, W_in1, W_out1, W_loop1, b1, num_nodes)
        h = h + res * _mgcn_conv(h, edge_index, edge_type, rel2, W_in2, W_out2, W_loop2, b2, num_nodes)
        return h @ mu_w + mu_b

    def _L0_mix_ref(x, Wq, Wk, Wv, Wo, bo, ln1_g, ln1_b, W1, b1, W2, b2, ln2_g, ln2_b):
        import jax, jax.numpy as jnp
        import numpy as np
        EMB, HEADS, DEPTH, SEQ, BATCH = (256, 8, 4, 256, 4)
        DH = EMB // HEADS
        FF = 4 * EMB
        EPS = 1e-05

        def _layernorm(x, g, b):
            mu = x.mean(-1, keepdims=True)
            var = ((x - mu) ** 2).mean(-1, keepdims=True)
            return (x - mu) * jax.lax.rsqrt(var + EPS) * g + b

        def _linear_attn(x, Wq, Wk, Wv, Wo, bo):
            b, n, dm = x.shape
            split = lambda t: t.reshape(b, n, HEADS, DH).transpose(0, 2, 1, 3)
            scale = DH ** (-0.25)
            q = jax.nn.softmax(split(x @ Wq) * scale, axis=-1)
            k = jax.nn.softmax(split(x @ Wk) * scale, axis=-2)
            v = split(x @ Wv)
            context = jnp.einsum('bhnd,bhne->bhde', k, v)
            out = jnp.einsum('bhnd,bhde->bhne', q, context)
            out = out.transpose(0, 2, 1, 3).reshape(b, n, dm)
            return out @ Wo + bo

        def _forward(x, Wq, Wk, Wv, Wo, bo, ln1_g, ln1_b, W1, b1, W2, b2, ln2_g, ln2_b):
            for i in range(DEPTH):
                h = _layernorm(x, ln1_g[i], ln1_b[i])
                x = x + _linear_attn(h, Wq[i], Wk[i], Wv[i], Wo[i], bo[i])
                h = _layernorm(x, ln2_g[i], ln2_b[i])
                x = x + (jax.nn.gelu(h @ W1[i] + b1[i], approximate=False) @ W2[i] + b2[i])
            return x
        return _forward(x, Wq, Wk, Wv, Wo, bo, ln1_g, ln1_b, W1, b1, W2, b2, ln2_g, ln2_b)

    def _L0_ffn_ref(x, sW1, sb1, sW2, sb2, sW3, sb3, eW1, eb1, eW2, eb2, eW3, eb3, gW, gb):
        import jax, jax.numpy as jnp
        import numpy as np
        B, A = (128, 8)
        IN, OUT = (256, 256)
        SH1, SH2 = (256, 128)
        EH1, EH2 = (128, 64)
        E, TOPK = (4, 2)

        def _shared_mlp(x, W1, b1, W2, b2, W3, b3):
            h = jax.nn.relu(x @ W1 + b1)
            h = jax.nn.relu(h @ W2 + b2)
            return h @ W3 + b3

        def _experts_mlp(x, eW1, eb1, eW2, eb2, eW3, eb3):
            h = jax.nn.relu(jnp.einsum('baf,efh->ebah', x, eW1) + eb1[:, None, None, :])
            h = jax.nn.relu(jnp.einsum('ebah,ehg->ebag', h, eW2) + eb2[:, None, None, :])
            o = jnp.einsum('ebag,ego->ebao', h, eW3) + eb3[:, None, None, :]
            return jnp.moveaxis(o, 0, -1)
        all_out = _experts_mlp(x, eW1, eb1, eW2, eb2, eW3, eb3)
        shared = _shared_mlp(x, sW1, sb1, sW2, sb2, sW3, sb3)
        gates = jax.nn.softmax(x @ gW + gb, axis=-1)
        topv, topi = jax.lax.top_k(gates, TOPK)
        topw = jax.nn.softmax(topv, axis=-1)
        sel = jnp.take_along_axis(all_out, topi[:, :, None, :], axis=-1)
        gated = jnp.sum(sel * topw[:, :, None, :], axis=-1)
        return shared + gated
    edge_index = jnp.stack([src, dst])
    xn = _layernorm(x, axis=-1)
    x = x + _L0_gnn_ref(xn, edge_index, edge_type_400, L0_gnn_rel1, L0_gnn_W_in1, L0_gnn_W_out1, L0_gnn_W_loop1, L0_gnn_b1, L0_gnn_rel2, L0_gnn_W_in2, L0_gnn_W_out2, L0_gnn_W_loop2, L0_gnn_b2, L0_gnn_res, L0_gnn_mu_w, L0_gnn_mu_b, 3125) + _L0_mix_ref(xn[None], L0_mix_Wq, L0_mix_Wk, L0_mix_Wv, L0_mix_Wo, L0_mix_bo, L0_mix_ln1_g, L0_mix_ln1_b, L0_mix_W1, L0_mix_b1, L0_mix_W2, L0_mix_b2, L0_mix_ln2_g, L0_mix_ln2_b)[0]
    x = x + _L0_ffn_ref(_layernorm(x, axis=-1)[None], L0_ffn_sW1, L0_ffn_sb1, L0_ffn_sW2, L0_ffn_sb2, L0_ffn_sW3, L0_ffn_sb3, L0_ffn_eW1, L0_ffn_eb1, L0_ffn_eW2, L0_ffn_eb2, L0_ffn_eW3, L0_ffn_eb3, L0_ffn_gW, L0_ffn_gb)[0]
    return x

_drawn_inputs = setup_inputs


def setup_inputs(seed=0):
    import zlib

    import numpy as np

    out = dict(_drawn_inputs(seed))
    spreads = {'L0_gnn_b1': (0.0, 2.0),
     'L0_gnn_b2': (0.0, 2.0),
     'L0_gnn_mu_b': (0.0, 0.1),
     'L0_mix_bo': (0.0, 0.1),
     'L0_mix_ln1_g': (1.0, 0.6),
     'L0_mix_ln1_b': (0.0, 0.8),
     'L0_mix_b1': (0.0, 0.1),
     'L0_mix_b2': (0.0, 0.1),
     'L0_mix_ln2_g': (1.0, 0.6),
     'L0_mix_ln2_b': (0.0, 0.709),
     'L0_ffn_sb1': (0.0, 0.8),
     'L0_ffn_sb2': (0.0, 0.42),
     'L0_ffn_sb3': (0.0, 0.1),
     'L0_ffn_eb1': (0.0, 2.0),
     'L0_ffn_eb2': (0.0, 0.8),
     'L0_ffn_eb3': (0.0, 0.361),
     'L0_ffn_gb': (0.0, 0.776)}
    factors = {'L0_gnn_rel1': 56.482,
     'L0_gnn_W_in1': 64.0,
     'L0_gnn_W_out1': 64.0,
     'L0_gnn_W_loop1': 7.37,
     'L0_gnn_rel2': 56.943,
     'L0_gnn_W_in2': 64.0,
     'L0_gnn_W_out2': 64.0,
     'L0_gnn_W_loop2': 7.484,
     'L0_mix_Wq': 8.0,
     'L0_mix_Wk': 8.0,
     'L0_mix_Wv': 3.086,
     'L0_mix_Wo': 2.88,
     'L0_ffn_eW1': 2.836}
    for name, (base, spread) in spreads.items():
        noise = np.random.default_rng([zlib.crc32(name.encode()), seed]).standard_normal(out[name].shape)
        drawn = base * np.exp(spread * noise) if base else spread * noise
        out[name] = jnp.asarray(drawn.astype(out[name].dtype))
    for name, factor in factors.items():
        out[name] = (out[name] * factor).astype(out[name].dtype)
    return out
```

```python
from contextlib import ExitStack

import numpy as np

import concourse.bass as bass
from concourse import mybir

F32 = mybir.dt.float32
I32 = mybir.dt.int32
ALU = mybir.AluOpType
ACT = mybir.ActivationFunctionType
AX = mybir.AxisListType.X
ds = bass.ds

P = 128
D = 256
KC = D // P
T = 125
GT = 5
HEADS, DH = 8, 32
EPS = 1e-5
RSQRT_SEED = float(0x5F3759DF)
FAR = 65536.0
RING = 8
QUAD = 4
STEPS_A, STEPS_C0, STEPS_C, STEPS_B0, STEPS_B = 8, 8, 16, 8, 16


def build(nc, io, out):
    N = io["x"].shape[0]
    E = io["src"].shape[0]
    L, _, FF = io["L0_mix_W1"].shape
    FC = FF // P
    NT = N // T
    NG = NT // GT
    ET = E // T
    HALF = E // 2
    HT = -(-HALF // T)
    SPLIT = HALF // T
    SPLIT_COL = HALF % T
    assert ET - SPLIT == HT and T * NT == N and T * ET == E
    AT_C0 = NG * STEPS_A
    AT_C = AT_C0 + STEPS_C0
    AT_B0 = AT_C + NG * STEPS_C
    AT_B = AT_B0 + STEPS_B0
    STEPS = AT_B + NG * STEPS_B
    assert all(n % RING == 0 for n in (STEPS_A, STEPS_C0, STEPS_C, STEPS_B0, STEPS_B)) and RING % QUAD == 0
    assert STEPS >= HT
    QUADS = STEPS // QUAD
    SCH = STEPS // 2
    assert SCH % QUAD == 0
    CHUNKS = (0, SCH, SPLIT, SPLIT + SCH)
    NX = io["L0_ffn_eW1"].shape[0]
    EH2 = io["L0_ffn_eW2"].shape[2]
    GL = 2
    SCALE = float(DH) ** -0.25
    AW = D + 1
    assert L == 2 * GL
    PD_ROWS, PD_FALLS, PD_KEYS = 6, 21, 50
    PAIR_ROWS = max(r for r in range(1, P + 1) if (E - 1) % r == 0)
    PAIRS = (E - 1) // PAIR_ROWS
    GTILES = 2 * HT
    KM_STEPS = NT + 4
    ED_STEPS = 64
    LAST_LOADS = 15 + NX

    xn_d = nc.dram_tensor("xn_rows", [N, D], F32, kind="Internal").ap()
    h1_d = nc.dram_tensor("h1_rows", [N, D], F32, kind="Internal").ap()
    q_d = nc.dram_tensor("q_rows", [N, D], F32, kind="Internal").ap()
    qT_d = nc.dram_tensor("q_columns", [NG, P, GT * KC * T], F32, kind="Internal").ap()

    def group_rows(t, gi):
        return t[ds(gi * (GT * T), GT * T), :].rearrange("(j p) d -> p j d", p=T)

    with ExitStack() as ctx:
        def sb(name, shape, dt=F32):
            return ctx.enter_context(nc.sbuf_tensor(name, shape, dt))

        def sem(name):
            return ctx.enter_context(nc.semaphore(name))

        def bank(name):
            return ctx.enter_context(nc.psum_tensor(name, [P, 512], F32))
        ps_seg = [bank("ps_seg0"), bank("ps_seg1")]
        ps_tr = bank("ps_tr")
        ps_qk = bank("ps_qk")
        ps_v = bank("ps_v")
        ps_ctx = bank("ps_ctx")
        ps_turn = [ps_tr, ps_ctx]
        ps_ao = [ps_ctx, ps_tr]
        ps_out = [ps_qk, ps_v]
        ps_hid = [bank("ps_hid0"), bank("ps_hid1")]
        ps_mm = [(ps_qk, ps_v), (ps_hid[0], ps_hid[1])]

        xres = sb("xres", [T, NT, D])
        kbuf = sb("kbuf", [T, NT, D])
        vbuf = sb("vbuf", [T, NT, D])
        acc = sb("acc", [T, 2 * NT, AW])
        wqkv = sb("wqkv", [P, KC, 3 * D])
        wo = sb("wo", [P, KC, D])
        wff = sb("wff", [P, 2 * KC * FF])
        w1 = wff[:, 0:KC * FF].rearrange("p (c f) -> p c f", c=KC)
        w2 = wff[:, KC * FF:].rearrange("p (f d) -> p f d", f=FC)
        wg = wqkv[:, :, :].rearrange("p c n -> p (c n)").rearrange("p (m c n) -> p m c n", m=3, c=KC)
        ln1p = sb("ln1p", [P, 2, KC])
        ln2p = sb("ln2p", [P, 2, KC])
        b1p = sb("b1p", [P, FC])
        bo_b = sb("bo_b", [T, D])
        b2_b = sb("b2_b", [T, D])
        res_b = sb("res_b", [T, 1])

        idx_tab = sb("idx_tab", [T, 2 * STEPS, 2], I32)
        key_tab = sb("key_tab", [T, 2 * STEPS])
        in_tile = sb("in_tile", [T, 2 * QUADS, 2])
        row_tab = sb("row_tab", [1, 2 * QUADS, 2], I32)
        idx_now = sb("idx_now", [T, 2, RING, 2], I32)
        xg = sb("xg", [T, RING, AW])
        rg = sb("rg", [T, RING, D])
        zrow = sb("zrow", [1, D + KC])
        hot = sb("hot", [T, QUAD, T])
        iota_t = sb("iota_t", [T, T])
        ident = sb("ident", [P, P])
        ones = sb("ones", [P, P])
        head_mask = sb("head_mask", [P, P])

        xh = sb("xh", [T, GT, D])
        hT = sb("hT", [P, GT, KC, T])
        q5p = sb("q5", [P, GT * D])
        q5 = q5p[0:T, :].rearrange("p (j d) -> p j d", j=GT)
        qT = q5p[:, 0:GT * KC * T].rearrange("p (j c t) -> p j c t", j=GT, c=KC)
        gT = sb("gT", [P, 2, FC, T])
        kmax = sb("kmax", [T, D])
        flat_g = gT[:, :, :, :].rearrange("p s f t -> p (s f t)")
        qrow = flat_g[0:T, 0:GT * D].rearrange("p (j d) -> p j d", j=GT)
        kmaxT = sb("kmaxT", [P, KC])
        ksh = sb("ksh", [T, D])
        gb_b = ksh
        ctxm, ctxT = (flat_g[:, a:a + D].rearrange("p (c d) -> p c d", c=KC)
                      for a in (GT * D, GT * D + D))
        kdiag = ctxm
        rsum = sb("rsum", [P, KC])
        cwo = sb("cwo", [P, KC, D])
        qm = sb("qm", [T, GT * HEADS])
        stat = sb("stat", [T, GT, 6])
        mv = sb("mv", [T, GT, 2])
        var = sb("var", [T, GT])
        seed = sb("seed", [T, GT], I32)
        rstd = sb("rstd", [T, GT])
        tmp = sb("tmp", [T, GT])
        norm = sb("norm", [T, GT])

        step_rows = vbuf[0:SCH, 0:6, :].rearrange("p a d -> p (a d)")[:, 0:12 * T].bitcast(I32)\
            .rearrange("p (m c t) -> p m c t", m=3, c=4)
        step_rows_f = kbuf[0:SCH, 0:6, :].rearrange("p a d -> p (a d)")[:, 0:12 * T]\
            .rearrange("p (m c t) -> p m c t", m=3, c=4)
        ps_tab = [ps_seg[0], ps_seg[1], ps_tr, ps_qk]

        def early(i, rows, n):
            return kbuf[0:rows, 8 + 2 * i:10 + 2 * i, :].rearrange("p a d -> p (a d)")[:, 0:n]
        iota_i = early(0, T, T).bitcast(I32)
        part_i = early(1, T, 1).bitcast(I32)
        ramp_i, ramp = early(1, SCH, NT)[:, 1:NT].bitcast(I32), early(2, SCH, NT)[:, 1:NT]
        enum_i = early(3, SCH, 4 * T).bitcast(I32).rearrange("p (c t) -> p c t", c=4)
        enum = early(4, SCH, 4 * T).rearrange("p (c t) -> p c t", c=4)
        dropped = early(5, SCH, T)
        spans = early(6, SCH, 4 * T).rearrange("p (c t) -> p c t", c=4)
        first, tile_of, base, place, bad = (early(7, SCH, 4 * (i + 1))[:, 4 * i:] for i in range(5))
        reached = early(7, SCH, 64 + NT)[:, 64:64 + NT - 1]
        nspread = early(7, SCH, 120)[:, 119:120]
        place_row = vbuf[0:1, 16:18, :].rearrange("p a d -> p (a d)")[:, 0:2 * QUADS]
        tile_row = vbuf[0:1, 18:20, :].rearrange("p a d -> p (a d)")[:, 0:2 * QUADS]
        quad_first = vbuf[0:SCH, 20, 0:SCH]
        pair_a, pair_b = (vbuf[0:PAIR_ROWS, a:a + 2, :].rearrange("p a d -> p (a d)")[:, 0:PAIRS].bitcast(I32)
                          for a in (8, 10))
        falls = vbuf[0:PAIR_ROWS, 12:14, :].rearrange("p a d -> p (a d)")[:, 0:PAIRS]
        nfall = vbuf[0:PAIR_ROWS, 14, 0:1]
        unsorted_f = sb("unsorted_f", [T, 1])
        unsorted_i = sb("unsorted_i", [1, 1], I32)
        part = sb("part", [T, 1])
        gsrc, gtype, gdst = idx_now[:, 0, 0, 0:1], idx_now[:, 0, 0, 1:2], idx_now[:, 0, 1, 0:1]
        gedge, gkey = tmp[:, 0:1], tmp[:, 1:2]
        lmask = sb("lmask", [T, NX, NX])
        lg, gate, gex = (rg[:, m, 0:GT * NX].rearrange("p (j e) -> p j e", j=GT) for m in range(2, 5))
        beat, beat2 = (rg[:, m, 0:GT * NX * NX].rearrange("p (j e o) -> p j e o", j=GT, e=NX) for m in range(2))
        gone = sb("gone", [T, GT])
        sb1p, sb2p, eb1p = b1p[:, 0:KC], b1p[:, KC:KC + 1], b1p[:, KC + 1:KC + 1 + NX]
        eb2p = ln2p[0:EH2].rearrange("p m c -> p (m c)")
        gateb = sb("gateb", [T, NX])

        START = {}

        def counted(name, start=0):
            s = sem(name)
            START[id(s)] = start
            return s

        s_x = sem("x_loaded")
        s_par = sem("params_loaded")
        s_const = sem("constants_made")
        s_clr = sem("table_rows_cleared")
        s_pair = sem("neighbours_loaded")
        s_tabl = sem("table_rows_loaded")
        s_pdve = sem("prologue_dve")
        s_ppe = sem("prologue_pe")
        s_ppool = sem("prologue_pool")
        s_tab = sem("tables_ready")
        s_xn_st = sem("xn_stored")
        s_h1_st = sem("h1_stored")
        s_out = sem("out_stored")
        s_edge = [sem(f"edge_gathered{i}") for i in range(RING)]
        s_idx = sem("idx_staged")
        s_claim = sem("slot_claimed")
        s_msg = counted("message_ready", RING + 1)
        s_seg = counted("segment_done", RING)
        s_acc = counted("acc_added", 3)
        s_zero = sem("acc_zeroed")
        s_gidx = sem("general_indices_loaded")
        s_ggat = sem("general_rows_gathered")
        s_gkey = sem("general_dve")
        s_ghot = sem("general_onehot_ready")
        s_gseg = sem("general_segment_done")
        s_gadd = counted("general_added", 1)
        s_xr = sem("x_ready")
        s_ln = sem("norm_dve")
        s_xh = sem("xh_ready")
        s_tr = counted("xh_transposed", GT)
        s_hT = counted("hT_ready", 1)
        s_mm = sem("qkv_done")
        s_wqkv = sem("wqkv_loaded")
        s_wff = sem("wff_loaded")
        s_ev = counted("qkv_copied", 1)
        s_qst = [counted(f"q_stored{j}", 16) for j in range(GT)]
        s_qrl = sem("q_rows_loaded")
        s_qtr = sem("q_transposed")
        s_qTe = counted("qT_copied", 1)
        s_qTst = counted("qT_stored", 16)
        s_qld = sem("q_loaded")
        s_qs = sem("q_shifted")
        s_qe = sem("q_exp")
        s_qn = sem("q_normed")
        s_qd = sem("q_dve")
        s_km = sem("kmax_dve")
        s_kmT = sem("kmax_transposed")
        s_kdg = sem("kmax_diagonal")
        s_kmB = sem("kmax_spread")
        s_ks = sem("k_shifted")
        s_ke = counted("k_exp", 1)
        s_ctx = counted("context_done", 1)
        s_ctT = sem("context_transposed")
        s_cmT = sem("context_turned")
        s_cm = sem("context_masked")
        s_cw = sem("context_wo_done")
        s_cwr = sem("context_wo_ready")
        s_ao = counted("attention_done", GT)
        s_xa = counted("x_attention_added", 1)
        s_up = sem("hidden_done")
        s_gel = counted("gelu_done", 2)
        s_fo = counted("ffn_done", 1)
        s_xf = counted("x_ffn_added", 1)
        s_gw = sem("graph_weights_loaded")
        s_hr = sem("h_rows_loaded")
        s_dd = sem("dense_dve")
        s_sc = sem("sums_scaled")
        s_dtr = counted("dense_transposed", 1)
        s_dT = counted("dense_T_ready", 1)
        s_bias = sem("attention_bias_added")
        s_dy = counted("dense_product_done", 1)
        s_db = counted("dense_biased", 1)
        s_dt = sem("dense_tanh")
        s_hn = sem("h_new_ready")
        s_ew = sem("last_weights_loaded")
        s_er = sem("last_rows_loaded")
        s_ed = sem("last_dve")
        s_erow = sem("h2_rows_staged")
        s_etr = sem("h2_transposed")
        s_eT = counted("h2T_ready", 1)
        s_emu = counted("mu_done", 1)
        s_emz = counted("mu_added", 1)
        s_exh = sem("last_xh_ready")
        s_ext = sem("last_xh_transposed")
        s_exT = counted("last_xhT_ready", 1)
        s_elg = sem("gate_logits_done")
        s_egx = sem("gates_shifted")
        s_ege = sem("gates_exp")
        s_e1 = sem("last_hidden1_done")
        s_e1a = counted("last_hidden1_ready", 1)
        s_e2 = sem("last_hidden2_done")
        s_e2a = counted("last_hidden2_ready", 1)
        s_eo = sem("experts_done")
        s_ez = counted("row_combined", 1)

        block = ctx.enter_context(nc.Block())

        class Chain:

            def __init__(self, eng, s, base=0):
                self.eng, self.s, self.base, self.n = eng, s, base, 0

            def __call__(self, ins):
                ins.then_inc(self.s, 1)
                self.n += 1

            def wait(self):
                self.eng.wait_ge(self.s, self.base + self.n)

        def hold(eng, s, value):
            eng.wait_ge(s, value)
            eng.sem_inc(s_claim, 1)

        def norm_stats(dve, chain, rows, between=lambda: None):
            for j in range(GT):
                chain(dve.bn_stats(stat[:, j, :], rows(j)))
            between()
            hold(dve, chain.s, chain.base + chain.n)
            for j in range(GT):
                chain(dve.bn_aggr(mv[:, j, :], stat[:, j, :]))
            between()
            chain.wait()
            chain(dve.tensor_scalar(var[:, :], mv[:, :, 1], EPS, None, ALU.add))
            chain.wait()
            chain(dve.tensor_scalar(seed[:, :], var[:, :].bitcast(I32), 1, None, ALU.arith_shift_right))
            chain.wait()
            chain(dve.tensor_scalar(rstd[:, :].bitcast(I32), seed[:, :], -1.0, RSQRT_SEED, ALU.mult, ALU.add))
            for newton in range(4):
                if newton == 2:
                    between()
                chain.wait()
                chain(dve.scalar_tensor_tensor(tmp[:, :], rstd[:, :], -0.5, var[:, :], ALU.mult, ALU.mult))
                chain.wait()
                chain(dve.tensor_tensor(tmp[:, :], tmp[:, :], rstd[:, :], ALU.mult))
                chain.wait()
                chain(dve.scalar_tensor_tensor(rstd[:, :], tmp[:, :], 1.5, rstd[:, :], ALU.add, ALU.mult))
            chain.wait()
        NORM_STEPS = 2 * GT + 3 + 12

        def norm_rows(dve, j, rows):
            return dve.tensor_scalar(xh[:, j, :], rows, mv[:, j, 0:1], rstd[:, j:j + 1], ALU.subtract, ALU.mult)

        def transpose_rows(pe, dst, rows):
            for c in range(KC):
                ins = pe.transpose(dst[:, c * T:(c + 1) * T], rows[:, c * P:(c + 1) * P], ident[0:T, 0:T])
            return ins

        def columns(v):
            return v.rearrange("(c p) -> p c", p=P)

        def rows_of(w):
            return w.rearrange("(c p) n -> p c n", p=P)

        def flat_qT(t):
            return t[:, :, :, :].rearrange("p j c t -> p (j c t)")

        def start(eng, *sems):
            for s in sems:
                eng.sem_inc(s, START.pop(id(s)))

        offs, at = {}, 0
        for name, cols in (("mu", KC * D), ("sW1", KC * D), ("sW2", KC * P), ("sW3", D), ("eW1", NX * KC * P),
                           ("eW2", NX * EH2), ("eW3", NX * D), ("gW", KC * NX)):
            offs[name] = (at, at + cols)
            at += cols
        assert at <= 2 * KC * FF

        def last_w(name, c):
            a, b = offs[name]
            return wff[:, a:b].rearrange("p (c n) -> p c n", c=c)

        mu_w, sW1, sW2, gW = (last_w(n, KC) for n in ("mu", "sW1", "sW2", "gW"))
        sW3 = last_w("sW3", 1)[:, 0, :]
        eW1 = last_w("eW1", NX).rearrange("p e (c n) -> p e c n", c=KC)
        eW2, eW3 = last_w("eW2", NX), last_w("eW3", NX)
        e2T = acc[0:EH2 + 1, 0:2, 0:2 * T].rearrange("p a (b t) -> p a b t", t=T)

        def e2T_of(e):
            return e2T[:, e // 2, e % 2, :]

        @block.sync
        def _(sp):
            for gi in range(NG):
                sp.dma_start(xres[:, gi * GT:(gi + 1) * GT, :], group_rows(io["x"], gi)).then_inc(s_x, 16)
            sp.wait_ge(s_clr, 1)
            for m, name in enumerate(("src", "dst", "edge_type_400")):
                for ch, at in enumerate(CHUNKS):
                    n = min(SCH, ET - at)
                    sp.dma_start(step_rows[0:n, m, ch, :], io[name][at * T:(at + n) * T].rearrange("(t p) -> t p", p=T))\
                        .then_inc(s_tabl, 16)
            for t, lag in ((pair_a, 0), (pair_b, 1)):
                sp.dma_start(t, io["dst"][lag:lag + E - 1].rearrange("(p n) -> p n", p=PAIR_ROWS)).then_inc(s_pair, 16)
            sp.dma_start(res_b[:, :], io["L0_gnn_res"].partition_broadcast(T)).then_inc(s_par, 16)
            for gi in range(NG):
                sp.wait_ge(s_xr, gi + 1)
                sp.dma_start(group_rows(xn_d, gi), xres[:, gi * GT:(gi + 1) * GT, :]).then_inc(s_xn_st, 16)

            def load_qkv(lay):
                for m, name in enumerate(("Wq", "Wk", "Wv")):
                    sp.dma_start(wqkv[:, :, m * D:(m + 1) * D], rows_of(io[f"L0_mix_{name}"][lay])).then_inc(s_wqkv, 16)
                sp.dma_start(ln1p[:, 0, :], columns(io["L0_mix_ln1_g"][lay]),
                             allow_slow_non_contiguous=True).then_inc(s_wqkv, 16)
                sp.dma_start(ln1p[:, 1, :], columns(io["L0_mix_ln1_b"][lay]),
                             allow_slow_non_contiguous=True).then_inc(s_wqkv, 16)

            def load_ff(lay):
                sp.dma_start(wo[:, :, :], rows_of(io["L0_mix_Wo"][lay])).then_inc(s_wff, 16)
                sp.dma_start(w1, rows_of(io["L0_mix_W1"][lay])).then_inc(s_wff, 16)
                sp.dma_start(w2, rows_of(io["L0_mix_W2"][lay])).then_inc(s_wff, 16)
                sp.dma_start(ln2p[:, 0, :], columns(io["L0_mix_ln2_g"][lay]),
                             allow_slow_non_contiguous=True).then_inc(s_wff, 16)
                sp.dma_start(ln2p[:, 1, :], columns(io["L0_mix_ln2_b"][lay]),
                             allow_slow_non_contiguous=True).then_inc(s_wff, 16)
                sp.dma_start(b1p[:, :], columns(io["L0_mix_b1"][lay]),
                             allow_slow_non_contiguous=True).then_inc(s_wff, 16)
                sp.dma_start(bo_b[:, :], io["L0_mix_bo"][lay].partition_broadcast(T)).then_inc(s_wff, 16)
                sp.dma_start(b2_b[:, :], io["L0_mix_b2"][lay].partition_broadcast(T)).then_inc(s_wff, 16)

            load_qkv(0)
            for lay in range(L):
                g, h = lay // 2, lay % 2
                sp.wait_ge(s_xr, NG * (lay + 1))
                load_ff(lay)
                with sp.Fori(0, NG) as gi:
                    for j in range(GT):
                        sp.wait_ge(s_ev, gi * GT + (j + 2 + lay * NT))
                        sp.dma_start(q_d[ds(gi * (GT * T) + j * T, T), :], q5[:, j, :]).then_inc(s_qst[j], 16)
                if h == 0:
                    load_qkv(lay + 1)
                else:
                    for m, name in enumerate(("W_in", "W_out", "W_loop")):
                        sp.dma_start(wg[:, m], rows_of(io[f"L0_gnn_{name}{g + 1}"])).then_inc(s_gw, 16)

                def load_q(gi):
                    sp.dma_start(qrow, group_rows(q_d, gi)).then_inc(s_qrl, 16)

                def store_qT(gi):
                    sp.wait_ge(s_qTe, gi * GT + (1 + GT + lay * NT))
                    sp.dma_start(qT_d[ds(gi, 1)].rearrange("o p n -> p (o n)"), flat_qT(hT)).then_inc(s_qTst, 16)
                for j in range(GT):
                    sp.wait_ge(s_qst[j], 16 + 16 * NG * (lay + 1))
                load_q(0)
                with sp.Fori(0, NG - 1) as gi:
                    sp.wait_ge(s_qtr, gi * GT + (GT + lay * NT))
                    load_q(gi + 1)
                    store_qT(gi)
                store_qT(NG - 1)
                sp.wait_ge(s_qTst, 16 + 16 * NG * (lay + 1))
                sp.wait_ge(s_ctx, 1 + (lay + 1) * NG)
                with sp.Fori(0, NG) as gi:
                    sp.wait_ge(s_ao, gi * GT + (GT + lay * NT))
                    sp.dma_start(flat_qT(qT), qT_d[ds(gi, 1)].rearrange("o p n -> p (o n)")).then_inc(s_qld, 16)
                if h == 1:
                    if g == 0:
                        sp.wait_ge(s_xn_st, 16 * NG)
                    else:
                        sp.wait_ge(s_h1_st, 16 * NG)
                    sp.dma_start(gb_b[:, :], io[f"L0_gnn_b{g + 1}"].partition_broadcast(T)).then_inc(s_gw, 16)
                    for gi in range(NG):
                        sp.dma_start(kbuf[:, gi * GT:(gi + 1) * GT, :],
                                     group_rows((xn_d, h1_d)[g], gi)).then_inc(s_hr, 16)
                    if g == 0:
                        for gi in range(NG):
                            sp.wait_ge(s_hn, (gi + 1) * GT)
                            sp.dma_start(group_rows(h1_d, gi), vbuf[:, gi * GT:(gi + 1) * GT, :]).then_inc(s_h1_st, 16)
                        load_qkv(lay + 1)
            sp.wait_ge(s_xr, NG * (L + 1))
            for t, src in (
                (mu_w, rows_of(io["L0_gnn_mu_w"])), (sW1, rows_of(io["L0_ffn_sW1"])), (sW2, rows_of(io["L0_ffn_sW2"])),
                (sW3, io["L0_ffn_sW3"]), (eW2, io["L0_ffn_eW2"].rearrange("e p n -> p e n")),
                (eW3[0:EH2], io["L0_ffn_eW3"].rearrange("e p n -> p e n")),
                (eW3[EH2:EH2 + 1], io["L0_ffn_eb3"].rearrange("(o e) n -> o e n", o=1)),
                (gW, rows_of(io["L0_ffn_gW"])), (sb1p, columns(io["L0_ffn_sb1"])),
                (sb2p, columns(io["L0_ffn_sb2"])), (eb1p, io["L0_ffn_eb1"].rearrange("e p -> p e")),
                (eb2p, io["L0_ffn_eb2"].rearrange("e p -> p e")),
                (bo_b[:, :], io["L0_gnn_mu_b"].partition_broadcast(T)),
                (b2_b[:, :], io["L0_ffn_sb3"].partition_broadcast(T)),
                (gateb[:, :], io["L0_ffn_gb"].partition_broadcast(T)),
            ):
                sp.dma_start(t, src, allow_slow_non_contiguous=True).then_inc(s_ew, 16)
            for e in range(NX):
                sp.dma_start(eW1[:, e], rows_of(io["L0_ffn_eW1"][e])).then_inc(s_ew, 16)
            sp.wait_ge(s_hn, GL * NT)
            for gi in range(NG):
                sp.dma_start(kbuf[:, gi * GT:(gi + 1) * GT, :], group_rows(io["x"], gi)).then_inc(s_er, 16)
            for gi in range(NG):
                sp.wait_ge(s_ez, 1 + (gi + 1) * GT)
                sp.dma_start(group_rows(out, gi), kbuf[:, gi * GT:(gi + 1) * GT, :]).then_inc(s_out, 16)
            sp.wait_ge(s_out, 16 * NG)

        @block.gpsimd
        def _(pool):
            pool.memset(step_rows[:, :, 3, :], 0).then_inc(s_clr, 1)
            pool.memset(ones[:, :], 1.0)
            pool.memset(zrow[:, :], 0.0)
            pool.memset(ident[:, :], 0.0)
            pool.memset(quad_first, 0.0)
            pool.memset(xg[:, :, D:AW], 1.0)
            pool.iota(part_i, [[0, 1]], base=0, channel_multiplier=1)
            pool.iota(ramp_i, [[T, NT - 1]], base=T, channel_multiplier=0)
            for ch, at in enumerate(CHUNKS):
                pool.iota(enum_i[:, ch, :], [[1, T]], base=at * T, channel_multiplier=T)
            pool.iota(iota_i, [[1, T]], base=0, channel_multiplier=0).then_inc(s_ppool, 1)
            pool.wait_ge(s_ppool, 1)
            pool.affine_select(out=ident[:, :], in_=ident[:, :], compare_op=ALU.not_equal, fill=1.0, base=0,
                               pattern=[[-1, P]], channel_multiplier=1)
            pool.affine_select(out=quad_first, in_=quad_first, compare_op=ALU.not_equal, fill=1.0, base=0,
                               pattern=[[-QUAD, SCH // QUAD], [0, QUAD]], channel_multiplier=1)
            pool.tensor_copy(iota_t[:, :], iota_i).then_inc(s_const, 1)
            pool.memset(acc[:, :, :], 0.0).then_inc(s_zero, 1)

            pool.wait_ge(s_tab, 1)
            for g in range(GL):
                rows, stored = ((xn_d, s_xn_st), (h1_d, s_h1_st))[g]
                pool.wait_ge(stored, 16 * NG)
                with pool.Fori(0, 2 * STEPS // (2 * RING)) as it:
                    for half in range(2):
                        s0 = it * (2 * RING) + (g * 2 * STEPS + half * RING)
                        pool.wait_ge(s_msg, s0 + 1)
                        pool.tensor_copy(idx_now[:, half], idx_tab[:, ds(it * (2 * RING) + half * RING, RING), :])\
                            .then_inc(s_idx, 1)
                        pool.wait_ge(s_idx, it * 2 + (g * 2 * STEPS // RING + half + 1))
                        for k in range(RING):
                            pool.wait_ge(s_seg, s0 + (k + 1))
                            pool.sem_inc(s_claim, 1)
                            pool.indirect_dma_start(
                                xg[:, k, 0:D], None, rows,
                                bass.IndirectOffsetOnAxis(ap=idx_now[:, half, k, 0:1], axis=0)).then_inc(s_edge[k], 16)
                            pool.indirect_dma_start(
                                rg[:, k, :], None, io[f"L0_gnn_rel{g + 1}"],
                                bass.IndirectOffsetOnAxis(ap=idx_now[:, half, k, 1:2], axis=0)).then_inc(s_edge[k], 16)
                hold(pool, s_seg, (g + 1) * (2 * STEPS) + RING)
                with pool.If(pool.value_load(unsorted_i[0:1, 0:1], min_val=0, max_val=1) == 1):
                    for half in range(2):
                        with pool.Fori(0, HT) as i:
                            n = i + (g * 2 + half) * HT
                            hold(pool, s_gadd, n * NT + 1)
                            for t, name in ((gsrc, "src"), (gtype, "edge_type_400"), (gdst, "dst")):
                                pool.dma_start(t, io[name][ds(i * T + half * SPLIT * T, T)].rearrange("(p o) -> p o", o=1),
                                               allow_slow_non_contiguous=True).then_inc(s_gidx, 16)
                            hold(pool, s_gidx, n * 48 + 48)
                            pool.indirect_dma_start(
                                xg[:, 0, 0:D], None, rows,
                                bass.IndirectOffsetOnAxis(ap=gsrc, axis=0)).then_inc(s_ggat, 16)
                            pool.indirect_dma_start(
                                rg[:, 0, :], None, io[f"L0_gnn_rel{g + 1}"],
                                bass.IndirectOffsetOnAxis(ap=gtype, axis=0)).then_inc(s_ggat, 16)

        @block.vector
        def _(dve):
            start(dve, s_gadd, s_msg, s_acc, s_xa, s_xf, s_db, s_emz, s_ez)

            for gi in range(NG):
                dve.wait_ge(s_x, 16 * NG)
                chain = Chain(dve, s_ln, gi * (NORM_STEPS + GT))
                norm_stats(dve, chain, lambda j: xres[:, gi * GT + j, :])
                for j in range(GT):
                    row = xres[:, gi * GT + j, :]
                    chain(dve.tensor_scalar(row, row, mv[:, j, 0:1], rstd[:, j:j + 1], ALU.subtract, ALU.mult))
                chain.wait()
                dve.sem_inc(s_xr, 1)
            LN0 = NG * (NORM_STEPS + GT)

            p = Chain(dve, s_pdve)
            dve.memset(lmask[:, :, :], 0.0)
            p(dve.memset(head_mask[:, :], 0.0))
            p.wait()
            for hd in range(P // DH):
                dve.memset(head_mask[hd * DH:(hd + 1) * DH, hd * DH:(hd + 1) * DH], 1.0)
            for e in range(1, NX):
                dve.memset(lmask[:, e, 0:e], 1.0)
            dve.wait_ge(s_const, 1)
            p(dve.tensor_copy(part[:, :], part_i))
            p(dve.tensor_copy(ramp, ramp_i))
            p(dve.tensor_copy(enum, enum_i))
            dve.wait_ge(s_tabl, 16 * 12)
            for m in (0, 2):
                dve.tensor_copy(step_rows_f[:, m], step_rows[:, m])
            p(dve.tensor_copy(step_rows_f[:, 1], step_rows[:, 1]))
            dve.wait_ge(s_pair, 2 * 16)
            p(dve.tensor_tensor(falls, pair_a, pair_b, ALU.is_gt))
            assert p.n == PD_ROWS
            p.wait()
            p(dve.tensor_reduce(nfall, falls, AX, ALU.add))
            dve.wait_ge(s_ppe, 1)
            p(dve.tensor_copy(first, ps_hid[0][0:SCH, 0:4]))
            p.wait()
            for ch in range(4):
                p(dve.tensor_scalar(reached, ramp, first[:, ch:ch + 1], None, ALU.is_le))
                p.wait()
                p(dve.tensor_reduce(tile_of[:, ch:ch + 1], reached, AX, ALU.add))
                p.wait()
                dve.tensor_scalar(spans[:, ch, :], step_rows_f[:, 1, ch, :], first[:, ch:ch + 1], float(T),
                                  ALU.subtract, ALU.is_ge)
            p(dve.tensor_scalar(base, tile_of, -float(T), None, ALU.mult))
            p.wait()
            p(dve.tensor_tensor(place, first, base, ALU.add))
            p(dve.tensor_reduce(bad, spans, AX, ALU.add))
            p.wait()
            p(dve.tensor_reduce(nspread, bad, AX, ALU.add))
            p(dve.tensor_scalar(tile_of[:, 2:4], tile_of[:, 2:4], float(NT), None, ALU.add))
            p.wait()
            assert p.n == PD_FALLS, p.n
            for ch in range(4):
                key = step_rows_f[:, 1, ch, :]
                p(dve.tensor_scalar(key, key, base[:, ch:ch + 1], None, ALU.add))
                p.wait()
                p(dve.tensor_scalar(dropped, key, float(T), -float(T), ALU.is_ge, ALU.mult))
                p.wait()
                p(dve.tensor_tensor(key, key, dropped, ALU.add))
                p.wait()
                for edge, op in (((HALF, ALU.is_ge),) if ch < 2 else ((HALF, ALU.is_lt), (E, ALU.is_ge))):
                    dve.tensor_scalar(dropped, enum[:, ch, :], float(edge), FAR, op, ALU.mult).then_inc(s_pdve, 1)
                    p.n += 1
                    p.wait()
                    p(dve.tensor_tensor(key, key, dropped, ALU.add))
                    p.wait()
            dve.wait_ge(s_ppe, 2)
            p(dve.tensor_scalar(unsorted_f[:, :], ps_hid[1][0:T, 0:1], 1.0, None, ALU.min))
            p.wait()
            p(dve.tensor_copy(unsorted_i[:, :], unsorted_f[0:1, :]))
            p.wait()
            p(dve.tensor_scalar(unsorted_f[:, :], unsorted_f[:, :], FAR, None, ALU.mult))
            p.wait()
            for m, row_f in ((0, tile_row), (1, place_row)):
                dve.wait_ge(s_ppe, 3 + m)
                p(dve.tensor_copy(row_f, (ps_tr, ps_qk)[m][0:1, 0:2 * STEPS].rearrange("p (q s) -> p q s", s=QUAD)[:, :, 0]))
            p.wait()
            assert p.n == PD_KEYS, p.n
            p(dve.tensor_copy(row_tab[:, :, 0], tile_row))
            p(dve.tensor_scalar(tile_row, tile_row, 1.0, None, ALU.add))
            p.wait()
            for h in range(2):
                half_row = tile_row[:, h * QUADS:(h + 1) * QUADS]
                p(dve.tensor_scalar(row_tab[:, h * QUADS:(h + 1) * QUADS, 1], half_row, float(h * NT + NT - 1), None, ALU.min))
            for m, tab in ((0, idx_tab[:, :, 0]), (1, key_tab[:, :]), (2, idx_tab[:, :, 1])):
                dve.wait_ge(s_ppe, 5 + m)
                if m == 1:
                    p(dve.tensor_scalar(tab, ps_tab[m][0:T, 0:2 * STEPS], unsorted_f[:, 0:1], None, ALU.add))
                else:
                    p(dve.tensor_copy(tab, ps_tab[m][0:T, 0:2 * STEPS]))
            dve.wait_ge(s_ppe, 8)
            for m, op in enumerate((ALU.is_le, ALU.is_gt)):
                p(dve.tensor_scalar(in_tile[:, :, m], ps_v[0:T, 0:2 * QUADS], part[:, 0:1], None, op))
            p.wait()
            dve.sem_inc(s_tab, 1)

            dve.wait_ge(s_zero, 1)

            def edge_steps(h, lay, at, per, gi):
                s0 = lay * STEPS + gi * per + at
                slot0 = lay * (STEPS // RING) + gi * (per // RING) + at // RING
                t0 = h * STEPS + gi * per + at
                quad0 = lay * QUADS + gi * (per // QUAD) + at // QUAD
                quad_t0 = h * QUADS + gi * (per // QUAD) + at // QUAD
                done = [0]
                rows = []

                def add(q):
                    dve.wait_ge(s_seg, s0 + (QUAD * (q + 1) + RING))
                    for m in range(2):
                        dve.wait_ge(s_acc, (quad0 + q) * 2 + (m + 3))
                        a = acc[:, ds(rows[2 * q + m], 1), :].rearrange("p o n -> p (o n)")
                        dve.scalar_tensor_tensor(a, ps_seg[q % 2][0:T, 0:AW], in_tile[:, ds(quad_t0 + q, 1), m], a,
                                                 ALU.mult, ALU.add).then_inc(s_acc, 1)

                def go(n):
                    for _ in range(n):
                        k = done[0]
                        done[0] += 1
                        if k % RING == 0:
                            rows.extend(nc.values_load_multi_w_load_instructions(
                                row_tab[0:1, ds(quad_t0 + k // QUAD, RING // QUAD), :].rearrange("p q m -> p (q m)"),
                                engines=(mybir.EngineType.DVE,),
                                min_val=0, max_val=2 * NT - 1, skip_runtime_bounds_check_because="clamped above")[1])
                        dve.wait_ge(s_seg, s0 + (k + 1 + RING - QUAD))
                        dve.tensor_scalar(hot[:, k % QUAD, :], iota_t[:, :], key_tab[:, ds(t0 + k, 1)], None, ALU.is_equal)
                        dve.wait_ge(s_edge[k % RING], slot0 * 32 + 32 * (k // RING + 1))
                        m = xg[:, k % RING, 0:D]
                        dve.tensor_tensor(m, m, rg[:, k % RING, :], ALU.mult).then_inc(s_msg, 1)
                        if k % QUAD == QUAD - 2 and k >= QUAD:
                            add(k // QUAD - 1)

                def end():
                    assert done[0] == per, (done, per)
                    add(per // QUAD - 1)
                return go, end

            with dve.Fori(0, GL) as g:
                with dve.Fori(0, 2) as h:
                    lay = g * 2 + h
                    dve.memset(kmax[:, :], -3.0e38).then_inc(s_km, 1)

                    def row(gi, j):
                        return xres[:, ds(gi * GT + j, 1), :].rearrange("p o d -> p (o d)")

                    def stats_A(gi, between=lambda: None):
                        chain = Chain(dve, s_ln, (lay * (2 * NG) + gi) * NORM_STEPS + LN0)
                        hold(dve, s_xr, lay * NG + gi + 1)
                        norm_stats(dve, chain, lambda j: row(gi, j), between)

                    def norm_A(gi, j):
                        dve.wait_ge(s_tr, lay * (2 * NT) + gi * GT + (j + 1))
                        norm_rows(dve, j, row(gi, j)).then_inc(s_xh, 1)

                    def group_A(gi, last):
                        tn = (lay * NG + gi) * GT
                        go, end = edge_steps(h, lay, 0, STEPS_A, gi)
                        km = Chain(dve, s_km, lay * KM_STEPS + gi * GT + 1)

                        def k_max(j):
                            km.wait()
                            dve.wait_ge(s_ev, tn + (j + 2))
                            k = kbuf[:, ds(gi * GT + j, 1), :].rearrange("p o d -> p (o d)")
                            km(dve.tensor_tensor(kmax[:, :], kmax[:, :], k, ALU.max))
                        beside = [0]

                        def between():
                            go(1)
                            if beside[0] in (1, 2):
                                k_max(beside[0] - 1)
                            beside[0] += 1
                        go(1)
                        if last:
                            for _ in range(3):
                                between()
                        else:
                            stats_A(gi + 1, between)
                            for j in range(3):
                                norm_A(gi + 1, j)
                        k_max(2)
                        go(1)
                        if not last:
                            norm_A(gi + 1, 3)
                            norm_A(gi + 1, 4)
                        k_max(3)
                        go(2)
                        k_max(4)
                        go(STEPS_A - 7)
                        end()
                    stats_A(0)
                    for j in range(GT):
                        norm_A(0, j)
                    with dve.Fori(0, NG - 1) as gi:
                        group_A(gi, False)
                    group_A(NG - 1, True)

                    go, end = edge_steps(h, lay, AT_C0, STEPS_C0, 0)
                    km = Chain(dve, s_km, lay * KM_STEPS + NT + 1)
                    dve.wait_ge(s_kmT, lay + 1)
                    km(dve.tensor_reduce(kmaxT[:, :], ps_ctx[:, 0:KC * T].rearrange("p (c t) -> p c t", c=KC), AX, ALU.max))
                    km.wait()
                    for c in range(KC):
                        ins = dve.tensor_scalar(kdiag[:, c, :], ident[:, :], kmaxT[:, c:c + 1], None, ALU.mult)
                    ins.then_inc(s_kdg, 1)
                    go(4)
                    dve.wait_ge(s_kmB, lay + 1)
                    km(dve.tensor_copy(ksh[:, :], ps_ctx[0:T, 0:D]))
                    go(STEPS_C0 - 4)
                    end()
                    hold(dve, s_km, km.base + km.n)
                    with dve.Fori(0, NG) as gi:
                        grp = lay * NG + gi
                        go, end = edge_steps(h, lay, AT_C, STEPS_C, gi)
                        k5 = kbuf[:, ds(gi * GT, GT), :]
                        dve.wait_ge(s_ke, grp + 1)
                        dve.tensor_tensor(xh[:, :, :], k5, ksh[:, :].unsqueeze(1).broadcast_to([T, GT, D]), ALU.subtract)\
                            .then_inc(s_ks, 1)
                        go(3)
                        qd = Chain(dve, s_qd, grp * 3)
                        qh = qrow.rearrange("p j (h e) -> p (j h) e", e=DH)
                        qmb = qm[:, :].unsqueeze(2).broadcast_to([T, GT * HEADS, DH])
                        dve.wait_ge(s_qrl, grp * 16 + 16)
                        qd(dve.tensor_reduce(qm[:, :], qh, AX, ALU.max))
                        go(1)
                        qd.wait()
                        dve.tensor_tensor(qh, qh, qmb, ALU.subtract).then_inc(s_qs, 1)
                        go(3)
                        dve.wait_ge(s_qe, grp + 1)
                        qd(dve.tensor_reduce(qm[:, :], qh, AX, ALU.add))
                        qd.wait()
                        qd(dve.reciprocal(qm[:, :], qm[:, :]))
                        qd.wait()
                        dve.tensor_tensor(qh, qh, qmb, ALU.mult).then_inc(s_qn, 1)
                        go(STEPS_C - 7)
                        end()
                    dve.wait_ge(s_ctx, (lay + 1) * NG + 1)
                    km(dve.reciprocal(rsum[:, :], ps_ctx[:, D:D + KC]))
                    km.wait()
                    for c in range(KC):
                        ins = dve.scalar_tensor_tensor(ctxm[:, c, :], ps_ctx[:, c * P:(c + 1) * P], rsum[:, c:c + 1],
                                                       head_mask[:, :], ALU.mult, ALU.mult)
                    ins.then_inc(s_cm, 1)
                    dve.wait_ge(s_ctT, lay + 1)
                    dve.tensor_copy(ctxT[:, :, :].rearrange("p c d -> p (c d)"), ps_tr[:, 0:D]).then_inc(s_cmT, 1)
                    dve.wait_ge(s_cw, lay + 1)
                    dve.tensor_copy(cwo[:, :, :].rearrange("p c d -> p (c d)"), ps_ctx[:, :]).then_inc(s_cwr, 1)

                    hold(dve, s_wff, (lay + 1) * (8 * 16))

                    def add_attention(gi, j):
                        dve.wait_ge(s_ao, (lay * NG + gi) * GT + (GT + j + 1))
                        dve.tensor_tensor(row(gi, j), row(gi, j), ps_ao[j % 2][0:T, 0:D], ALU.add).then_inc(s_xa, 1)

                    def stats_B(gi, between=lambda: None):
                        grp = lay * NG + gi
                        chain = Chain(dve, s_ln, (lay * (2 * NG) + gi + NG) * NORM_STEPS + LN0)
                        dve.wait_ge(s_xa, grp * GT + (1 + GT))
                        x5 = xres[:, ds(gi * GT, GT), :]
                        dve.tensor_tensor(x5, x5, bo_b[:, :].unsqueeze(1).broadcast_to([T, GT, D]), ALU.add).then_inc(s_bias, 1)
                        between()
                        hold(dve, s_bias, grp + 1)
                        norm_stats(dve, chain, lambda j: row(gi, j), between)

                    def norm_B(gi, j):
                        dve.wait_ge(s_tr, lay * (2 * NT) + gi * GT + (NT + j + 1))
                        norm_rows(dve, j, row(gi, j)).then_inc(s_xh, 1)

                    def add_ffn(gi, j):
                        dve.wait_ge(s_fo, (lay * NG + gi) * GT + (j + 2))
                        dve.tensor_tensor(row(gi, j), row(gi, j), ps_out[j % 2][0:T, 0:D], ALU.add).then_inc(s_xf, 1)

                    def group_B(gi, last):
                        go, end = edge_steps(h, lay, AT_B, STEPS_B, gi)
                        n = gi + 1
                        rest = [4]

                        def between():
                            if rest[0]:
                                rest[0] -= 1
                                go(1)
                        go(5)
                        add_ffn(gi, 0)
                        if not last:
                            for j in range(3):
                                add_attention(n, j)
                        go(3)
                        add_ffn(gi, 1)
                        if last:
                            go(4)
                        else:
                            add_attention(n, 3)
                            add_attention(n, 4)
                            stats_B(n, between)
                        add_ffn(gi, 2)
                        if not last:
                            for j in range(GT):
                                norm_B(n, j)
                        go(2)
                        add_ffn(gi, 3)
                        go(1)
                        add_ffn(gi, 4)
                        x5 = xres[:, ds(gi * GT, GT), :]
                        dve.wait_ge(s_xf, (lay * NG + gi) * GT + (1 + GT))
                        dve.tensor_tensor(x5, x5, b2_b[:, :].unsqueeze(1).broadcast_to([T, GT, D]), ALU.add)\
                            .then_inc(s_xr, 1)
                        go(STEPS_B - 15)
                        end()

                    go, end = edge_steps(h, lay, AT_B0, STEPS_B0, 0)
                    for j in range(GT):
                        add_attention(0, j)
                        if j >= 2:
                            go(1)
                    stats_B(0, lambda: go(1))
                    for j in range(GT):
                        norm_B(0, j)
                    go(STEPS_B0 - 7)
                    end()
                    with dve.Fori(0, NG - 1) as gi:
                        group_B(gi, False)
                    group_B(NG - 1, True)

                hold(dve, s_acc, (g + 1) * (4 * QUADS) + 3)
                with dve.If(dve.value_load(unsorted_i[0:1, 0:1], min_val=0, max_val=1) == 1):
                    for half in range(2):
                        dve.tensor_scalar(gedge, part[:, 0:1], float(half * SPLIT * T), None, ALU.add).then_inc(s_gkey, 1)
                        with dve.Fori(0, HT) as i:
                            n = (g * 2 + half) * HT + i
                            gk = Chain(dve, s_gkey, n * 5 + (g * 2 + half + 1))
                            hold(dve, s_ggat, n * 32 + 32)
                            gk.wait()
                            gk(dve.tensor_scalar(gkey, gedge, float(HALF), float(N), ALU.is_ge, ALU.mult))
                            gk.wait()
                            gk(dve.tensor_tensor(gkey, gkey, gdst, ALU.add))
                            gk(dve.tensor_scalar(gedge, gedge, float(T), None, ALU.add))
                            gk.wait()
                            gk(dve.tensor_scalar(gkey, gkey, float(-half * N), None, ALU.add))
                            m = xg[:, 0, 0:D]
                            gk(dve.tensor_tensor(m, m, rg[:, 0, :], ALU.mult))
                            hold(dve, s_gkey, gk.base + gk.n)
                            with dve.Fori(0, NT) as d:
                                q = n * NT + d
                                hold(dve, s_gadd, q + 1)
                                dve.tensor_scalar(hot[:, 0, :], iota_t[:, :], gkey, None, ALU.is_equal).then_inc(s_ghot, 1)
                                dve.wait_ge(s_ghot, q + 1)
                                dve.tensor_scalar(gkey, gkey, float(-T), None, ALU.add)
                                dve.wait_ge(s_gseg, q + 1)
                                a = acc[:, ds(d + half * NT, 1), :].rearrange("p o n -> p (o n)")
                                dve.tensor_tensor(a, a, ps_seg[0][0:T, 0:AW], ALU.add).then_inc(s_gadd, 1)
                    hold(dve, s_gadd, (g + 1) * (GTILES * NT) + 1)
                dve.wait_ge(s_gw, (g + 1) * (4 * 16))
                dve.wait_ge(s_par, 16)
                hold(dve, s_hr, (g + 1) * (NG * 16))
                with dve.Fori(0, NG) as gi:
                    dn = g * NT + gi * GT

                    def a_row(j, half):
                        return acc[:, ds(gi * GT + (j + half * NT), 1), :].rearrange("p o n -> p (o n)")

                    def h_row(t, j):
                        return t[:, ds(gi * GT + j, 1), :].rearrange("p o d -> p (o d)")
                    dd = Chain(dve, s_dd, (g * NG + gi) * 3)
                    deg = [acc[:, ds(gi * GT + half * NT, GT), D:AW].rearrange("p j o -> p (j o)") for half in range(2)]
                    dd(dve.tensor_tensor(norm[:, :], deg[0], deg[1], ALU.add))
                    dd.wait()
                    dd(dve.tensor_scalar(norm[:, :], norm[:, :], 1.0, None, ALU.max))
                    dd.wait()
                    dd(dve.reciprocal(norm[:, :], norm[:, :]))
                    dd.wait()
                    def scale(j):
                        dve.wait_ge(s_dtr, dn + (j if j else 1))
                        for half in range(2):
                            dve.tensor_scalar(q5[:, (j % 2) * 2 + half, :], a_row(j, half)[:, 0:D], norm[:, j:j + 1], None,
                                              ALU.mult)
                        dve.tensor_copy(xh[:, j % 2, :], h_row(kbuf, j)).then_inc(s_sc, 1)

                    def update(j):
                        dve.wait_ge(s_dt, dn + (j + 1))
                        dve.scalar_tensor_tensor(h_row(vbuf, j), h_row(vbuf, j), res_b[:, 0:1], h_row(kbuf, j),
                                                 ALU.mult, ALU.add).then_inc(s_hn, 1)
                    scale(0)
                    for j in range(GT):
                        if j + 1 < GT:
                            scale(j + 1)
                        dve.wait_ge(s_sc, dn + (j + 1))
                        for half in range(2):
                            dve.tensor_scalar(a_row(j, half), ones[0:T, 0:1].broadcast_to([T, AW]), 0.0, None, ALU.mult)
                        dve.wait_ge(s_dy, dn + (j + 2))
                        dve.tensor_tensor(h_row(vbuf, j), ps_out[j % 2][0:T, 0:D], gb_b[:, :], ALU.add)\
                            .then_inc(s_db, 1)
                        if j:
                            update(j - 1)
                    update(GT - 1)

            dve.wait_ge(s_er, 16 * NG)
            dve.wait_ge(s_ew, 16 * LAST_LOADS)
            dve.wait_ge(s_xr, NG * (L + 1))
            dve.memset(acc[EH2:EH2 + 1, 0:2, 0:2 * T], 1.0).then_inc(s_ed, 1)
            with dve.Fori(0, NG) as gi:
                dn = gi * GT
                z5 = kbuf[:, ds(gi * GT, GT), :]

                def z_row(j):
                    return kbuf[:, ds(gi * GT + j, 1), :].rearrange("p o d -> p (o d)")
                ed = Chain(dve, s_ed, gi * ED_STEPS + 1)
                dve.tensor_copy(q5[:, :, :], vbuf[:, ds(gi * GT, GT), :]).then_inc(s_erow, 1)
                ed(dve.tensor_tensor(z5, z5, xres[:, ds(gi * GT, GT), :], ALU.add))
                ed.wait()
                ed(dve.tensor_tensor(z5, z5, bo_b[:, :].unsqueeze(1).broadcast_to([T, GT, D]), ALU.add))
                ed.wait()
                for j in range(GT):
                    dve.wait_ge(s_emu, dn + (j + 2))
                    dve.tensor_tensor(z_row(j), z_row(j), ps_seg[1][0:T, 0:D], ALU.add).then_inc(s_emz, 1)
                hold(dve, s_emz, dn + (GT + 1))
                norm_stats(dve, ed, z_row)
                for j in range(GT):
                    norm_rows(dve, j, z_row(j)).then_inc(s_exh, 1)
                dve.wait_ge(s_exh, dn + GT)
                ed(dve.tensor_tensor(z5, z5, b2_b[:, :].unsqueeze(1).broadcast_to([T, GT, D]), ALU.add))
                dve.wait_ge(s_elg, gi + 1)
                ed(dve.tensor_tensor(lg, ps_seg[1][0:T, 0:GT * NX].rearrange("p (j e) -> p j e", e=NX),
                                     gateb[:, :].unsqueeze(1).broadcast_to([T, GT, NX]), ALU.add))
                ed.wait()

                def spread(t):
                    return t[:, :].unsqueeze(2).broadcast_to([T, GT, NX])
                ed(dve.tensor_reduce(gone[:, :], lg, AX, ALU.max))
                ed.wait()
                dve.tensor_tensor(lg, lg, spread(gone), ALU.subtract).then_inc(s_egx, 1)
                dve.wait_ge(s_ege, gi * 2 + 1)
                ed(dve.tensor_reduce(gone[:, :], lg, AX, ALU.add))
                ed.wait()
                ed(dve.reciprocal(gone[:, :], gone[:, :]))
                ed.wait()
                ed(dve.tensor_tensor(gate, lg, spread(gone), ALU.mult))
                ed.wait()
                ed(dve.tensor_reduce(gone[:, :], gate, AX, ALU.max))
                ed.wait()
                dve.tensor_tensor(gex, gate, spread(gone), ALU.subtract).then_inc(s_egx, 1)
                g_own = gate.unsqueeze(3).broadcast_to([T, GT, NX, NX])
                g_oth = gate.unsqueeze(2).broadcast_to([T, GT, NX, NX])
                ed(dve.tensor_tensor(beat, g_oth, g_own, ALU.is_gt))
                ed(dve.tensor_tensor(beat2, g_oth, g_own, ALU.is_equal))
                ed.wait()
                ed(dve.tensor_tensor(beat2, beat2,
                                     lmask[:, :, :].unsqueeze(1).broadcast_to([T, GT, NX, NX]), ALU.mult))
                ed.wait()
                ed(dve.tensor_tensor(beat, beat, beat2, ALU.add))
                ed.wait()
                ed(dve.tensor_reduce(lg, beat, AX, ALU.add))
                ed.wait()
                ed(dve.tensor_scalar(lg, lg, 1.5, None, ALU.is_lt))
                ed.wait()
                dve.wait_ge(s_ege, gi * 2 + 2)
                ed(dve.tensor_tensor(gate, gex, lg, ALU.mult))
                ed.wait()
                ed(dve.tensor_reduce(gone[:, :], gate, AX, ALU.add))
                ed.wait()
                ed(dve.reciprocal(gone[:, :], gone[:, :]))
                ed.wait()
                ed(dve.tensor_tensor(gate, gate, spread(gone), ALU.mult))
                ed.wait()
                for j in range(GT):
                    dve.wait_ge(s_eo, dn + (j + 1))
                    ed(dve.tensor_tensor(z_row(j), z_row(j), ps_qk[0:T, 0:D], ALU.add))
                    ed.wait()
                    for e in range(NX):
                        o = (ps_qk[0:T, D:2 * D], ps_v[0:T, 0:D], ps_v[0:T, D:2 * D], ps_seg[0][0:T, 0:D])[e]
                        ins = dve.scalar_tensor_tensor(z_row(j), o, gate[:, j, e:e + 1], z_row(j), ALU.mult, ALU.add)
                        if e < NX - 1:
                            ed(ins)
                            ed.wait()
                    ins.then_inc(s_ez, 1)
                assert ed.n == ED_STEPS, ed.n

        @block.scalar
        def _(act):
            start(act, s_hT, s_ev, s_qTe, s_gel, s_dT, s_eT, s_exT, s_e1a, s_e2a, s_ke, s_qTst, *s_qst)

            def copy(dst, src):
                return act.activation(dst, src, ACT.Identity)

            def dense_tanh(gi, dn, j):
                act.wait_ge(s_db, dn + (j + 2))
                row = vbuf[:, ds(gi * GT + j, 1), :].rearrange("p o d -> p (o d)")
                act.activation(row, row, ACT.Tanh).then_inc(s_dt, 1)

            def norm_out(j, u, par):
                act.wait_ge(s_tr, u + (GT + j + 1))
                for c in range(KC):
                    ins = act.activation(hT[:, j, c, :], ps_turn[j % 2][:, c * T:(c + 1) * T], ACT.Identity,
                                         bias=par[:, 1, c:c + 1], scale=par[:, 0, c:c + 1])
                ins.then_inc(s_hT, 1)

            with act.Fori(0, GL) as g:
                with act.Fori(0, 2) as h:
                    lay = g * 2 + h
                    act.wait_ge(s_wqkv, (lay + 1) * (5 * 16))
                    def group_A(gi, last):
                        grp = lay * NG + gi
                        tn = grp * GT
                        u = lay * (2 * NT) + gi * GT
                        for j in range(GT):
                            if j + 1 < GT:
                                norm_out(j + 1, u, ln1p)
                            act.wait_ge(s_qst[j], grp * 16 + 16)
                            act.wait_ge(s_mm, tn + (j + 1))
                            qk, v = ps_mm[j % 2]
                            copy(q5[:, j, :], qk[0:T, 0:D])
                            copy(kbuf[:, ds(gi * GT + j, 1), :].rearrange("p o d -> p (o d)"), qk[0:T, D:2 * D])
                            copy(vbuf[:, ds(gi * GT + j, 1), :].rearrange("p o d -> p (o d)"), v[0:T, 0:D])\
                                .then_inc(s_ev, 1)
                        if not last:
                            norm_out(0, u + GT, ln1p)
                    norm_out(0, lay * (2 * NT), ln1p)
                    with act.Fori(0, NG - 1) as gi:
                        group_A(gi, False)
                    group_A(NG - 1, True)
                    for j in range(GT):
                        act.wait_ge(s_qst[j], (lay + 1) * (NG * 16) + 16)
                    with act.Fori(0, NG) as gi:
                        grp = lay * NG + gi
                        tn = grp * GT
                        act.wait_ge(s_ks, grp + 1)
                        act.wait_ge(s_ctx, grp + 1)
                        act.activation(q5[:, :, :], xh[:, :, :], ACT.Exp, scale=SCALE).then_inc(s_ke, 1)
                        act.wait_ge(s_qs, grp + 1)
                        act.activation(qrow, qrow, ACT.Exp, scale=SCALE).then_inc(s_qe, 1)
                        act.wait_ge(s_qTst, grp * 16 + 16)
                        for j in range(GT):
                            act.wait_ge(s_qtr, tn + (j + 1))
                            copy(hT[:, j, :, :].rearrange("p c t -> p (c t)"), ps_out[j % 2][:, 0:KC * T]).then_inc(s_qTe, 1)
                    act.wait_ge(s_wff, (lay + 1) * (8 * 16))
                    act.wait_ge(s_qTst, (lay + 1) * (NG * 16) + 16)
                    for j in range(GT):
                        norm_out(j, lay * (2 * NT) + NT, ln2p)

                    def gelu_group(gi):
                        tn = (lay * NG + gi) * GT
                        for j in range(GT):
                            for hf in range(2):
                                if hf == 0:
                                    act.wait_ge(s_fo, tn + (j if j else 1))
                                act.wait_ge(s_up, tn * 2 + (2 * j + hf + 1))
                                for f in range(FC // 2):
                                    ff = hf * (FC // 2) + f
                                    ins = act.activation(gT[:, j % 2, ff, :], ps_hid[hf][:, f * T:(f + 1) * T],
                                                         ACT.Gelu, bias=b1p[:, ff:ff + 1])
                                ins.then_inc(s_gel, 1)
                    with act.Fori(0, NG - 1) as gi:
                        gelu_group(gi)
                        for j in range(GT):
                            norm_out(j, lay * (2 * NT) + (gi + 1) * GT + NT, ln2p)
                    gelu_group(NG - 1)
                with act.Fori(0, NG) as gi:
                    dn = g * NT + gi * GT
                    for j in range(GT):
                        act.wait_ge(s_dtr, dn + (j + 2))
                        act.wait_ge(s_dy, dn + (j if j else 1))
                        copy(gT[:, j % 2, 0:4, :].rearrange("p f t -> p (f t)"), ps_hid[0][:, 0:4 * T])
                        copy(gT[:, j % 2, 4:6, :].rearrange("p f t -> p (f t)"), ps_hid[1][:, 0:2 * T]).then_inc(s_dT, 1)
                        if j:
                            dense_tanh(gi, dn, j - 1)
                    dense_tanh(gi, dn, GT - 1)

            act.wait_ge(s_ew, 16 * LAST_LOADS)
            act.wait_ge(s_ed, 1)
            with act.Fori(0, NG) as gi:
                dn = gi * GT
                for j in range(GT):
                    act.wait_ge(s_etr, dn + (j + 1))
                    copy(hT[:, j, :, :].rearrange("p c t -> p (c t)"), ps_tr[:, 0:KC * T]).then_inc(s_eT, 1)
                for j in range(GT):
                    act.wait_ge(s_ext, dn + (j + 1))
                    copy(hT[:, j, :, :].rearrange("p c t -> p (c t)"), ps_tr[:, 0:KC * T]).then_inc(s_exT, 1)
                for m in range(2):
                    act.wait_ge(s_egx, gi * 2 + (m + 1))
                    src, dst = ((lg, lg), (gex, gex))[m]
                    act.activation(dst[:, :, :], src[:, :, :], ACT.Exp).then_inc(s_ege, 1)
                for j in range(GT):
                    act.wait_ge(s_e1, dn + (j + 1))
                    for f in range(KC):
                        act.activation(gT[:, 0, f, :], ps_hid[0][:, f * T:(f + 1) * T], ACT.Relu, bias=sb1p[:, f:f + 1])
                    for e in range(NX):
                        ins = act.activation(gT[:, 0, KC + e, :], ps_hid[1][:, e * T:(e + 1) * T], ACT.Relu,
                                             bias=eb1p[:, e:e + 1])
                    ins.then_inc(s_e1a, 1)
                    act.wait_ge(s_e2, dn + (j + 1))
                    act.activation(gT[:, 1, 0, :], ps_hid[0][:, 3 * P:3 * P + T], ACT.Relu, bias=sb2p[:, 0:1])
                    for e in range(NX):
                        ins = act.activation(e2T_of(e)[0:EH2], ps_ctx[0:EH2, e * T:(e + 1) * T], ACT.Relu,
                                             bias=eb2p[:, e:e + 1])
                    ins.then_inc(s_e2a, 1)

        @block.tensor
        def _(pe):
            start(pe, s_seg, s_tr, s_ao, s_fo, s_dy, s_dtr, s_emu, s_ctx)

            pe.wait_ge(s_const, 1)
            pe.wait_ge(s_pdve, PD_ROWS)
            pe.matmul(ps_hid[0][0:SCH, 0:4], quad_first, step_rows_f[:, 1, :, 0], start=True, stop=True).then_inc(s_ppe, 1)
            pe.wait_ge(s_pdve, PD_FALLS)
            pe.matmul(ps_hid[1][:, 0:1], ones[0:PAIR_ROWS, :], nfall, start=True, stop=False)
            pe.matmul(ps_hid[1][:, 0:1], ones[0:SCH, :], nspread, start=False, stop=True).then_inc(s_ppe, 1)
            for m, (bank_m, rows) in enumerate(((ps_tr, tile_of), (ps_qk, place))):
                for ch in range(4):
                    ins = pe.transpose(bank_m[0:1, ch * SCH:(ch + 1) * SCH], rows[:, ch:ch + 1], ident[0:SCH, 0:SCH])
                ins.then_inc(s_ppe, 1)
            pe.wait_ge(s_pdve, PD_KEYS)
            for m in range(3):
                for ch in range(4):
                    ins = pe.transpose(ps_tab[m][0:T, ch * SCH:(ch + 1) * SCH], step_rows_f[:, m, ch, :], ident[0:SCH, 0:SCH])
                ins.then_inc(s_ppe, 1)
            pe.matmul(ps_v[0:T, 0:2 * QUADS], ones[0:1, 0:T], place_row, start=True, stop=True).then_inc(s_ppe, 1)

            def edge_steps(lay, at, per, gi):
                s0 = lay * STEPS + gi * per + at
                quad0 = lay * QUADS + gi * (per // QUAD) + at // QUAD
                done = [0]

                def go(n):
                    for _ in range(n):
                        k = done[0]
                        done[0] += 1
                        q = k // QUAD
                        if k % QUAD == 0:
                            pe.wait_ge(s_acc, (quad0 + q) * 2 + 1)
                        pe.wait_ge(s_msg, s0 + (k + 2 + RING))
                        pe.matmul(ps_seg[q % 2][0:T, 0:AW], hot[:, k % QUAD, :], xg[:, k % RING, :],
                                  start=k % QUAD == 0, stop=k % QUAD == QUAD - 1).then_inc(s_seg, 1)
                return go

            def turn(j, u):
                pe.wait_ge(s_hT, u + (j if j else 1))
                pe.wait_ge(s_xh, u + (j + 1))
                transpose_rows(pe, ps_turn[j % 2], xh[:, j, :]).then_inc(s_tr, 1)

            with pe.Fori(0, GL) as g:
                with pe.Fori(0, 2) as h:
                    lay = g * 2 + h
                    pe.wait_ge(s_wqkv, (lay + 1) * (5 * 16))
                    def group_A(gi, last):
                        tn = (lay * NG + gi) * GT
                        u = lay * (2 * NT) + gi * GT
                        go = edge_steps(lay, 0, STEPS_A, gi)
                        for j in range(GT):
                            if j + 1 < GT:
                                turn(j + 1, u)
                            pe.wait_ge(s_hT, u + (j + 2))
                            pe.wait_ge(s_ev, tn + (j if j else 1))
                            qk, v = ps_mm[j % 2]
                            for c in range(KC):
                                pe.matmul(qk[0:T, :], hT[:, j, c, :], wqkv[:, c, 0:2 * D], start=c == 0, stop=c == KC - 1)
                            for c in range(KC):
                                ins = pe.matmul(v[0:T, 0:D], hT[:, j, c, :], wqkv[:, c, 2 * D:], start=c == 0,
                                                stop=c == KC - 1)
                            ins.then_inc(s_mm, 1)
                            go(1)
                        if not last:
                            turn(0, u + GT)
                        go(STEPS_A - GT)
                    turn(0, lay * (2 * NT))
                    with pe.Fori(0, NG - 1) as gi:
                        group_A(gi, False)
                    group_A(NG - 1, True)
                    go = edge_steps(lay, AT_C0, STEPS_C0, 0)
                    pe.wait_ge(s_km, lay * KM_STEPS + NT + 1)
                    transpose_rows(pe, ps_ctx, kmax[:, :]).then_inc(s_kmT, 1)
                    go(3)
                    pe.wait_ge(s_kdg, lay + 1)
                    for c in range(KC):
                        ins = pe.matmul(ps_ctx[0:T, c * P:(c + 1) * P], ones[:, 0:T], kdiag[:, c, :], start=True, stop=True)
                    ins.then_inc(s_kmB, 1)
                    go(STEPS_C0 - 3)
                    pe.wait_ge(s_km, lay * KM_STEPS + NT + 3)
                    pe.matmul(ps_ctx[:, 0:D + KC], ones[0:1, :], zrow[:, :], start=True, stop=False, skip_group_check=True)
                    with pe.Fori(0, NG) as gi:
                        tn = (lay * NG + gi) * GT
                        go = edge_steps(lay, AT_C, STEPS_C, gi)
                        go(2)
                        pe.wait_ge(s_ke, lay * NG + gi + 2)
                        for j in range(GT):
                            for c in range(KC):
                                vj = vbuf[:, ds(gi * GT + j, 1), c * P:(c + 1) * P].rearrange("p o d -> p (o d)")
                                pe.matmul(ps_ctx[:, c * P:(c + 1) * P], q5[:, j, c * P:(c + 1) * P], vj,
                                          start=False, stop=True, skip_group_check=True)
                                ins = pe.matmul(ps_ctx[:, D + c:D + c + 1], q5[:, j, c * P:(c + 1) * P], ones[0:T, 0:1],
                                                start=False, stop=True, skip_group_check=True)
                            if j == GT - 1:
                                ins.then_inc(s_ctx, 1)
                            go(1)
                        pe.wait_ge(s_qn, lay * NG + gi + 1)
                        for j in range(GT):
                            pe.wait_ge(s_qTe, tn + (j if j else 1))
                            transpose_rows(pe, ps_out[j % 2], qrow[:, j, :]).then_inc(s_qtr, 1)
                            if j % 2:
                                go(1)
                        go(STEPS_C - 9)
                    pe.wait_ge(s_wff, (lay + 1) * (8 * 16))
                    pe.wait_ge(s_cm, lay + 1)
                    for c in range(KC):
                        ins = pe.transpose(ps_tr[:, c * P:(c + 1) * P], ctxm[:, c, :], ident[:, :])
                    ins.then_inc(s_ctT, 1)
                    pe.wait_ge(s_cmT, lay + 1)
                    for c in range(KC):
                        ins = pe.matmul(ps_ctx[:, c * D:(c + 1) * D], ctxT[:, c, :], wo[:, c, :], start=True, stop=True)
                    ins.then_inc(s_cw, 1)
                    pe.wait_ge(s_cwr, lay + 1)

                    def attend(gi, j):
                        grp = lay * NG + gi
                        pe.wait_ge(s_qld, grp * 16 + 16)
                        pe.wait_ge(s_xa, grp * GT + (j if j else 1))
                        for c in range(KC):
                            ins = pe.matmul(ps_ao[j % 2][0:T, 0:D], qT[:, j, c, :], cwo[:, c, :], start=c == 0, stop=c == KC - 1)
                        ins.then_inc(s_ao, 1)

                    def turn_B(gi, j):
                        turn(j, lay * (2 * NT) + gi * GT + NT)

                    def group_B(gi, last):
                        tn = (lay * NG + gi) * GT
                        u = lay * (2 * NT) + gi * GT + NT
                        go = edge_steps(lay, AT_B, STEPS_B, gi)

                        def up(j):
                            for hf in range(2):
                                if hf == 0:
                                    pe.wait_ge(s_hT, u + (j + 2))
                                pe.wait_ge(s_gel, tn * 2 + (2 * j + hf + 1))
                                for f in range(FC // 2):
                                    ff = hf * (FC // 2) + f
                                    for c in range(KC):
                                        ins = pe.matmul(ps_hid[hf][:, f * T:(f + 1) * T], w1[:, c, ff * P:(ff + 1) * P],
                                                        hT[:, j, c, :], start=c == 0, stop=c == KC - 1)
                                ins.then_inc(s_up, 1)
                                go(1)

                        def down(j):
                            pe.wait_ge(s_xf, tn + (j if j else 1))
                            pe.wait_ge(s_gel, tn * 2 + (2 * j + 4))
                            for f in range(FC):
                                ins = pe.matmul(ps_out[j % 2][0:T, 0:D], gT[:, j % 2, f, :], w2[:, f, :],
                                                start=f == 0, stop=f == FC - 1)
                            ins.then_inc(s_fo, 1)
                        n = gi + 1
                        up(0)
                        for j in range(GT):
                            if j + 1 < GT:
                                up(j + 1)
                            if not last and j == 3:
                                turn_B(n, 0)
                                turn_B(n, 1)
                            if not last and j == 4:
                                turn_B(n, 2)
                                turn_B(n, 3)
                            down(j)
                            if not last and j == 0:
                                pe.wait_ge(s_hT, u + (GT + 1))
                                for a in range(3):
                                    attend(n, a)
                            if not last and j == 1:
                                attend(n, 3)
                                attend(n, 4)
                            if j < GT - 1:
                                go(1)
                        if not last:
                            turn_B(n, 4)
                        go(STEPS_B - 14)

                    go = edge_steps(lay, AT_B0, STEPS_B0, 0)
                    for j in range(GT):
                        attend(0, j)
                        if j >= 3:
                            go(1)
                    go(4)
                    for j in range(GT):
                        turn_B(0, j)
                    go(STEPS_B0 - 6)
                    with pe.Fori(0, NG - 1) as gi:
                        group_B(gi, False)
                    group_B(NG - 1, True)
                hold(pe, s_acc, (g + 1) * (4 * QUADS) + 3)
                with pe.If(pe.value_load(unsorted_i[0:1, 0:1], min_val=0, max_val=1) == 1):
                    with pe.Fori(0, GTILES * NT) as q:
                        pe.wait_ge(s_ghot, g * (GTILES * NT) + q + 1)
                        pe.matmul(ps_seg[0][0:T, 0:AW], hot[:, 0, :], xg[:, 0, :], start=True, stop=True).then_inc(s_gseg, 1)
                pe.wait_ge(s_gw, (g + 1) * (4 * 16))
                hold(pe, s_hr, (g + 1) * (NG * 16))
                with pe.Fori(0, NG) as gi:
                    dn = g * NT + gi * GT

                    def turn_sums(j):
                        pe.wait_ge(s_dT, dn + (j + 1))
                        pe.wait_ge(s_sc, dn + (j + 1))
                        for m in range(2):
                            transpose_rows(pe, ps_hid[0][:, m * KC * T:(m + 1) * KC * T], q5[:, (j % 2) * 2 + m, :])
                        transpose_rows(pe, ps_hid[1], xh[:, j % 2, :]).then_inc(s_dtr, 1)
                    turn_sums(0)
                    for j in range(GT):
                        pe.wait_ge(s_dT, dn + (j + 2))
                        if j + 1 < GT:
                            turn_sums(j + 1)
                        pe.wait_ge(s_db, dn + (j if j else 1))
                        for m in range(3):
                            for c in range(KC):
                                ins = pe.matmul(ps_out[j % 2][0:T, 0:D], gT[:, j % 2, m * KC + c, :],
                                                wg[:, m, c, :], start=m == 0 and c == 0, stop=m == 2 and c == KC - 1)
                        ins.then_inc(s_dy, 1)

            pe.wait_ge(s_ew, 16 * LAST_LOADS)
            pe.wait_ge(s_hn, GL * NT)
            with pe.Fori(0, NG) as gi:
                dn = gi * GT
                for j in range(GT):
                    if j == 0:
                        pe.wait_ge(s_exT, dn + 1)
                    pe.wait_ge(s_eT, dn + (j + 1))
                    pe.wait_ge(s_erow, gi + 1)
                    transpose_rows(pe, ps_tr, q5[:, j, :]).then_inc(s_etr, 1)
                    pe.wait_ge(s_eT, dn + (j + 2))
                    pe.wait_ge(s_emz, dn + (j + 1))
                    for c in range(KC):
                        ins = pe.matmul(ps_seg[1][0:T, 0:D], hT[:, j, c, :], mu_w[:, c, :], start=c == 0, stop=c == KC - 1)
                    ins.then_inc(s_emu, 1)
                for j in range(GT):
                    pe.wait_ge(s_exT, dn + (j + 1))
                    pe.wait_ge(s_exh, dn + (j + 1))
                    transpose_rows(pe, ps_tr, xh[:, j, :]).then_inc(s_ext, 1)
                for j in range(GT):
                    if j == 0:
                        pe.wait_ge(s_exT, dn + (GT + 1))
                    for c in range(KC):
                        ins = pe.matmul(ps_seg[1][0:T, j * NX:(j + 1) * NX], hT[:, j, c, :], gW[:, c, :], start=c == 0,
                                        stop=c == KC - 1)
                ins.then_inc(s_elg, 1)
                for j in range(GT):
                    pe.wait_ge(s_e1a, dn + (j + 1))
                    pe.wait_ge(s_e2a, dn + (j + 1))
                    for f in range(KC):
                        for c in range(KC):
                            pe.matmul(ps_hid[0][:, f * T:(f + 1) * T], sW1[:, c, f * P:(f + 1) * P], hT[:, j, c, :],
                                      start=c == 0, stop=c == KC - 1)
                    for e in range(NX):
                        for c in range(KC):
                            ins = pe.matmul(ps_hid[1][:, e * T:(e + 1) * T], eW1[:, e, c, :], hT[:, j, c, :],
                                            start=c == 0, stop=c == KC - 1)
                    ins.then_inc(s_e1, 1)
                    pe.wait_ge(s_e1a, dn + (j + 2))
                    for c in range(KC):
                        pe.matmul(ps_hid[0][:, 3 * P:3 * P + T], sW2[:, c, :], gT[:, 0, c, :], start=c == 0, stop=c == KC - 1)
                    for e in range(NX):
                        ins = pe.matmul(ps_ctx[0:EH2, e * T:(e + 1) * T], eW2[:, e, :], gT[:, 0, KC + e, :],
                                        start=True, stop=True)
                    ins.then_inc(s_e2, 1)
                    pe.wait_ge(s_e2a, dn + (j + 2))
                    pe.wait_ge(s_ez, dn + (j + 1))
                    pe.matmul(ps_qk[0:T, 0:D], gT[:, 1, 0, :], sW3, start=True, stop=True)
                    for e in range(NX):
                        o = (ps_qk[0:T, D:2 * D], ps_v[0:T, 0:D], ps_v[0:T, D:2 * D], ps_seg[0][0:T, 0:D])[e]
                        ins = pe.matmul(o, e2T_of(e), eW3[0:EH2 + 1, e, :], start=True, stop=True)
                    ins.then_inc(s_eo, 1)

        assert not START, "free buffers not handed out"


def kernel(**inputs):
    import concourse.bacc as bacc
    from concourse.bass_utils import run_bass_kernel_spmd

    nc = bacc.Bacc("TRN2", target_bir_lowering=False, num_devices=1)
    arrays, io = {}, {}
    for name, value in inputs.items():
        a = np.ascontiguousarray(value)
        arrays[name] = a
        io[name] = nc.dram_tensor(name, a.shape, mybir.dt.from_np(a.dtype), kind="ExternalInput").ap()
    out = nc.dram_tensor("out", inputs["x"].shape, F32, kind="ExternalOutput").ap()
    build(nc, io, out)
    return run_bass_kernel_spmd(nc, [arrays], core_ids=[0]).results[0]["out"]
```

```python
from contextlib import ExitStack

import numpy as np

import concourse.bass as bass
from concourse import mybir

F32 = mybir.dt.float32
I32 = mybir.dt.int32
ALU = mybir.AluOpType
ACT = mybir.ActivationFunctionType
AX = mybir.AxisListType.X
ds = bass.ds

P = 128
D = 256
KC = D // P
T = 125
GT = 5
HEADS, DH = 8, 32
EPS = 1e-5
RSQRT_SEED = float(0x5F3759DF)
FAR = 65536.0
RING = 8
SLOTS = 4
QUAD = 4
STEPS_A, STEPS_C0, STEPS_C, STEPS_B0, STEPS_B = 8, 8, 8, 8, 24


def build(nc, io, out):
    N = io["x"].shape[0]
    E = io["src"].shape[0]
    L, _, FF = io["L0_mix_W1"].shape
    FC = FF // P
    NT = N // T
    NG = NT // GT
    ET = E // T
    HALF = E // 2
    HT = -(-HALF // T)
    SPLIT = HALF // T
    SPLIT_COL = HALF % T
    assert ET - SPLIT == HT and T * NT == N and T * ET == E
    AT_C0 = NG * STEPS_A
    AT_C = AT_C0 + STEPS_C0
    AT_B0 = AT_C + NG * STEPS_C
    AT_B = AT_B0 + STEPS_B0
    STEPS = AT_B + NG * STEPS_B
    assert all(n % RING == 0 for n in (STEPS_A, STEPS_C0, STEPS_C, STEPS_B0, STEPS_B)) and RING % QUAD == 0
    assert STEPS >= HT
    QUADS = STEPS // QUAD
    SCH = STEPS // 2
    assert SCH % QUAD == 0
    CHUNKS = (0, SCH, SPLIT, SPLIT + SCH)
    NX = io["L0_ffn_eW1"].shape[0]
    EH2 = io["L0_ffn_eW2"].shape[2]
    GL = 2
    SCALE = float(DH) ** -0.25
    AW = D + 1
    assert L == 2 * GL
    PD_ROWS, PD_FALLS, PD_KEYS = 6, 21, 50
    PAIR_ROWS = max(r for r in range(1, P + 1) if (E - 1) % r == 0)
    PAIRS = (E - 1) // PAIR_ROWS
    GTILES = 2 * HT
    KM_STEPS = NT + 4
    LAST_LOADS = 15 + NX

    xn_d = nc.dram_tensor("xn_rows", [N, D], F32, kind="Internal").ap()
    h1_d = nc.dram_tensor("h1_rows", [N, D], F32, kind="Internal").ap()
    q_d = nc.dram_tensor("q_rows", [N, D], F32, kind="Internal").ap()
    qT_d = nc.dram_tensor("q_columns", [NG, P, GT * KC * T], F32, kind="Internal").ap()

    def group_rows(t, gi):
        return t[ds(gi * (GT * T), GT * T), :].rearrange("(j p) d -> p j d", p=T)

    with ExitStack() as ctx:
        def sb(name, shape, dt=F32):
            return ctx.enter_context(nc.sbuf_tensor(name, shape, dt))

        def sem(name):
            return ctx.enter_context(nc.semaphore(name))

        def bank(name):
            return ctx.enter_context(nc.psum_tensor(name, [P, 512], F32))
        ps_seg = [bank("ps_seg0"), bank("ps_seg1")]
        ps_tr = bank("ps_tr")
        ps_qk = bank("ps_qk")
        ps_v = bank("ps_v")
        ps_ctx = bank("ps_ctx")
        ps_turn = [ps_tr, ps_ctx]
        ps_ao = [ps_ctx, ps_tr]
        ps_out = [ps_qk, ps_v]
        ps_hid = [bank("ps_hid0"), bank("ps_hid1")]
        ps_mm = [(ps_qk, ps_v), (ps_hid[0], ps_hid[1])]

        xres = sb("xres", [T, NT, D])
        kbuf = sb("kbuf", [T, NT, D])
        vbuf = sb("vbuf", [T, NT, D])
        accp = sb("acc", [P, 2 * NT, AW])
        acc = accp[0:T]
        wqkv = sb("wqkv", [P, KC, 3 * D])
        wo = sb("wo", [P, KC, D])
        wff = sb("wff", [P, 2 * KC * FF])
        w1 = wff[:, 0:KC * FF].rearrange("p (c f) -> p c f", c=KC)
        w2 = wff[:, KC * FF:].rearrange("p (f d) -> p f d", f=FC)
        wg = wqkv[:, :, :].rearrange("p c n -> p (c n)").rearrange("p (m c n) -> p m c n", m=3, c=KC)
        ln1p = sb("ln1p", [P, 2, KC])
        ln2p = sb("ln2p", [P, 2, KC])
        b1p = sb("b1p", [P, FC])
        bo_b = sb("bo_b", [T, D])
        b2_b = sb("b2_b", [T, D])
        res_b = sb("res_b", [T, 1])

        idx_tab = sb("idx_tab", [T, 2 * STEPS, 2], I32)
        key_tab = sb("key_tab", [T, 2 * STEPS])
        in_tile = sb("in_tile", [T, 2 * QUADS, 2])
        row_tab = sb("row_tab", [1, 2 * QUADS, 2], I32)
        idx_now = sb("idx_now", [T, 2, RING, 2], I32)
        xg = sb("xg", [T, RING, AW])
        rg = sb("rg", [T, RING, D])
        zrow = sb("zrow", [1, D + KC])
        hot = sb("hot", [T, QUAD, T])
        iota_t = sb("iota_t", [T, T])
        ident = sb("ident", [P, P])
        ones = sb("ones", [P, P])
        head_mask = sb("head_mask", [P, P])

        xh = sb("xh", [T, GT, D])
        hT = sb("hT", [P, GT, KC, T])
        q5p = sb("q5", [P, GT * D])
        q5 = q5p[0:T, :].rearrange("p (j d) -> p j d", j=GT)
        qT = q5p[:, 0:GT * KC * T].rearrange("p (j c t) -> p j c t", j=GT, c=KC)
        gT = sb("gT", [P, 2, FC, T])
        kmax = sb("kmax", [T, D])
        flat_g = gT[:, :, :, :].rearrange("p s f t -> p (s f t)")
        qrow = flat_g[0:T, 0:GT * D].rearrange("p (j d) -> p j d", j=GT)
        kmaxT = sb("kmaxT", [P, KC])
        ksh = sb("ksh", [T, D])
        gb_b = ksh
        ctxm, ctxT = (flat_g[:, a:a + D].rearrange("p (c d) -> p c d", c=KC)
                      for a in (GT * D, GT * D + D))
        kdiag = ctxm
        rsum = sb("rsum", [P, KC])
        cwo = sb("cwo", [P, KC, D])
        qm = sb("qm", [T, GT * HEADS])
        stat = sb("stat", [T, GT, 6])
        mv = sb("mv", [T, GT, 2])
        var = sb("var", [T, GT])
        seed = sb("seed", [T, GT], I32)
        rstd = sb("rstd", [T, GT])
        tmp = sb("tmp", [T, GT])
        norm = qm[:, 0:NT]
        staged = [(q5[:, k, :], hT[0:T].rearrange("p j c t -> p (j c t)")[:, k * D:(k + 1) * D], xh[:, k, :])
                  for k in range(SLOTS)]

        step_rows = vbuf[0:SCH, 0:6, :].rearrange("p a d -> p (a d)")[:, 0:12 * T].bitcast(I32)\
            .rearrange("p (m c t) -> p m c t", m=3, c=4)
        step_rows_f = kbuf[0:SCH, 0:6, :].rearrange("p a d -> p (a d)")[:, 0:12 * T]\
            .rearrange("p (m c t) -> p m c t", m=3, c=4)
        ps_tab = [ps_seg[0], ps_seg[1], ps_tr, ps_qk]

        def early(i, rows, n):
            return kbuf[0:rows, 8 + 2 * i:10 + 2 * i, :].rearrange("p a d -> p (a d)")[:, 0:n]
        iota_i = early(0, T, T).bitcast(I32)
        part_i = early(1, T, 1).bitcast(I32)
        ramp_i, ramp = early(1, SCH, NT)[:, 1:NT].bitcast(I32), early(2, SCH, NT)[:, 1:NT]
        enum_i = early(3, SCH, 4 * T).bitcast(I32).rearrange("p (c t) -> p c t", c=4)
        enum = early(4, SCH, 4 * T).rearrange("p (c t) -> p c t", c=4)
        dropped = early(5, SCH, T)
        spans = early(6, SCH, 4 * T).rearrange("p (c t) -> p c t", c=4)
        first, tile_of, base, place, bad = (early(7, SCH, 4 * (i + 1))[:, 4 * i:] for i in range(5))
        reached = early(7, SCH, 64 + NT)[:, 64:64 + NT - 1]
        nspread = early(7, SCH, 120)[:, 119:120]
        place_row = vbuf[0:1, 16:18, :].rearrange("p a d -> p (a d)")[:, 0:2 * QUADS]
        tile_row = vbuf[0:1, 18:20, :].rearrange("p a d -> p (a d)")[:, 0:2 * QUADS]
        quad_first = vbuf[0:SCH, 20, 0:SCH]
        pair_a, pair_b = (vbuf[0:PAIR_ROWS, a:a + 2, :].rearrange("p a d -> p (a d)")[:, 0:PAIRS].bitcast(I32)
                          for a in (8, 10))
        falls = vbuf[0:PAIR_ROWS, 12:14, :].rearrange("p a d -> p (a d)")[:, 0:PAIRS]
        nfall = vbuf[0:PAIR_ROWS, 14, 0:1]
        unsorted_f = sb("unsorted_f", [T, 1])
        unsorted_i = sb("unsorted_i", [1, 1], I32)
        part = sb("part", [T, 1])
        gsrc, gtype, gdst = idx_now[:, 0, 0, 0:1], idx_now[:, 0, 0, 1:2], idx_now[:, 0, 1, 0:1]
        gedge, gkey = tmp[:, 0:1], tmp[:, 1:2]
        lmask = sb("lmask", [T, NX, NX])
        flat_acc = accp[:, :, :].rearrange("p a n -> p (a n)")
        last_at = [2 * AW]

        def last_buf(*shape, parts=T):
            n = int(np.prod(shape))
            v = flat_acc[0:parts, last_at[0]:last_at[0] + n]
            last_at[0] += n
            names = " ".join("abc"[:len(shape)])
            return v.rearrange(f"p ({names}) -> p {names}", **dict(zip("abc", shape))) if len(shape) > 1 else v
        hT_all = last_buf(NT, KC * T, parts=P)
        mv_all = last_buf(NT, 2)
        var_all, seed_all, rstd_all, tmp_all, gone = (last_buf(NT) for _ in range(5))
        lg, gate, gex = (last_buf(NT, NX) for _ in range(3))
        beat, beat2 = (last_buf(NT, NX, NX) for _ in range(2))
        assert last_at[0] <= 2 * NT * AW
        sb1p, sb2p, eb1p = b1p[:, 0:KC], b1p[:, KC:KC + 1], b1p[:, KC + 1:KC + 1 + NX]
        eb2p = ln2p[0:EH2].rearrange("p m c -> p (m c)")
        gateb = sb("gateb", [T, NX])

        START = {}

        def counted(name, start=0):
            s = sem(name)
            START[id(s)] = start
            return s

        s_x = sem("x_loaded")
        s_par = sem("params_loaded")
        s_const = sem("constants_made")
        s_clr = sem("table_rows_cleared")
        s_pair = sem("neighbours_loaded")
        s_tabl = sem("table_rows_loaded")
        s_pdve = sem("prologue_dve")
        s_ppe = sem("prologue_pe")
        s_ppool = sem("prologue_pool")
        s_tab = sem("tables_ready")
        s_xn_st = sem("xn_stored")
        s_h1_st = sem("h1_stored")
        s_out = sem("out_stored")
        s_edge = [sem(f"edge_gathered{i}") for i in range(RING)]
        s_idx = sem("idx_staged")
        s_claim = sem("slot_claimed")
        s_msg = counted("message_ready", RING + 1)
        s_seg = counted("segment_done", RING)
        s_acc = counted("acc_added", 3)
        s_zero = sem("acc_zeroed")
        s_gidx = sem("general_indices_loaded")
        s_ggat = sem("general_rows_gathered")
        s_gkey = sem("general_dve")
        s_ghot = sem("general_onehot_ready")
        s_gseg = sem("general_segment_done")
        s_gadd = counted("general_added", 1)
        s_xr = sem("x_ready")
        s_ln = sem("norm_dve")
        s_xh = sem("xh_ready")
        s_tr = counted("xh_transposed", GT)
        s_hT = counted("hT_ready", 1)
        s_mm = sem("qkv_done")
        s_wqkv = sem("wqkv_loaded")
        s_wff = sem("wff_loaded")
        s_ev = counted("qkv_copied", 1)
        s_qst = [counted(f"q_stored{j}", 16) for j in range(GT)]
        s_qrl = sem("q_rows_loaded")
        s_qtr = sem("q_transposed")
        s_qTe = counted("qT_copied", 1)
        s_qTst = counted("qT_stored", 16)
        s_qld = sem("q_loaded")
        s_qs = sem("q_shifted")
        s_qe = sem("q_exp")
        s_qn = sem("q_normed")
        s_qd = sem("q_dve")
        s_km = sem("kmax_dve")
        s_kmT = sem("kmax_transposed")
        s_kdg = sem("kmax_diagonal")
        s_kmB = sem("kmax_spread")
        s_ks = sem("k_shifted")
        s_ke = counted("k_exp", 1)
        s_ctx = counted("context_done", 1)
        s_ctT = sem("context_transposed")
        s_cmT = sem("context_turned")
        s_cm = sem("context_masked")
        s_cw = sem("context_wo_done")
        s_cwr = sem("context_wo_ready")
        s_ao = counted("attention_done", GT)
        s_b2 = sem("ffn_bias_added")
        s_xa = counted("x_attention_added", 1)
        s_up = sem("hidden_done")
        s_gel = counted("gelu_done", 2)
        s_fo = counted("ffn_done", 1)
        s_xf = counted("x_ffn_added", 1)
        s_gw = sem("graph_weights_loaded")
        s_hr = sem("h_rows_loaded")
        s_dd = sem("dense_dve")
        s_hx = [sem(f"h_tile_loaded{k}") for k in range(SLOTS)]
        s_sc = sem("sums_scaled")
        s_dtr = counted("dense_transposed", SLOTS)
        s_dT = counted("dense_T_ready", 1)
        s_bias = sem("attention_bias_added")
        s_dy = counted("dense_product_done", 2)
        s_db = counted("dense_biased", 2)
        s_dt = sem("dense_tanh")
        s_hn = sem("h_new_ready")
        s_ew = sem("last_weights_loaded")
        s_er = sem("last_rows_loaded")
        s_ed = sem("last_dve")
        s_erow = sem("h2_rows_staged")
        s_etr = counted("h2_transposed", GT)
        s_eT = counted("h2T_ready", 1)
        s_emu = counted("mu_done", 1)
        s_emz = counted("mu_added", 1)
        s_exh = sem("last_xh_ready")
        s_ext = counted("last_xh_transposed", GT)
        s_exT = counted("last_xhT_ready", 1)
        s_elg = sem("gate_logits_done")
        s_elr = counted("gate_logits_read", 1)
        s_esb = sem("shared_bias_added")
        s_egx = sem("gates_shifted")
        s_ege = sem("gates_exp")
        s_e1 = sem("last_hidden1_done")
        s_e1a = counted("last_hidden1_ready", 1)
        s_e2 = sem("last_hidden2_done")
        s_e2a = counted("last_hidden2_ready", 1)
        s_eo = counted("experts_done", 1)
        s_ez = counted("row_combined", 1)

        block = ctx.enter_context(nc.Block())

        class Chain:

            def __init__(self, eng, s, base=0):
                self.eng, self.s, self.base, self.n = eng, s, base, 0

            def __call__(self, ins):
                ins.then_inc(self.s, 1)
                self.n += 1

            def wait(self):
                self.eng.wait_ge(self.s, self.base + self.n)

        def hold(eng, s, value):
            eng.wait_ge(s, value)
            eng.sem_inc(s_claim, 1)

        def inv_sqrt(dve, chain, variance, v, bits, y, t, between=lambda: None):
            chain(dve.tensor_scalar(v, variance, EPS, None, ALU.add))
            chain.wait()
            chain(dve.tensor_scalar(bits, v.bitcast(I32), 1, None, ALU.arith_shift_right))
            chain.wait()
            chain(dve.tensor_scalar(y.bitcast(I32), bits, -1.0, RSQRT_SEED, ALU.mult, ALU.add))
            for newton in range(4):
                if newton == 2:
                    between()
                chain.wait()
                chain(dve.scalar_tensor_tensor(t, y, -0.5, v, ALU.mult, ALU.mult))
                chain.wait()
                chain(dve.tensor_tensor(t, t, y, ALU.mult))
                chain.wait()
                chain(dve.scalar_tensor_tensor(y, t, 1.5, y, ALU.add, ALU.mult))

        def norm_stats(dve, chain, rows, between=lambda: None):
            for j in range(GT):
                chain(dve.bn_stats(stat[:, j, :], rows(j)))
            between()
            hold(dve, chain.s, chain.base + chain.n)
            for j in range(GT):
                chain(dve.bn_aggr(mv[:, j, :], stat[:, j, :]))
            between()
            chain.wait()
            inv_sqrt(dve, chain, mv[:, :, 1], var[:, :], seed[:, :], rstd[:, :], tmp[:, :], between)
            chain.wait()
        NORM_STEPS = 2 * GT + 3 + 12

        def norm_rows(dve, j, rows):
            return dve.tensor_scalar(xh[:, j, :], rows, mv[:, j, 0:1], rstd[:, j:j + 1], ALU.subtract, ALU.mult)

        def transpose_rows(pe, dst, rows):
            for c in range(KC):
                ins = pe.transpose(dst[:, c * T:(c + 1) * T], rows[:, c * P:(c + 1) * P], ident[0:T, 0:T])
            return ins

        def columns(v):
            return v.rearrange("(c p) -> p c", p=P)

        def rows_of(w):
            return w.rearrange("(c p) n -> p c n", p=P)

        def flat_qT(t):
            return t[:, :, :, :].rearrange("p j c t -> p (j c t)")

        def start(eng, *sems):
            for s in sems:
                eng.sem_inc(s, START.pop(id(s)))

        def dense_tiles(eng, tile):
            tile(0, 0, True, False)
            with eng.Fori(0, (NT - 2) // SLOTS) as it:
                for j in range(1, SLOTS + 1):
                    tile(it * SLOTS + j, j, False, False)
            for t in range((NT - 2) // SLOTS * SLOTS + 1, NT):
                tile(t, t, False, t)

        offs, at = {}, 0
        for name, cols in (("mu", KC * D), ("sW1", KC * D), ("sW2", KC * P), ("sW3", D), ("eW1", NX * KC * P),
                           ("eW2", NX * EH2), ("eW3", NX * D), ("gW", KC * NX)):
            offs[name] = (at, at + cols)
            at += cols
        assert at <= 2 * KC * FF

        def last_w(name, c):
            a, b = offs[name]
            return wff[:, a:b].rearrange("p (c n) -> p c n", c=c)

        mu_w, sW1, sW2, gW = (last_w(n, KC) for n in ("mu", "sW1", "sW2", "gW"))
        sW3 = last_w("sW3", 1)[:, 0, :]
        eW1 = last_w("eW1", NX).rearrange("p e (c n) -> p e c n", c=KC)
        eW2, eW3 = last_w("eW2", NX), last_w("eW3", NX)
        e2T = acc[0:EH2 + 1, 0:2, 0:2 * T].rearrange("p a (b t) -> p a b t", t=T)

        def e2T_of(e):
            return e2T[:, e // 2, e % 2, :]

        @block.sync
        def _(sp):
            for gi in range(NG):
                sp.dma_start(xres[:, gi * GT:(gi + 1) * GT, :], group_rows(io["x"], gi)).then_inc(s_x, 16)
            sp.wait_ge(s_clr, 1)
            for m, name in enumerate(("src", "dst", "edge_type_400")):
                for ch, at in enumerate(CHUNKS):
                    n = min(SCH, ET - at)
                    sp.dma_start(step_rows[0:n, m, ch, :], io[name][at * T:(at + n) * T].rearrange("(t p) -> t p", p=T))\
                        .then_inc(s_tabl, 16)
            for t, lag in ((pair_a, 0), (pair_b, 1)):
                sp.dma_start(t, io["dst"][lag:lag + E - 1].rearrange("(p n) -> p n", p=PAIR_ROWS)).then_inc(s_pair, 16)
            sp.dma_start(res_b[:, :], io["L0_gnn_res"].partition_broadcast(T)).then_inc(s_par, 16)
            for gi in range(NG):
                sp.wait_ge(s_xr, gi + 1)
                sp.dma_start(group_rows(xn_d, gi), xres[:, gi * GT:(gi + 1) * GT, :]).then_inc(s_xn_st, 16)

            def load_qkv(lay):
                for m, name in enumerate(("Wq", "Wk", "Wv")):
                    sp.dma_start(wqkv[:, :, m * D:(m + 1) * D], rows_of(io[f"L0_mix_{name}"][lay])).then_inc(s_wqkv, 16)
                sp.dma_start(ln1p[:, 0, :], columns(io["L0_mix_ln1_g"][lay]),
                             allow_slow_non_contiguous=True).then_inc(s_wqkv, 16)
                sp.dma_start(ln1p[:, 1, :], columns(io["L0_mix_ln1_b"][lay]),
                             allow_slow_non_contiguous=True).then_inc(s_wqkv, 16)

            def load_ff(lay):
                sp.dma_start(wo[:, :, :], rows_of(io["L0_mix_Wo"][lay])).then_inc(s_wff, 16)
                sp.dma_start(w1, rows_of(io["L0_mix_W1"][lay])).then_inc(s_wff, 16)
                sp.dma_start(w2, rows_of(io["L0_mix_W2"][lay])).then_inc(s_wff, 16)
                sp.dma_start(ln2p[:, 0, :], columns(io["L0_mix_ln2_g"][lay]),
                             allow_slow_non_contiguous=True).then_inc(s_wff, 16)
                sp.dma_start(ln2p[:, 1, :], columns(io["L0_mix_ln2_b"][lay]),
                             allow_slow_non_contiguous=True).then_inc(s_wff, 16)
                sp.dma_start(b1p[:, :], columns(io["L0_mix_b1"][lay]),
                             allow_slow_non_contiguous=True).then_inc(s_wff, 16)
                sp.dma_start(bo_b[:, :], io["L0_mix_bo"][lay].partition_broadcast(T)).then_inc(s_wff, 16)
                sp.dma_start(b2_b[:, :], io["L0_mix_b2"][lay].partition_broadcast(T)).then_inc(s_wff, 16)

            load_qkv(0)
            for lay in range(L):
                g, h = lay // 2, lay % 2
                sp.wait_ge(s_xr, NG * (lay + 1))
                load_ff(lay)
                with sp.Fori(0, NG) as gi:
                    for j in range(GT):
                        sp.wait_ge(s_ev, gi * GT + (j + 2 + lay * NT))
                        sp.dma_start(q_d[ds(gi * (GT * T) + j * T, T), :], q5[:, j, :]).then_inc(s_qst[j], 16)
                if h == 0:
                    load_qkv(lay + 1)
                else:
                    for m, name in enumerate(("W_in", "W_out", "W_loop")):
                        sp.dma_start(wg[:, m], rows_of(io[f"L0_gnn_{name}{g + 1}"])).then_inc(s_gw, 16)

                def load_q(gi):
                    sp.dma_start(qrow, group_rows(q_d, gi)).then_inc(s_qrl, 16)

                def store_qT(gi):
                    sp.wait_ge(s_qTe, gi * GT + (1 + GT + lay * NT))
                    sp.dma_start(qT_d[ds(gi, 1)].rearrange("o p n -> p (o n)"), flat_qT(hT)).then_inc(s_qTst, 16)
                for j in range(GT):
                    sp.wait_ge(s_qst[j], 16 + 16 * NG * (lay + 1))
                load_q(0)
                with sp.Fori(0, NG - 1) as gi:
                    sp.wait_ge(s_qtr, gi * GT + (GT + lay * NT))
                    load_q(gi + 1)
                    store_qT(gi)
                store_qT(NG - 1)
                sp.wait_ge(s_qTst, 16 + 16 * NG * (lay + 1))
                sp.wait_ge(s_ctx, 1 + (lay + 1) * NG)
                with sp.Fori(0, NG) as gi:
                    sp.wait_ge(s_ao, gi * GT + (GT + lay * NT))
                    sp.dma_start(flat_qT(qT), qT_d[ds(gi, 1)].rearrange("o p n -> p (o n)")).then_inc(s_qld, 16)
                if h == 1:
                    if g == 0:
                        sp.wait_ge(s_xn_st, 16 * NG)
                    else:
                        sp.wait_ge(s_h1_st, 16 * NG)
                    sp.dma_start(gb_b[:, :], io[f"L0_gnn_b{g + 1}"].partition_broadcast(T)).then_inc(s_gw, 16)
                    for gi in range(NG):
                        sp.dma_start(kbuf[:, gi * GT:(gi + 1) * GT, :],
                                     group_rows((xn_d, h1_d)[g], gi)).then_inc(s_hr, 16)
                    sp.wait_ge(s_tr, (lay + 1) * (2 * NT) + GT)

                    def load_h(it, n):
                        for k in range(n):
                            sp.wait_ge(s_dtr, it * SLOTS + (g * NT + k + 1))
                            sp.dma_start(staged[k][2], (xn_d, h1_d)[g][ds(it * (SLOTS * T) + k * T, T), :])\
                                .then_inc(s_hx[k], 16)

                    def store_h1(gi):
                        sp.wait_ge(s_hn, gi * GT + GT)
                        sp.dma_start(group_rows(h1_d, gi), vbuf[:, ds(gi * GT, GT), :]).then_inc(s_h1_st, 16)
                    load_h(0, SLOTS)
                    load_h(1, SLOTS)
                    with sp.Fori(0, NG - 1) as it:
                        load_h(it + 2, SLOTS)
                        if g == 0:
                            store_h1(it)
                    for it in range(NG + 1, -(-NT // SLOTS)):
                        load_h(it, min(SLOTS, NT - it * SLOTS))
                    if g == 0:
                        store_h1(NG - 1)
                        load_qkv(lay + 1)
            sp.wait_ge(s_xr, NG * (L + 1))
            for t, src in (
                (mu_w, rows_of(io["L0_gnn_mu_w"])), (sW1, rows_of(io["L0_ffn_sW1"])), (sW2, rows_of(io["L0_ffn_sW2"])),
                (sW3, io["L0_ffn_sW3"]), (eW2, io["L0_ffn_eW2"].rearrange("e p n -> p e n")),
                (eW3[0:EH2], io["L0_ffn_eW3"].rearrange("e p n -> p e n")),
                (eW3[EH2:EH2 + 1], io["L0_ffn_eb3"].rearrange("(o e) n -> o e n", o=1)),
                (gW, rows_of(io["L0_ffn_gW"])), (sb1p, columns(io["L0_ffn_sb1"])),
                (sb2p, columns(io["L0_ffn_sb2"])), (eb1p, io["L0_ffn_eb1"].rearrange("e p -> p e")),
                (eb2p, io["L0_ffn_eb2"].rearrange("e p -> p e")),
                (bo_b[:, :], io["L0_gnn_mu_b"].partition_broadcast(T)),
                (b2_b[:, :], io["L0_ffn_sb3"].partition_broadcast(T)),
                (gateb[:, :], io["L0_ffn_gb"].partition_broadcast(T)),
            ):
                sp.dma_start(t, src, allow_slow_non_contiguous=True).then_inc(s_ew, 16)
            for e in range(NX):
                sp.dma_start(eW1[:, e], rows_of(io["L0_ffn_eW1"][e])).then_inc(s_ew, 16)
            sp.wait_ge(s_hn, GL * NT)
            for gi in range(NG):
                sp.dma_start(kbuf[:, gi * GT:(gi + 1) * GT, :], group_rows(io["x"], gi)).then_inc(s_er, 16)
            for gi in range(NG):
                sp.wait_ge(s_ez, 1 + (gi + 1) * GT)
                sp.dma_start(group_rows(out, gi), kbuf[:, gi * GT:(gi + 1) * GT, :]).then_inc(s_out, 16)
            sp.wait_ge(s_out, 16 * NG)

        @block.gpsimd
        def _(pool):
            pool.memset(step_rows[:, :, 3, :], 0).then_inc(s_clr, 1)
            pool.memset(ones[:, :], 1.0)
            pool.memset(zrow[:, :], 0.0)
            pool.memset(ident[:, :], 0.0)
            pool.memset(quad_first, 0.0)
            pool.memset(xg[:, :, D:AW], 1.0)
            pool.iota(part_i, [[0, 1]], base=0, channel_multiplier=1)
            pool.iota(ramp_i, [[T, NT - 1]], base=T, channel_multiplier=0)
            for ch, at in enumerate(CHUNKS):
                pool.iota(enum_i[:, ch, :], [[1, T]], base=at * T, channel_multiplier=T)
            pool.iota(iota_i, [[1, T]], base=0, channel_multiplier=0).then_inc(s_ppool, 1)
            pool.wait_ge(s_ppool, 1)
            pool.affine_select(out=ident[:, :], in_=ident[:, :], compare_op=ALU.not_equal, fill=1.0, base=0,
                               pattern=[[-1, P]], channel_multiplier=1)
            pool.affine_select(out=quad_first, in_=quad_first, compare_op=ALU.not_equal, fill=1.0, base=0,
                               pattern=[[-QUAD, SCH // QUAD], [0, QUAD]], channel_multiplier=1)
            pool.tensor_copy(iota_t[:, :], iota_i).then_inc(s_const, 1)
            pool.memset(acc[:, :, :], 0.0).then_inc(s_zero, 1)

            pool.wait_ge(s_tab, 1)
            for g in range(GL):
                rows, stored = ((xn_d, s_xn_st), (h1_d, s_h1_st))[g]
                pool.wait_ge(stored, 16 * NG)
                with pool.Fori(0, 2 * STEPS // (2 * RING)) as it:
                    for half in range(2):
                        s0 = it * (2 * RING) + (g * 2 * STEPS + half * RING)
                        pool.wait_ge(s_msg, s0 + 1)
                        pool.tensor_copy(idx_now[:, half], idx_tab[:, ds(it * (2 * RING) + half * RING, RING), :])\
                            .then_inc(s_idx, 1)
                        pool.wait_ge(s_idx, it * 2 + (g * 2 * STEPS // RING + half + 1))
                        for k in range(RING):
                            pool.wait_ge(s_seg, s0 + (k + 1))
                            pool.sem_inc(s_claim, 1)
                            pool.indirect_dma_start(
                                xg[:, k, 0:D], None, rows,
                                bass.IndirectOffsetOnAxis(ap=idx_now[:, half, k, 0:1], axis=0)).then_inc(s_edge[k], 16)
                            pool.indirect_dma_start(
                                rg[:, k, :], None, io[f"L0_gnn_rel{g + 1}"],
                                bass.IndirectOffsetOnAxis(ap=idx_now[:, half, k, 1:2], axis=0)).then_inc(s_edge[k], 16)
                hold(pool, s_seg, (g + 1) * (2 * STEPS) + RING)
                with pool.If(pool.value_load(unsorted_i[0:1, 0:1], min_val=0, max_val=1) == 1):
                    for half in range(2):
                        with pool.Fori(0, HT) as i:
                            n = i + (g * 2 + half) * HT
                            hold(pool, s_gadd, n * NT + 1)
                            for t, name in ((gsrc, "src"), (gtype, "edge_type_400"), (gdst, "dst")):
                                pool.dma_start(t, io[name][ds(i * T + half * SPLIT * T, T)].rearrange("(p o) -> p o", o=1),
                                               allow_slow_non_contiguous=True).then_inc(s_gidx, 16)
                            hold(pool, s_gidx, n * 48 + 48)
                            pool.indirect_dma_start(
                                xg[:, 0, 0:D], None, rows,
                                bass.IndirectOffsetOnAxis(ap=gsrc, axis=0)).then_inc(s_ggat, 16)
                            pool.indirect_dma_start(
                                rg[:, 0, :], None, io[f"L0_gnn_rel{g + 1}"],
                                bass.IndirectOffsetOnAxis(ap=gtype, axis=0)).then_inc(s_ggat, 16)

        @block.vector
        def _(dve):
            start(dve, s_gadd, s_msg, s_acc, s_xa, s_xf, s_db, s_emz, s_ez, s_elr)

            for gi in range(NG):
                dve.wait_ge(s_x, 16 * NG)
                chain = Chain(dve, s_ln, gi * (NORM_STEPS + GT))
                norm_stats(dve, chain, lambda j: xres[:, gi * GT + j, :])
                for j in range(GT):
                    row = xres[:, gi * GT + j, :]
                    chain(dve.tensor_scalar(row, row, mv[:, j, 0:1], rstd[:, j:j + 1], ALU.subtract, ALU.mult))
                chain.wait()
                dve.sem_inc(s_xr, 1)
            LN0 = NG * (NORM_STEPS + GT)

            p = Chain(dve, s_pdve)
            dve.memset(lmask[:, :, :], 0.0)
            p(dve.memset(head_mask[:, :], 0.0))
            p.wait()
            for hd in range(P // DH):
                dve.memset(head_mask[hd * DH:(hd + 1) * DH, hd * DH:(hd + 1) * DH], 1.0)
            for e in range(1, NX):
                dve.memset(lmask[:, e, 0:e], 1.0)
            dve.wait_ge(s_const, 1)
            p(dve.tensor_copy(part[:, :], part_i))
            p(dve.tensor_copy(ramp, ramp_i))
            p(dve.tensor_copy(enum, enum_i))
            dve.wait_ge(s_tabl, 16 * 12)
            for m in (0, 2):
                dve.tensor_copy(step_rows_f[:, m], step_rows[:, m])
            p(dve.tensor_copy(step_rows_f[:, 1], step_rows[:, 1]))
            dve.wait_ge(s_pair, 2 * 16)
            p(dve.tensor_tensor(falls, pair_a, pair_b, ALU.is_gt))
            assert p.n == PD_ROWS
            p.wait()
            p(dve.tensor_reduce(nfall, falls, AX, ALU.add))
            dve.wait_ge(s_ppe, 1)
            p(dve.tensor_copy(first, ps_hid[0][0:SCH, 0:4]))
            p.wait()
            for ch in range(4):
                p(dve.tensor_scalar(reached, ramp, first[:, ch:ch + 1], None, ALU.is_le))
                p.wait()
                p(dve.tensor_reduce(tile_of[:, ch:ch + 1], reached, AX, ALU.add))
                p.wait()
                dve.tensor_scalar(spans[:, ch, :], step_rows_f[:, 1, ch, :], first[:, ch:ch + 1], float(T),
                                  ALU.subtract, ALU.is_ge)
            p(dve.tensor_scalar(base, tile_of, -float(T), None, ALU.mult))
            p.wait()
            p(dve.tensor_tensor(place, first, base, ALU.add))
            p(dve.tensor_reduce(bad, spans, AX, ALU.add))
            p.wait()
            p(dve.tensor_reduce(nspread, bad, AX, ALU.add))
            p(dve.tensor_scalar(tile_of[:, 2:4], tile_of[:, 2:4], float(NT), None, ALU.add))
            p.wait()
            assert p.n == PD_FALLS, p.n
            for ch in range(4):
                key = step_rows_f[:, 1, ch, :]
                p(dve.tensor_scalar(key, key, base[:, ch:ch + 1], None, ALU.add))
                p.wait()
                p(dve.tensor_scalar(dropped, key, float(T), -float(T), ALU.is_ge, ALU.mult))
                p.wait()
                p(dve.tensor_tensor(key, key, dropped, ALU.add))
                p.wait()
                for edge, op in (((HALF, ALU.is_ge),) if ch < 2 else ((HALF, ALU.is_lt), (E, ALU.is_ge))):
                    dve.tensor_scalar(dropped, enum[:, ch, :], float(edge), FAR, op, ALU.mult).then_inc(s_pdve, 1)
                    p.n += 1
                    p.wait()
                    p(dve.tensor_tensor(key, key, dropped, ALU.add))
                    p.wait()
            dve.wait_ge(s_ppe, 2)
            p(dve.tensor_scalar(unsorted_f[:, :], ps_hid[1][0:T, 0:1], 1.0, None, ALU.min))
            p.wait()
            p(dve.tensor_copy(unsorted_i[:, :], unsorted_f[0:1, :]))
            p.wait()
            p(dve.tensor_scalar(unsorted_f[:, :], unsorted_f[:, :], FAR, None, ALU.mult))
            p.wait()
            for m, row_f in ((0, tile_row), (1, place_row)):
                dve.wait_ge(s_ppe, 3 + m)
                p(dve.tensor_copy(row_f, (ps_tr, ps_qk)[m][0:1, 0:2 * STEPS].rearrange("p (q s) -> p q s", s=QUAD)[:, :, 0]))
            p.wait()
            assert p.n == PD_KEYS, p.n
            p(dve.tensor_copy(row_tab[:, :, 0], tile_row))
            p(dve.tensor_scalar(tile_row, tile_row, 1.0, None, ALU.add))
            p.wait()
            for h in range(2):
                half_row = tile_row[:, h * QUADS:(h + 1) * QUADS]
                p(dve.tensor_scalar(row_tab[:, h * QUADS:(h + 1) * QUADS, 1], half_row, float(h * NT + NT - 1), None, ALU.min))
            for m, tab in ((0, idx_tab[:, :, 0]), (1, key_tab[:, :]), (2, idx_tab[:, :, 1])):
                dve.wait_ge(s_ppe, 5 + m)
                if m == 1:
                    p(dve.tensor_scalar(tab, ps_tab[m][0:T, 0:2 * STEPS], unsorted_f[:, 0:1], None, ALU.add))
                else:
                    p(dve.tensor_copy(tab, ps_tab[m][0:T, 0:2 * STEPS]))
            dve.wait_ge(s_ppe, 8)
            for m, op in enumerate((ALU.is_le, ALU.is_gt)):
                p(dve.tensor_scalar(in_tile[:, :, m], ps_v[0:T, 0:2 * QUADS], part[:, 0:1], None, op))
            p.wait()
            dve.sem_inc(s_tab, 1)

            dve.wait_ge(s_zero, 1)

            def edge_steps(h, lay, at, per, gi):
                s0 = lay * STEPS + gi * per + at
                slot0 = lay * (STEPS // RING) + gi * (per // RING) + at // RING
                t0 = h * STEPS + gi * per + at
                quad0 = lay * QUADS + gi * (per // QUAD) + at // QUAD
                quad_t0 = h * QUADS + gi * (per // QUAD) + at // QUAD
                done = [0]
                rows = []

                def add(q):
                    dve.wait_ge(s_seg, s0 + (QUAD * (q + 1) + RING))
                    for m in range(2):
                        dve.wait_ge(s_acc, (quad0 + q) * 2 + (m + 3))
                        a = acc[:, ds(rows[2 * q + m], 1), :].rearrange("p o n -> p (o n)")
                        dve.scalar_tensor_tensor(a, ps_seg[q % 2][0:T, 0:AW], in_tile[:, ds(quad_t0 + q, 1), m], a,
                                                 ALU.mult, ALU.add).then_inc(s_acc, 1)

                def go(n):
                    for _ in range(n):
                        k = done[0]
                        done[0] += 1
                        if k % RING == 0:
                            rows.extend(nc.values_load_multi_w_load_instructions(
                                row_tab[0:1, ds(quad_t0 + k // QUAD, RING // QUAD), :].rearrange("p q m -> p (q m)"),
                                engines=(mybir.EngineType.DVE,),
                                min_val=0, max_val=2 * NT - 1, skip_runtime_bounds_check_because="clamped above")[1])
                        dve.wait_ge(s_seg, s0 + (k + 1 + RING - QUAD))
                        dve.tensor_scalar(hot[:, k % QUAD, :], iota_t[:, :], key_tab[:, ds(t0 + k, 1)], None, ALU.is_equal)
                        dve.wait_ge(s_edge[k % RING], slot0 * 32 + 32 * (k // RING + 1))
                        m = xg[:, k % RING, 0:D]
                        dve.tensor_tensor(m, m, rg[:, k % RING, :], ALU.mult).then_inc(s_msg, 1)
                        if k % QUAD == QUAD - 2 and k >= QUAD:
                            add(k // QUAD - 1)

                def end():
                    assert done[0] == per, (done, per)
                    add(per // QUAD - 1)
                return go, end

            with dve.Fori(0, GL) as g:
                with dve.Fori(0, 2) as h:
                    lay = g * 2 + h
                    dve.memset(kmax[:, :], -3.0e38).then_inc(s_km, 1)

                    def row(gi, j):
                        return xres[:, ds(gi * GT + j, 1), :].rearrange("p o d -> p (o d)")

                    def stats_A(gi, between=lambda: None):
                        chain = Chain(dve, s_ln, (lay * (2 * NG) + gi) * NORM_STEPS + LN0)
                        hold(dve, s_xr, lay * NG + gi + 1)
                        norm_stats(dve, chain, lambda j: row(gi, j), between)

                    def norm_A(gi, j):
                        dve.wait_ge(s_tr, lay * (2 * NT) + gi * GT + (j + 1))
                        norm_rows(dve, j, row(gi, j)).then_inc(s_xh, 1)

                    def group_A(gi, last):
                        tn = (lay * NG + gi) * GT
                        go, end = edge_steps(h, lay, 0, STEPS_A, gi)
                        km = Chain(dve, s_km, lay * KM_STEPS + gi * GT + 1)

                        def k_max(j):
                            km.wait()
                            dve.wait_ge(s_ev, tn + (j + 2))
                            k = kbuf[:, ds(gi * GT + j, 1), :].rearrange("p o d -> p (o d)")
                            km(dve.tensor_tensor(kmax[:, :], kmax[:, :], k, ALU.max))
                        beside = [0]

                        def between():
                            go(1)
                            if beside[0] in (1, 2):
                                k_max(beside[0] - 1)
                            beside[0] += 1
                        go(1)
                        if last:
                            for _ in range(3):
                                between()
                        else:
                            stats_A(gi + 1, between)
                            for j in range(3):
                                norm_A(gi + 1, j)
                        k_max(2)
                        go(1)
                        if not last:
                            norm_A(gi + 1, 3)
                            norm_A(gi + 1, 4)
                        k_max(3)
                        go(2)
                        k_max(4)
                        go(STEPS_A - 7)
                        end()
                    stats_A(0)
                    for j in range(GT):
                        norm_A(0, j)
                    with dve.Fori(0, NG - 1) as gi:
                        group_A(gi, False)
                    group_A(NG - 1, True)

                    go, end = edge_steps(h, lay, AT_C0, STEPS_C0, 0)
                    km = Chain(dve, s_km, lay * KM_STEPS + NT + 1)
                    dve.wait_ge(s_kmT, lay + 1)
                    km(dve.tensor_reduce(kmaxT[:, :], ps_ctx[:, 0:KC * T].rearrange("p (c t) -> p c t", c=KC), AX, ALU.max))
                    km.wait()
                    for c in range(KC):
                        ins = dve.tensor_scalar(kdiag[:, c, :], ident[:, :], kmaxT[:, c:c + 1], None, ALU.mult)
                    ins.then_inc(s_kdg, 1)
                    go(4)
                    dve.wait_ge(s_kmB, lay + 1)
                    km(dve.tensor_copy(ksh[:, :], ps_ctx[0:T, 0:D]))
                    go(STEPS_C0 - 4)
                    end()
                    hold(dve, s_km, km.base + km.n)
                    def k_shift(gi):
                        k5 = kbuf[:, ds(gi * GT, GT), :]
                        dve.wait_ge(s_ke, lay * NG + gi + 1)
                        dve.tensor_tensor(xh[:, :, :], k5, ksh[:, :].unsqueeze(1).broadcast_to([T, GT, D]), ALU.subtract)\
                            .then_inc(s_ks, 1)

                    def group_C(gi, last):
                        grp = lay * NG + gi
                        go, end = edge_steps(h, lay, AT_C, STEPS_C, gi)
                        go(2)
                        qd = Chain(dve, s_qd, grp * 3)
                        qh = qrow.rearrange("p j (h e) -> p (j h) e", e=DH)
                        qmb = qm[:, :].unsqueeze(2).broadcast_to([T, GT * HEADS, DH])
                        dve.wait_ge(s_qrl, grp * 16 + 16)
                        qd(dve.tensor_reduce(qm[:, :], qh, AX, ALU.max))
                        go(1)
                        qd.wait()
                        dve.tensor_tensor(qh, qh, qmb, ALU.subtract).then_inc(s_qs, 1)
                        go(2)
                        if not last:
                            k_shift(gi + 1)
                        dve.wait_ge(s_qe, grp + 1)
                        qd(dve.tensor_reduce(qm[:, :], qh, AX, ALU.add))
                        qd.wait()
                        qd(dve.reciprocal(qm[:, :], qm[:, :]))
                        go(1)
                        qd.wait()
                        dve.tensor_tensor(qh, qh, qmb, ALU.mult).then_inc(s_qn, 1)
                        go(STEPS_C - 6)
                        x5 = xres[:, ds(gi * GT, GT), :]
                        dve.wait_ge(s_wff, (lay + 1) * (8 * 16))
                        dve.tensor_tensor(x5, x5, bo_b[:, :].unsqueeze(1).broadcast_to([T, GT, D]), ALU.add).then_inc(s_bias, 1)
                        end()
                    k_shift(0)
                    with dve.Fori(0, NG - 1) as gi:
                        group_C(gi, False)
                    group_C(NG - 1, True)
                    dve.wait_ge(s_ctx, (lay + 1) * NG + 1)
                    km(dve.reciprocal(rsum[:, :], ps_ctx[:, D:D + KC]))
                    km.wait()
                    for c in range(KC):
                        ins = dve.scalar_tensor_tensor(ctxm[:, c, :], ps_ctx[:, c * P:(c + 1) * P], rsum[:, c:c + 1],
                                                       head_mask[:, :], ALU.mult, ALU.mult)
                    ins.then_inc(s_cm, 1)
                    dve.wait_ge(s_ctT, lay + 1)
                    dve.tensor_copy(ctxT[:, :, :].rearrange("p c d -> p (c d)"), ps_tr[:, 0:D]).then_inc(s_cmT, 1)
                    dve.wait_ge(s_cw, lay + 1)
                    dve.tensor_copy(cwo[:, :, :].rearrange("p c d -> p (c d)"), ps_ctx[:, :]).then_inc(s_cwr, 1)

                    hold(dve, s_wff, (lay + 1) * (8 * 16))

                    def add_attention(gi, j):
                        dve.wait_ge(s_ao, (lay * NG + gi) * GT + (GT + j + 1))
                        dve.tensor_tensor(row(gi, j), row(gi, j), ps_ao[j % 2][0:T, 0:D], ALU.add).then_inc(s_xa, 1)

                    def stats_B(gi, between=lambda: None):
                        chain = Chain(dve, s_ln, (lay * (2 * NG) + gi + NG) * NORM_STEPS + LN0)
                        hold(dve, s_xa, (lay * NG + gi) * GT + (1 + GT))
                        norm_stats(dve, chain, lambda j: row(gi, j), between)

                    def norm_B(gi, j):
                        dve.wait_ge(s_tr, lay * (2 * NT) + gi * GT + (NT + j + 1))
                        norm_rows(dve, j, row(gi, j)).then_inc(s_xh, 1)

                    def add_b2(gi):
                        dve.wait_ge(s_xh, (lay * (2 * NG) + gi + (NG + 1)) * GT)
                        x5 = xres[:, ds(gi * GT, GT), :]
                        dve.tensor_tensor(x5, x5, b2_b[:, :].unsqueeze(1).broadcast_to([T, GT, D]), ALU.add).then_inc(s_b2, 1)

                    def add_ffn(gi, j):
                        if j == 0:
                            dve.wait_ge(s_b2, lay * NG + gi + 1)
                        dve.wait_ge(s_fo, (lay * NG + gi) * GT + (j + 2))
                        dve.tensor_tensor(row(gi, j), row(gi, j), ps_out[j % 2][0:T, 0:D], ALU.add).then_inc(s_xf, 1)

                    def group_B(gi, last):
                        go, end = edge_steps(h, lay, AT_B, STEPS_B, gi)
                        n = gi + 1
                        go(11)
                        add_ffn(gi, 0)
                        if not last:
                            for j in range(3):
                                add_attention(n, j)
                        go(5)
                        add_ffn(gi, 1)
                        if last:
                            go(4)
                        else:
                            add_attention(n, 3)
                            add_attention(n, 4)
                            go(1)
                            stats_B(n, lambda: go(1))
                            for j in range(GT):
                                norm_B(n, j)
                        add_ffn(gi, 2)
                        go(2)
                        if not last:
                            add_b2(n)
                        go(2)
                        add_ffn(gi, 3)
                        end()
                        add_ffn(gi, 4)
                        dve.wait_ge(s_xf, (lay * NG + gi) * GT + (1 + GT))
                        dve.sem_inc(s_xr, 1)

                    go, end = edge_steps(h, lay, AT_B0, STEPS_B0, 0)
                    dve.wait_ge(s_bias, (lay + 1) * NG)
                    for j in range(GT):
                        add_attention(0, j)
                        if j >= 2:
                            go(1)
                    stats_B(0, lambda: go(1))
                    for j in range(GT):
                        norm_B(0, j)
                    add_b2(0)
                    go(STEPS_B0 - 6)
                    end()
                    with dve.Fori(0, NG - 1) as gi:
                        group_B(gi, False)
                    group_B(NG - 1, True)

                hold(dve, s_acc, (g + 1) * (4 * QUADS) + 3)
                with dve.If(dve.value_load(unsorted_i[0:1, 0:1], min_val=0, max_val=1) == 1):
                    for half in range(2):
                        dve.tensor_scalar(gedge, part[:, 0:1], float(half * SPLIT * T), None, ALU.add).then_inc(s_gkey, 1)
                        with dve.Fori(0, HT) as i:
                            n = (g * 2 + half) * HT + i
                            gk = Chain(dve, s_gkey, n * 5 + (g * 2 + half + 1))
                            hold(dve, s_ggat, n * 32 + 32)
                            gk.wait()
                            gk(dve.tensor_scalar(gkey, gedge, float(HALF), float(N), ALU.is_ge, ALU.mult))
                            gk.wait()
                            gk(dve.tensor_tensor(gkey, gkey, gdst, ALU.add))
                            gk(dve.tensor_scalar(gedge, gedge, float(T), None, ALU.add))
                            gk.wait()
                            gk(dve.tensor_scalar(gkey, gkey, float(-half * N), None, ALU.add))
                            m = xg[:, 0, 0:D]
                            gk(dve.tensor_tensor(m, m, rg[:, 0, :], ALU.mult))
                            hold(dve, s_gkey, gk.base + gk.n)
                            with dve.Fori(0, NT) as d:
                                q = n * NT + d
                                hold(dve, s_gadd, q + 1)
                                dve.tensor_scalar(hot[:, 0, :], iota_t[:, :], gkey, None, ALU.is_equal).then_inc(s_ghot, 1)
                                dve.wait_ge(s_ghot, q + 1)
                                dve.tensor_scalar(gkey, gkey, float(-T), None, ALU.add)
                                dve.wait_ge(s_gseg, q + 1)
                                a = acc[:, ds(d + half * NT, 1), :].rearrange("p o n -> p (o n)")
                                dve.tensor_tensor(a, a, ps_seg[0][0:T, 0:AW], ALU.add).then_inc(s_gadd, 1)
                    hold(dve, s_gadd, (g + 1) * (GTILES * NT) + 1)
                dve.wait_ge(s_gw, (g + 1) * (4 * 16))
                dve.wait_ge(s_par, 16)
                hold(dve, s_hr, (g + 1) * (NG * 16))
                dd = Chain(dve, s_dd, g * 3)
                deg = [acc[:, half * NT:(half + 1) * NT, D:AW].rearrange("p t o -> p (t o)") for half in range(2)]
                dd(dve.tensor_tensor(norm, deg[0], deg[1], ALU.add))
                dd.wait()
                dd(dve.tensor_scalar(norm, norm, 1.0, None, ALU.max))
                dd.wait()
                dd(dve.reciprocal(norm, norm))
                hold(dve, s_dd, dd.base + dd.n)

                def at_tile(b, t):
                    return b[:, ds(t, 1), :].rearrange("p o n -> p (o n)")

                def scale(t, j):
                    dve.wait_ge(s_dtr, g * NT + t + 1)
                    for half in range(2):
                        ins = dve.tensor_scalar(staged[j % SLOTS][half], at_tile(acc, t + half * NT)[:, 0:D],
                                                norm[:, ds(t, 1)], None, ALU.mult)
                    ins.then_inc(s_sc, 1)

                def update(t):
                    dve.wait_ge(s_dt, g * NT + t + 1)
                    v = at_tile(vbuf, t)
                    dve.scalar_tensor_tensor(v, v, res_b[:, 0:1], at_tile(kbuf, t), ALU.mult, ALU.add).then_inc(s_hn, 1)

                def dense_tile(t, j, first, last):
                    if not last or last + 2 < NT:
                        scale(t + 2, j + 2)
                    dve.wait_ge(s_sc, g * NT + t + 1)
                    for half in range(2):
                        dve.tensor_scalar(at_tile(acc, t + half * NT), ones[0:T, 0:1].broadcast_to([T, AW]), 0.0, None,
                                          ALU.mult)
                    dve.wait_ge(s_dy, g * NT + t + 3)
                    dve.tensor_tensor(at_tile(vbuf, t), ps_out[j % 2][0:T, 0:D], gb_b[:, :], ALU.add).then_inc(s_db, 1)
                    if not first:
                        update(t - 1)
                scale(0, 0)
                scale(1, 1)
                dense_tiles(dve, dense_tile)
                update(NT - 1)

            dve.wait_ge(s_er, 16 * NG)
            dve.wait_ge(s_ew, 16 * LAST_LOADS)
            dve.wait_ge(s_xr, NG * (L + 1))
            dve.memset(acc[EH2:EH2 + 1, 0:2, 0:2 * T], 1.0).then_inc(s_ed, 1)
            def z_rows(gi):
                return kbuf[:, ds(gi * GT, GT), :]

            def z_row(t):
                return kbuf[:, ds(t, 1), :].rearrange("p o d -> p (o d)")

            def add_rows(chain, gi, rows):
                chain(dve.tensor_tensor(z_rows(gi), z_rows(gi), rows, ALU.add))

            def over_rows(b):
                return b[:, :].unsqueeze(1).broadcast_to([T, GT, D])

            def stage_h2(gi):
                dve.wait_ge(s_etr, gi * GT + GT)
                dve.tensor_copy(q5[:, :, :], vbuf[:, ds(gi * GT, GT), :]).then_inc(s_erow, 1)

            def group_z(gi, last):
                ed = Chain(dve, s_ed, gi * (3 + 2 * GT) + 1)
                add_rows(ed, gi, xres[:, ds(gi * GT, GT), :])
                ed.wait()
                add_rows(ed, gi, over_rows(bo_b))
                ed.wait()
                for j in range(GT):
                    dve.wait_ge(s_emu, gi * GT + (j + 2))
                    z = z_row(gi * GT + j)
                    dve.tensor_tensor(z, z, ps_out[j % 2][0:T, 0:D], ALU.add).then_inc(s_emz, 1)
                if not last:
                    stage_h2(gi + 1)
                hold(dve, s_emz, gi * GT + (GT + 1))
                for j in range(GT):
                    ed(dve.bn_stats(stat[:, j, :], z_row(gi * GT + j)))
                hold(dve, ed.s, ed.base + ed.n)
                for j in range(GT):
                    ed(dve.bn_aggr(mv[:, j, :], stat[:, j, :]))
                ed.wait()
                ed(dve.tensor_copy(mv_all[:, ds(gi * GT, GT), :], mv[:, :, :]))
            stage_h2(0)
            with dve.Fori(0, NG - 1) as gi:
                group_z(gi, False)
            group_z(NG - 1, True)
            ed = Chain(dve, s_ed, NG * (3 + 2 * GT) + 1)
            ed.wait()
            inv_sqrt(dve, ed, mv_all[:, :, 1], var_all, seed_all.bitcast(I32), rstd_all, tmp_all)
            hold(dve, s_ed, ed.base + ed.n)

            with dve.Fori(0, NG) as gi:
                for j in range(GT):
                    t = gi * GT + j
                    dve.wait_ge(s_ext, t + 1)
                    dve.tensor_scalar(xh[:, j, :], z_row(t), mv_all[:, ds(t, 1), 0], rstd_all[:, ds(t, 1)],
                                      ALU.subtract, ALU.mult).then_inc(s_exh, 1)
                dve.wait_ge(s_exh, gi * GT + GT)
                dve.tensor_tensor(z_rows(gi), z_rows(gi), over_rows(b2_b), ALU.add).then_inc(s_esb, 1)
                dve.wait_ge(s_elg, gi + 1)
                dve.tensor_tensor(lg[:, ds(gi * GT, GT), :], ps_seg[1][0:T, 0:GT * NX].rearrange("p (j e) -> p j e", e=NX),
                                  gateb[:, :].unsqueeze(1).broadcast_to([T, GT, NX]), ALU.add).then_inc(s_elr, 1)

            def spread(v):
                return v.unsqueeze(2).broadcast_to([T, NT, NX])
            dve.wait_ge(s_elr, NG + 1)
            ed(dve.tensor_reduce(gone, lg, AX, ALU.max))
            ed.wait()
            dve.tensor_tensor(lg, lg, spread(gone), ALU.subtract).then_inc(s_egx, 1)
            dve.wait_ge(s_ege, 1)
            ed(dve.tensor_reduce(gone, lg, AX, ALU.add))
            ed.wait()
            ed(dve.reciprocal(gone, gone))
            ed.wait()
            ed(dve.tensor_tensor(gate, lg, spread(gone), ALU.mult))
            ed.wait()
            ed(dve.tensor_reduce(gone, gate, AX, ALU.max))
            ed.wait()
            dve.tensor_tensor(gex, gate, spread(gone), ALU.subtract).then_inc(s_egx, 1)
            g_own = gate.unsqueeze(3).broadcast_to([T, NT, NX, NX])
            g_oth = gate.unsqueeze(2).broadcast_to([T, NT, NX, NX])
            ed(dve.tensor_tensor(beat, g_oth, g_own, ALU.is_gt))
            ed(dve.tensor_tensor(beat2, g_oth, g_own, ALU.is_equal))
            ed.wait()
            ed(dve.tensor_tensor(beat2, beat2, lmask[:, :, :].unsqueeze(1).broadcast_to([T, NT, NX, NX]), ALU.mult))
            ed.wait()
            ed(dve.tensor_tensor(beat, beat, beat2, ALU.add))
            ed.wait()
            ed(dve.tensor_reduce(lg, beat, AX, ALU.add))
            ed.wait()
            ed(dve.tensor_scalar(lg, lg, 1.5, None, ALU.is_lt))
            ed.wait()
            dve.wait_ge(s_ege, 2)
            ed(dve.tensor_tensor(gate, gex, lg, ALU.mult))
            ed.wait()
            ed(dve.tensor_reduce(gone, gate, AX, ALU.add))
            ed.wait()
            ed(dve.reciprocal(gone, gone))
            ed.wait()
            ed(dve.tensor_tensor(gate, gate, spread(gone), ALU.mult))
            ed.wait()
            hold(dve, s_esb, NG)
            ED0 = ed.base + ed.n
            with dve.Fori(0, NT) as t:
                ed = Chain(dve, s_ed, t * NX + ED0)
                dve.wait_ge(s_eo, t + 2)
                z = z_row(t)
                ed(dve.tensor_tensor(z, z, ps_qk[0:T, 0:D], ALU.add))
                for e in range(NX):
                    ed.wait()
                    o = (ps_qk[0:T, D:2 * D], ps_v[0:T, 0:D], ps_v[0:T, D:2 * D], ps_seg[0][0:T, 0:D])[e]
                    ins = dve.scalar_tensor_tensor(z, o, gate[:, ds(t, 1), e], z, ALU.mult, ALU.add)
                    if e < NX - 1:
                        ed(ins)
                ins.then_inc(s_ez, 1)

        @block.scalar
        def _(act):
            start(act, s_hT, s_ev, s_qTe, s_gel, s_dT, s_eT, s_exT, s_e1a, s_e2a, s_ke, s_qTst, *s_qst)

            def copy(dst, src):
                return act.activation(dst, src, ACT.Identity)

            def dense_tanh(g, t):
                act.wait_ge(s_db, g * NT + t + 3)
                row = vbuf[:, ds(t, 1), :].rearrange("p o d -> p (o d)")
                act.activation(row, row, ACT.Tanh).then_inc(s_dt, 1)

            def norm_out(j, u, par):
                act.wait_ge(s_tr, u + (GT + j + 1))
                for c in range(KC):
                    ins = act.activation(hT[:, j, c, :], ps_turn[j % 2][:, c * T:(c + 1) * T], ACT.Identity,
                                         bias=par[:, 1, c:c + 1], scale=par[:, 0, c:c + 1])
                ins.then_inc(s_hT, 1)

            with act.Fori(0, GL) as g:
                with act.Fori(0, 2) as h:
                    lay = g * 2 + h
                    act.wait_ge(s_wqkv, (lay + 1) * (5 * 16))
                    def group_A(gi, last):
                        grp = lay * NG + gi
                        tn = grp * GT
                        u = lay * (2 * NT) + gi * GT
                        for j in range(GT):
                            if j + 1 < GT:
                                norm_out(j + 1, u, ln1p)
                            act.wait_ge(s_qst[j], grp * 16 + 16)
                            act.wait_ge(s_mm, tn + (j + 1))
                            qk, v = ps_mm[j % 2]
                            copy(q5[:, j, :], qk[0:T, 0:D])
                            copy(kbuf[:, ds(gi * GT + j, 1), :].rearrange("p o d -> p (o d)"), qk[0:T, D:2 * D])
                            copy(vbuf[:, ds(gi * GT + j, 1), :].rearrange("p o d -> p (o d)"), v[0:T, 0:D])\
                                .then_inc(s_ev, 1)
                        if not last:
                            norm_out(0, u + GT, ln1p)
                    norm_out(0, lay * (2 * NT), ln1p)
                    with act.Fori(0, NG - 1) as gi:
                        group_A(gi, False)
                    group_A(NG - 1, True)
                    for j in range(GT):
                        act.wait_ge(s_qst[j], (lay + 1) * (NG * 16) + 16)
                    def k_exp(gi):
                        grp = lay * NG + gi
                        act.wait_ge(s_ks, grp + 1)
                        act.wait_ge(s_ctx, grp + 1)
                        act.activation(q5[:, :, :], xh[:, :, :], ACT.Exp, scale=SCALE).then_inc(s_ke, 1)

                    def group_C(gi, last):
                        grp = lay * NG + gi
                        act.wait_ge(s_qs, grp + 1)
                        act.activation(qrow, qrow, ACT.Exp, scale=SCALE).then_inc(s_qe, 1)
                        if not last:
                            k_exp(gi + 1)
                        act.wait_ge(s_qTst, grp * 16 + 16)
                        for j in range(GT):
                            act.wait_ge(s_qtr, grp * GT + (j + 1))
                            copy(hT[:, j, :, :].rearrange("p c t -> p (c t)"), ps_out[j % 2][:, 0:KC * T]).then_inc(s_qTe, 1)
                    k_exp(0)
                    with act.Fori(0, NG - 1) as gi:
                        group_C(gi, False)
                    group_C(NG - 1, True)
                    act.wait_ge(s_wff, (lay + 1) * (8 * 16))
                    act.wait_ge(s_qTst, (lay + 1) * (NG * 16) + 16)
                    for j in range(GT):
                        norm_out(j, lay * (2 * NT) + NT, ln2p)

                    def gelu_group(gi):
                        tn = (lay * NG + gi) * GT
                        for j in range(GT):
                            for hf in range(2):
                                if hf == 0:
                                    act.wait_ge(s_fo, tn + (j if j else 1))
                                act.wait_ge(s_up, tn * 2 + (2 * j + hf + 1))
                                for f in range(FC // 2):
                                    ff = hf * (FC // 2) + f
                                    ins = act.activation(gT[:, j % 2, ff, :], ps_hid[hf][:, f * T:(f + 1) * T],
                                                         ACT.Gelu, bias=b1p[:, ff:ff + 1])
                                ins.then_inc(s_gel, 1)
                    with act.Fori(0, NG - 1) as gi:
                        gelu_group(gi)
                        for j in range(GT):
                            norm_out(j, lay * (2 * NT) + (gi + 1) * GT + NT, ln2p)
                    gelu_group(NG - 1)
                def dense_tile(t, j, first, last):
                    act.wait_ge(s_dtr, g * NT + t + (SLOTS + 1))
                    act.wait_ge(s_dy, g * NT + t + 1)
                    copy(gT[:, j % 2, 0:4, :].rearrange("p f t -> p (f t)"), ps_hid[0][:, 0:4 * T])
                    copy(gT[:, j % 2, 4:6, :].rearrange("p f t -> p (f t)"), ps_hid[1][:, 0:2 * T]).then_inc(s_dT, 1)
                    if not first:
                        dense_tanh(g, t - 1)
                dense_tiles(act, dense_tile)
                dense_tanh(g, NT - 1)

            act.wait_ge(s_ew, 16 * LAST_LOADS)
            act.wait_ge(s_ed, 1)

            def copy_T(dst, j):
                return copy(dst, ps_turn[j % 2][:, 0:KC * T])
            with act.Fori(0, NG) as gi:
                for j in range(GT):
                    act.wait_ge(s_etr, gi * GT + (GT + j + 1))
                    copy_T(hT[:, j, :, :].rearrange("p c t -> p (c t)"), j).then_inc(s_eT, 1)
            with act.Fori(0, NG) as gi:
                for j in range(GT):
                    act.wait_ge(s_ext, gi * GT + (GT + j + 1))
                    copy_T(hT[:, j, :, :].rearrange("p c t -> p (c t)"), j)
                    copy_T(hT_all[:, ds(gi * GT + j, 1), :].rearrange("p o n -> p (o n)"), j).then_inc(s_exT, 1)
            for m in range(2):
                act.wait_ge(s_egx, m + 1)
                gates = (lg, gex)[m]
                act.activation(gates, gates, ACT.Exp).then_inc(s_ege, 1)
            with act.Fori(0, NT) as t:
                act.wait_ge(s_e1, t + 1)
                for f in range(KC):
                    act.activation(gT[:, 0, f, :], ps_hid[0][:, f * T:(f + 1) * T], ACT.Relu, bias=sb1p[:, f:f + 1])
                for e in range(NX):
                    ins = act.activation(gT[:, 0, KC + e, :], ps_hid[1][:, e * T:(e + 1) * T], ACT.Relu, bias=eb1p[:, e:e + 1])
                ins.then_inc(s_e1a, 1)
                act.wait_ge(s_e2, t + 1)
                act.wait_ge(s_eo, t + 1)
                act.activation(gT[:, 1, 0, :], ps_tr[:, 0:T], ACT.Relu, bias=sb2p[:, 0:1])
                for e in range(NX):
                    ins = act.activation(e2T_of(e)[0:EH2], ps_ctx[0:EH2, e * T:(e + 1) * T], ACT.Relu, bias=eb2p[:, e:e + 1])
                ins.then_inc(s_e2a, 1)

        @block.tensor
        def _(pe):
            start(pe, s_seg, s_tr, s_ao, s_fo, s_dy, s_dtr, s_emu, s_ctx, s_etr, s_ext, s_eo)

            pe.wait_ge(s_const, 1)
            pe.wait_ge(s_pdve, PD_ROWS)
            pe.matmul(ps_hid[0][0:SCH, 0:4], quad_first, step_rows_f[:, 1, :, 0], start=True, stop=True).then_inc(s_ppe, 1)
            pe.wait_ge(s_pdve, PD_FALLS)
            pe.matmul(ps_hid[1][:, 0:1], ones[0:PAIR_ROWS, :], nfall, start=True, stop=False)
            pe.matmul(ps_hid[1][:, 0:1], ones[0:SCH, :], nspread, start=False, stop=True).then_inc(s_ppe, 1)
            for m, (bank_m, rows) in enumerate(((ps_tr, tile_of), (ps_qk, place))):
                for ch in range(4):
                    ins = pe.transpose(bank_m[0:1, ch * SCH:(ch + 1) * SCH], rows[:, ch:ch + 1], ident[0:SCH, 0:SCH])
                ins.then_inc(s_ppe, 1)
            pe.wait_ge(s_pdve, PD_KEYS)
            for m in range(3):
                for ch in range(4):
                    ins = pe.transpose(ps_tab[m][0:T, ch * SCH:(ch + 1) * SCH], step_rows_f[:, m, ch, :], ident[0:SCH, 0:SCH])
                ins.then_inc(s_ppe, 1)
            pe.matmul(ps_v[0:T, 0:2 * QUADS], ones[0:1, 0:T], place_row, start=True, stop=True).then_inc(s_ppe, 1)

            def edge_steps(lay, at, per, gi):
                s0 = lay * STEPS + gi * per + at
                quad0 = lay * QUADS + gi * (per // QUAD) + at // QUAD
                done = [0]

                def go(n):
                    for _ in range(n):
                        k = done[0]
                        done[0] += 1
                        q = k // QUAD
                        if k % QUAD == 0:
                            pe.wait_ge(s_acc, (quad0 + q) * 2 + 1)
                        pe.wait_ge(s_msg, s0 + (k + 2 + RING))
                        pe.matmul(ps_seg[q % 2][0:T, 0:AW], hot[:, k % QUAD, :], xg[:, k % RING, :],
                                  start=k % QUAD == 0, stop=k % QUAD == QUAD - 1).then_inc(s_seg, 1)
                return go

            def turn(j, u):
                pe.wait_ge(s_hT, u + (j if j else 1))
                pe.wait_ge(s_xh, u + (j + 1))
                transpose_rows(pe, ps_turn[j % 2], xh[:, j, :]).then_inc(s_tr, 1)

            with pe.Fori(0, GL) as g:
                with pe.Fori(0, 2) as h:
                    lay = g * 2 + h
                    pe.wait_ge(s_wqkv, (lay + 1) * (5 * 16))
                    def group_A(gi, last):
                        tn = (lay * NG + gi) * GT
                        u = lay * (2 * NT) + gi * GT
                        go = edge_steps(lay, 0, STEPS_A, gi)
                        for j in range(GT):
                            if j + 1 < GT:
                                turn(j + 1, u)
                            pe.wait_ge(s_hT, u + (j + 2))
                            pe.wait_ge(s_ev, tn + (j if j else 1))
                            qk, v = ps_mm[j % 2]
                            for c in range(KC):
                                pe.matmul(qk[0:T, :], hT[:, j, c, :], wqkv[:, c, 0:2 * D], start=c == 0, stop=c == KC - 1)
                            for c in range(KC):
                                ins = pe.matmul(v[0:T, 0:D], hT[:, j, c, :], wqkv[:, c, 2 * D:], start=c == 0,
                                                stop=c == KC - 1)
                            ins.then_inc(s_mm, 1)
                            go(1)
                        if not last:
                            turn(0, u + GT)
                        go(STEPS_A - GT)
                    turn(0, lay * (2 * NT))
                    with pe.Fori(0, NG - 1) as gi:
                        group_A(gi, False)
                    group_A(NG - 1, True)
                    go = edge_steps(lay, AT_C0, STEPS_C0, 0)
                    pe.wait_ge(s_km, lay * KM_STEPS + NT + 1)
                    transpose_rows(pe, ps_ctx, kmax[:, :]).then_inc(s_kmT, 1)
                    go(3)
                    pe.wait_ge(s_kdg, lay + 1)
                    for c in range(KC):
                        ins = pe.matmul(ps_ctx[0:T, c * P:(c + 1) * P], ones[:, 0:T], kdiag[:, c, :], start=True, stop=True)
                    ins.then_inc(s_kmB, 1)
                    go(STEPS_C0 - 3)
                    pe.wait_ge(s_km, lay * KM_STEPS + NT + 3)
                    pe.matmul(ps_ctx[:, 0:D + KC], ones[0:1, :], zrow[:, :], start=True, stop=False, skip_group_check=True)
                    with pe.Fori(0, NG) as gi:
                        tn = (lay * NG + gi) * GT
                        go = edge_steps(lay, AT_C, STEPS_C, gi)
                        go(2)
                        pe.wait_ge(s_ke, lay * NG + gi + 2)
                        for j in range(GT):
                            for c in range(KC):
                                vj = vbuf[:, ds(gi * GT + j, 1), c * P:(c + 1) * P].rearrange("p o d -> p (o d)")
                                pe.matmul(ps_ctx[:, c * P:(c + 1) * P], q5[:, j, c * P:(c + 1) * P], vj,
                                          start=False, stop=True, skip_group_check=True)
                                ins = pe.matmul(ps_ctx[:, D + c:D + c + 1], q5[:, j, c * P:(c + 1) * P], ones[0:T, 0:1],
                                                start=False, stop=True, skip_group_check=True)
                            if j == GT - 1:
                                ins.then_inc(s_ctx, 1)
                            go(1)
                        pe.wait_ge(s_qn, lay * NG + gi + 1)
                        for j in range(GT):
                            pe.wait_ge(s_qTe, tn + (j if j else 1))
                            transpose_rows(pe, ps_out[j % 2], qrow[:, j, :]).then_inc(s_qtr, 1)
                        go(STEPS_C - 7)
                    pe.wait_ge(s_wff, (lay + 1) * (8 * 16))
                    pe.wait_ge(s_cm, lay + 1)
                    for c in range(KC):
                        ins = pe.transpose(ps_tr[:, c * P:(c + 1) * P], ctxm[:, c, :], ident[:, :])
                    ins.then_inc(s_ctT, 1)
                    pe.wait_ge(s_cmT, lay + 1)
                    for c in range(KC):
                        ins = pe.matmul(ps_ctx[:, c * D:(c + 1) * D], ctxT[:, c, :], wo[:, c, :], start=True, stop=True)
                    ins.then_inc(s_cw, 1)
                    pe.wait_ge(s_cwr, lay + 1)

                    def attend(gi, j):
                        grp = lay * NG + gi
                        pe.wait_ge(s_qld, grp * 16 + 16)
                        pe.wait_ge(s_xa, grp * GT + (j if j else 1))
                        for c in range(KC):
                            ins = pe.matmul(ps_ao[j % 2][0:T, 0:D], qT[:, j, c, :], cwo[:, c, :], start=c == 0, stop=c == KC - 1)
                        ins.then_inc(s_ao, 1)

                    def turn_B(gi, j):
                        turn(j, lay * (2 * NT) + gi * GT + NT)

                    def group_B(gi, last):
                        tn = (lay * NG + gi) * GT
                        u = lay * (2 * NT) + gi * GT + NT
                        go = edge_steps(lay, AT_B, STEPS_B, gi)

                        def up(j):
                            for hf in range(2):
                                if hf == 0:
                                    pe.wait_ge(s_hT, u + (j + 2))
                                pe.wait_ge(s_gel, tn * 2 + (2 * j + hf + 1))
                                for f in range(FC // 2):
                                    ff = hf * (FC // 2) + f
                                    for c in range(KC):
                                        ins = pe.matmul(ps_hid[hf][:, f * T:(f + 1) * T], w1[:, c, ff * P:(ff + 1) * P],
                                                        hT[:, j, c, :], start=c == 0, stop=c == KC - 1)
                                ins.then_inc(s_up, 1)
                                go(2)

                        def down(j):
                            pe.wait_ge(s_xf, tn + (j if j else 1))
                            pe.wait_ge(s_gel, tn * 2 + (2 * j + 4))
                            for f in range(FC):
                                ins = pe.matmul(ps_out[j % 2][0:T, 0:D], gT[:, j % 2, f, :], w2[:, f, :],
                                                start=f == 0, stop=f == FC - 1)
                            ins.then_inc(s_fo, 1)
                        n = gi + 1
                        up(0)
                        for j in range(GT):
                            if j + 1 < GT:
                                up(j + 1)
                            if not last and j == 3:
                                turn_B(n, 0)
                                turn_B(n, 1)
                            if not last and j == 4:
                                turn_B(n, 2)
                                turn_B(n, 3)
                            down(j)
                            if not last and j == 0:
                                pe.wait_ge(s_hT, u + (GT + 1))
                                for a in range(3):
                                    attend(n, a)
                            if not last and j == 1:
                                attend(n, 3)
                                attend(n, 4)
                            if j < GT - 1:
                                go(1)
                        if not last:
                            turn_B(n, 4)
                        go(STEPS_B - 24)

                    go = edge_steps(lay, AT_B0, STEPS_B0, 0)
                    for j in range(GT):
                        attend(0, j)
                        if j >= 3:
                            go(1)
                    go(4)
                    for j in range(GT):
                        turn_B(0, j)
                    go(STEPS_B0 - 6)
                    with pe.Fori(0, NG - 1) as gi:
                        group_B(gi, False)
                    group_B(NG - 1, True)
                hold(pe, s_acc, (g + 1) * (4 * QUADS) + 3)
                with pe.If(pe.value_load(unsorted_i[0:1, 0:1], min_val=0, max_val=1) == 1):
                    with pe.Fori(0, GTILES * NT) as q:
                        pe.wait_ge(s_ghot, g * (GTILES * NT) + q + 1)
                        pe.matmul(ps_seg[0][0:T, 0:AW], hot[:, 0, :], xg[:, 0, :], start=True, stop=True).then_inc(s_gseg, 1)
                pe.wait_ge(s_gw, (g + 1) * (4 * 16))

                def turn_sums(t, j):
                    k = j % SLOTS
                    uses = len(range(k, NT, SLOTS))
                    pe.wait_ge(s_dT, g * NT + t + 1)
                    pe.wait_ge(s_sc, g * NT + t + 1)
                    pe.wait_ge(s_hx[k], g * (uses * 16) + (t - k) * (16 // SLOTS) + 16)
                    for m in range(2):
                        transpose_rows(pe, ps_hid[0][:, m * KC * T:(m + 1) * KC * T], staged[k][m])
                    transpose_rows(pe, ps_hid[1], staged[k][2]).then_inc(s_dtr, 1)

                def dense_tile(t, j, first, last):
                    pe.wait_ge(s_dT, g * NT + t + 2)
                    if not last or last + 1 < NT:
                        turn_sums(t + 1, j + 1)
                    pe.wait_ge(s_db, g * NT + t + 1)
                    for m in range(3):
                        for c in range(KC):
                            ins = pe.matmul(ps_out[j % 2][0:T, 0:D], gT[:, j % 2, m * KC + c, :], wg[:, m, c, :],
                                            start=m == 0 and c == 0, stop=m == 2 and c == KC - 1)
                    ins.then_inc(s_dy, 1)
                turn_sums(0, 0)
                dense_tiles(pe, dense_tile)

            pe.wait_ge(s_ew, 16 * LAST_LOADS)
            pe.wait_ge(s_hn, GL * NT)
            with pe.Fori(0, NG) as gi:
                dn = gi * GT

                def turn_h2(j):
                    pe.wait_ge(s_eT, dn + (j if j else 1))
                    pe.wait_ge(s_erow, gi + 1)
                    transpose_rows(pe, ps_turn[j % 2], q5[:, j, :]).then_inc(s_etr, 1)
                turn_h2(0)
                for j in range(GT):
                    if j + 1 < GT:
                        turn_h2(j + 1)
                    pe.wait_ge(s_eT, dn + (j + 2))
                    pe.wait_ge(s_emz, dn + (j if j else 1))
                    for c in range(KC):
                        ins = pe.matmul(ps_out[j % 2][0:T, 0:D], hT[:, j, c, :], mu_w[:, c, :], start=c == 0, stop=c == KC - 1)
                    ins.then_inc(s_emu, 1)
            pe.wait_ge(s_eT, NT + 1)
            with pe.Fori(0, NG) as gi:
                dn = gi * GT

                def turn_z(j):
                    pe.wait_ge(s_exT, dn + (j if j else 1))
                    pe.wait_ge(s_exh, dn + (j + 1))
                    transpose_rows(pe, ps_turn[j % 2], xh[:, j, :]).then_inc(s_ext, 1)
                turn_z(0)
                for j in range(GT):
                    if j + 1 < GT:
                        turn_z(j + 1)
                    if j == 0:
                        pe.wait_ge(s_elr, gi + 1)
                    pe.wait_ge(s_exT, dn + (j + 2))
                    for c in range(KC):
                        ins = pe.matmul(ps_seg[1][0:T, j * NX:(j + 1) * NX], hT[:, j, c, :], gW[:, c, :], start=c == 0,
                                        stop=c == KC - 1)
                ins.then_inc(s_elg, 1)

            def layer_1(t):
                x = hT_all[:, ds(t, 1), :].rearrange("p o (c t) -> p (o c) t", c=KC)
                pe.wait_ge(s_e1a, t + 1)
                for f in range(KC):
                    for c in range(KC):
                        pe.matmul(ps_hid[0][:, f * T:(f + 1) * T], sW1[:, c, f * P:(f + 1) * P], x[:, c, :],
                                  start=c == 0, stop=c == KC - 1)
                for e in range(NX):
                    for c in range(KC):
                        ins = pe.matmul(ps_hid[1][:, e * T:(e + 1) * T], eW1[:, e, c, :], x[:, c, :],
                                        start=c == 0, stop=c == KC - 1)
                ins.then_inc(s_e1, 1)

            def layer_2(t):
                pe.wait_ge(s_e2a, t + 1)
                pe.wait_ge(s_e1a, t + 2)
                for c in range(KC):
                    pe.matmul(ps_tr[:, 0:T], sW2[:, c, :], gT[:, 0, c, :], start=c == 0, stop=c == KC - 1)
                for e in range(NX):
                    ins = pe.matmul(ps_ctx[0:EH2, e * T:(e + 1) * T], eW2[:, e, :], gT[:, 0, KC + e, :], start=True, stop=True)
                ins.then_inc(s_e2, 1)

            def layer_3(t):
                pe.wait_ge(s_e2a, t + 2)
                pe.wait_ge(s_ez, t + 1)
                pe.matmul(ps_qk[0:T, 0:D], gT[:, 1, 0, :], sW3, start=True, stop=True)
                for e in range(NX):
                    o = (ps_qk[0:T, D:2 * D], ps_v[0:T, 0:D], ps_v[0:T, D:2 * D], ps_seg[0][0:T, 0:D])[e]
                    ins = pe.matmul(o, e2T_of(e), eW3[0:EH2 + 1, e, :], start=True, stop=True)
                ins.then_inc(s_eo, 1)
            layer_1(0)
            layer_2(0)
            with pe.Fori(0, NT - 1) as t:
                layer_1(t + 1)
                layer_3(t)
                layer_2(t + 1)
            layer_3(NT - 1)

        assert not START, "free buffers not handed out"


def kernel(**inputs):
    import concourse.bacc as bacc
    from concourse.bass_utils import run_bass_kernel_spmd

    nc = bacc.Bacc("TRN2", target_bir_lowering=False, num_devices=1)
    arrays, io = {}, {}
    for name, value in inputs.items():
        a = np.ascontiguousarray(value)
        arrays[name] = a
        io[name] = nc.dram_tensor(name, a.shape, mybir.dt.from_np(a.dtype), kind="ExternalInput").ap()
    out = nc.dram_tensor("out", inputs["x"].shape, F32, kind="ExternalOutput").ap()
    build(nc, io, out)
    return run_bass_kernel_spmd(nc, [arrays], core_ids=[0]).results[0]["out"]
```

```python
from contextlib import ExitStack

import numpy as np

import concourse.bass as bass
from concourse import mybir

F32 = mybir.dt.float32
I32 = mybir.dt.int32
ALU = mybir.AluOpType
ACT = mybir.ActivationFunctionType
AX = mybir.AxisListType.X
ds = bass.ds

P = 128
D = 256
KC = D // P
T = 125
EP = P
GT = 5
HEADS, DH = 8, 32
EPS = 1e-5
RSQRT_SEED = float(0x5F3759DF)
FAR = 65536.0
RING = 8
SLOTS = 4
QUAD = 4
STEPS_A, STEPS_C, STEPS_B0, STEPS_B = 8, 8, 8, 24
LEAD = 2


def build(nc, io, out):
    N = io["x"].shape[0]
    E = io["src"].shape[0]
    L, _, FF = io["L0_mix_W1"].shape
    FC = FF // P
    NT = N // T
    NG = NT // GT
    HALF = E // 2
    GHT = -(-HALF // T)
    SPLIT = HALF // T
    assert E // T - SPLIT == GHT and T * NT == N and E % T == 0
    AT_C = NG * STEPS_A
    AT_B0 = AT_C + NG * STEPS_C
    AT_B = AT_B0 + STEPS_B0
    STEPS = AT_B + NG * STEPS_B
    assert all(n % RING == 0 for n in (STEPS_A, STEPS_C, STEPS_B0, STEPS_B)) and RING % QUAD == 0
    QUADS = STEPS // QUAD
    SCH = STEPS // 2
    assert SCH % QUAD == 0
    CHUNKS = ((0, HALF), (SCH * EP, HALF), (HALF, E), (HALF + SCH * EP, E))
    assert all(SCH * EP <= end - at for at, end in CHUNKS[::2])
    assert all((SCH - QUAD) * EP < end - at < SCH * EP for at, end in CHUNKS[1::2])
    NX = io["L0_ffn_eW1"].shape[0]
    EH2 = io["L0_ffn_eW2"].shape[2]
    GL = 2
    SCALE = float(DH) ** -0.25
    AW = D + 1
    assert L == 2 * GL
    PD_ROWS, PD_FALLS, PD_KEYS = 6, 21, 42
    PAIR_ROWS = max(r for r in range(1, P + 1) if (E - 1) % r == 0)
    PAIRS = (E - 1) // PAIR_ROWS
    GTILES = 2 * GHT
    KM_STEPS = NT + 5
    LAST_LOADS = 15 + NX

    xn_d = nc.dram_tensor("xn_rows", [N, D], F32, kind="Internal").ap()
    h1_d = nc.dram_tensor("h1_rows", [N, D], F32, kind="Internal").ap()
    hT_d = nc.dram_tensor("normed_columns", [NG, P, GT * KC * T], F32, kind="Internal").ap()
    qT_d = nc.dram_tensor("q_columns", [NG, P, GT * KC * T], F32, kind="Internal").ap()

    def group_rows(t, gi):
        return t[ds(gi * (GT * T), GT * T), :].rearrange("(j p) d -> p j d", p=T)

    with ExitStack() as ctx:
        def sb(name, shape, dt=F32):
            return ctx.enter_context(nc.sbuf_tensor(name, shape, dt))

        def sem(name):
            return ctx.enter_context(nc.semaphore(name))

        def bank(name):
            return ctx.enter_context(nc.psum_tensor(name, [P, 512], F32))
        ps_seg = [bank("ps_seg0"), bank("ps_seg1")]
        ps_tr = bank("ps_tr")
        ps_kv0, ps_kv1 = bank("ps_kv0"), bank("ps_kv1")
        ps_ctx = bank("ps_ctx")
        ps_turn = [ps_tr, ps_ctx]
        ps_ao = [ps_ctx, ps_tr]
        ps_out = [ps_kv0, ps_kv1]
        ps_hid = [bank("ps_hid0"), bank("ps_hid1")]
        ps_kv = [ps_kv0, ps_kv1]
        ps_q = [ps_hid[0], ps_hid[1], ps_tr]

        xres = sb("xres", [T, NT, D])
        kbuf = sb("kbuf", [T, NT, D])
        flat_v = sb("vbuf", [T, NT * (D + KC)])
        v_ones = flat_v[:, :].rearrange("p (t c n) -> p t c n", c=KC, n=P + 1)
        vbuf = flat_v[:, 0:NT * D].rearrange("p (t d) -> p t d", d=D)
        accp = sb("acc", [P, 2 * NT, AW])
        acc = accp[0:T]
        wqkv = sb("wqkv", [P, KC, 3 * D])
        wo = sb("wo", [P, KC, D])
        wff = sb("wff", [P, 2 * KC * FF])
        w1 = wff[:, 0:KC * FF].rearrange("p (c f) -> p c f", c=KC)
        w2 = wff[:, KC * FF:].rearrange("p (f d) -> p f d", f=FC)
        hq = wff[:, KC * FF:KC * FF + GT * KC * T].rearrange("p (j c t) -> p j c t", j=GT, c=KC)
        wg = wqkv[:, :, :].rearrange("p c n -> p (c n)").rearrange("p (m c n) -> p m c n", m=3, c=KC)
        ln1p = sb("ln1p", [P, 2, KC])
        ln2p = sb("ln2p", [P, 2, KC])
        b1p = sb("b1p", [P, FC])
        bo_b = sb("bo_b", [T, D])
        b2_b = sb("b2_b", [T, D])
        res_b = sb("res_b", [T, 1])

        idx_tab = sb("idx_tab", [EP, 2 * STEPS, 2], I32)
        key_tab = sb("key_tab", [EP, 2 * STEPS])
        in_tile = sb("in_tile", [T, 2 * QUADS, 2])
        row_tab = sb("row_tab", [1, 2 * QUADS, 2], I32)
        idx_now = sb("idx_now", [EP, 2, RING, 2], I32)
        xg = sb("xg", [EP, RING, AW])
        rg = sb("rg", [EP, RING, D])
        zrow = sb("zrow", [1, D + KC])
        hot = sb("hot", [EP, QUAD, T])
        iota_t = sb("iota_t", [EP, T])
        ident = sb("ident", [P, P])
        ones = sb("ones", [P, P])
        head_mask = sb("head_mask", [P, P])

        xh = sb("xh", [T, GT, D])
        hT = sb("hT", [P, GT, KC, T])
        q5p = sb("q5", [P, GT * D])
        q5 = q5p[0:T, :].rearrange("p (j d) -> p j d", j=GT)
        qT = q5p[:, 0:GT * KC * T].rearrange("p (j c t) -> p j c t", j=GT, c=KC)
        gT = sb("gT", [P, 2, FC, T])
        kmax = sb("kmax", [T, D])
        flat_g = gT[:, :, :, :].rearrange("p s f t -> p (s f t)")
        qrow = flat_g[0:T, 0:GT * D].rearrange("p (j d) -> p j d", j=GT)
        kmaxT = sb("kmaxT", [P, KC])
        ksh = sb("ksh", [T, D])
        gb_b = ksh
        ctxm, ctxT = (flat_g[:, a:a + D].rearrange("p (c d) -> p c d", c=KC)
                      for a in (GT * D, GT * D + D))
        kdiag = ctxm
        rsum = sb("rsum", [P, KC])
        cwo = sb("cwo", [P, KC, D])
        qm = sb("qm", [T, GT * HEADS])
        stat = sb("stat", [T, GT, 6])
        mv = sb("mv", [T, GT, 2])
        var = sb("var", [T, GT])
        seed = sb("seed", [T, GT], I32)
        rstd = sb("rstd", [T, GT])
        tmp = sb("tmp", [T, GT])
        norm = qm[:, 0:NT]
        staged = [(q5[:, k, :], hT[0:T].rearrange("p j c t -> p (j c t)")[:, k * D:(k + 1) * D], xh[:, k, :])
                  for k in range(SLOTS)]

        at_norm = [P]

        def norm_buf(*shape):
            n = int(np.prod(shape))
            v = flat_g[0:T, at_norm[0]:at_norm[0] + n]
            at_norm[0] += n
            return v if len(shape) == 1 else v.rearrange("p (t n) -> p t n", n=shape[1])
        stat_all, mv_all = norm_buf(NT, 6), norm_buf(NT, 2)
        var_all, rstd_all, tmp_all, shift_all = (norm_buf(NT) for _ in range(4))
        seed_all = norm_buf(NT).bitcast(I32)
        step_rows = vbuf[0:SCH, 0:6, :].rearrange("p a d -> p (a d)")[:, 0:12 * EP].bitcast(I32)\
            .rearrange("p (m c t) -> p m c t", m=3, c=4)
        step_rows_f = kbuf[0:SCH, 0:6, :].rearrange("p a d -> p (a d)")[:, 0:12 * EP]\
            .rearrange("p (m c t) -> p m c t", m=3, c=4)
        ps_tab = [ps_seg[0], ps_seg[1], ps_tr, ps_kv0]

        def early(i, rows, n):
            return kbuf[0:rows, 8 + 2 * i:10 + 2 * i, :].rearrange("p a d -> p (a d)")[:, 0:n]
        iota_i = flat_g[0:EP, 0:T].bitcast(I32)
        part_i = early(1, T, 1).bitcast(I32)
        ramp_i, ramp = early(1, SCH, NT)[:, 1:NT].bitcast(I32), early(2, SCH, NT)[:, 1:NT]
        enum_i = early(3, SCH, 4 * EP).bitcast(I32).rearrange("p (c t) -> p c t", c=4)
        enum = early(4, SCH, 4 * EP).rearrange("p (c t) -> p c t", c=4)
        dropped = early(5, SCH, EP)
        spans = early(6, SCH, 4 * EP).rearrange("p (c t) -> p c t", c=4)
        first, tile_of, base, place, bad = (early(7, SCH, 4 * (i + 1))[:, 4 * i:] for i in range(5))
        reached = early(7, SCH, 64 + NT)[:, 64:64 + NT - 1]
        nspread = early(7, SCH, 120)[:, 119:120]
        place_row = vbuf[0:1, 16:18, :].rearrange("p a d -> p (a d)")[:, 0:2 * QUADS]
        tile_row = vbuf[0:1, 18:20, :].rearrange("p a d -> p (a d)")[:, 0:2 * QUADS]
        quad_first = vbuf[0:SCH, 20, 0:SCH]
        pair_a, pair_b = (vbuf[0:PAIR_ROWS, a:a + 2, :].rearrange("p a d -> p (a d)")[:, 0:PAIRS].bitcast(I32)
                          for a in (8, 10))
        falls = vbuf[0:PAIR_ROWS, 12:14, :].rearrange("p a d -> p (a d)")[:, 0:PAIRS]
        nfall = vbuf[0:PAIR_ROWS, 14, 0:1]
        unsorted_f = sb("unsorted_f", [EP, 1])
        unsorted_i = sb("unsorted_i", [1, 1], I32)
        part = sb("part", [T, 1])
        gsrc, gtype, gdst = idx_now[0:T, 0, 0, 0:1], idx_now[0:T, 0, 0, 1:2], idx_now[0:T, 0, 1, 0:1]
        gedge, gkey = tmp[:, 0:1], tmp[:, 1:2]
        lmask = sb("lmask", [T, NX, NX])
        flat_acc = accp[:, :, :].rearrange("p a n -> p (a n)")
        last_at = [2 * AW]

        def last_buf(*shape, parts=T):
            n = int(np.prod(shape))
            v = flat_acc[0:parts, last_at[0]:last_at[0] + n]
            last_at[0] += n
            names = " ".join("abc"[:len(shape)])
            return v.rearrange(f"p ({names}) -> p {names}", **dict(zip("abc", shape))) if len(shape) > 1 else v
        hT_all = last_buf(NT, KC * T, parts=P)
        gone = last_buf(NT)
        lg, gate, gex = (last_buf(NT, NX) for _ in range(3))
        beat, beat2 = (last_buf(NT, NX, NX) for _ in range(2))
        assert last_at[0] <= 2 * NT * AW
        sb1p, sb2p, eb1p = b1p[:, 0:KC], b1p[:, KC:KC + 1], b1p[:, KC + 1:KC + 1 + NX]
        eb2p = ln2p[0:EH2].rearrange("p m c -> p (m c)")
        gateb = sb("gateb", [T, NX])

        START = {}

        def counted(name, start=0):
            s = sem(name)
            START[id(s)] = start
            return s

        s_x = [sem(f"x_loaded{gi}") for gi in range(NG)]
        s_par = sem("params_loaded")
        s_const = sem("constants_made")
        s_clr = sem("table_rows_cleared")
        s_pair = sem("neighbours_loaded")
        s_tabl = sem("table_rows_loaded")
        s_pdve = sem("prologue_dve")
        s_ppe = sem("prologue_pe")
        s_ppool = sem("prologue_pool")
        s_tab = sem("tables_ready")
        s_xn_st = sem("xn_stored")
        s_h1_st = sem("h1_stored")
        s_out = sem("out_stored")
        s_edge = [sem(f"edge_gathered{i}") for i in range(RING)]
        s_idx = sem("idx_staged")
        s_claim = sem("slot_claimed")
        s_msg = counted("message_ready", RING + 1)
        s_seg = counted("segment_done", RING)
        s_acc = counted("acc_added", 3)
        s_zero = sem("acc_zeroed")
        s_gidx = sem("general_indices_loaded")
        s_ggat = sem("general_rows_gathered")
        s_gkey = sem("general_dve")
        s_ghot = sem("general_onehot_ready")
        s_gseg = sem("general_segment_done")
        s_gadd = counted("general_added", 1)
        s_xr = sem("x_ready")
        s_ln = sem("norm_dve")
        s_xh = sem("xh_ready")
        s_tr = counted("xh_transposed", GT)
        s_hT = counted("hT_ready", 1)
        s_mm = sem("kv_done")
        s_wqkv = sem("wqkv_loaded")
        s_wff = sem("wff_loaded")
        s_ev = counted("kv_copied", 1)
        s_hst = [counted(f"normed_rows_stored{j}", 16) for j in range(GT)]
        s_hql = sem("normed_rows_loaded")
        s_w2 = sem("w2_loaded")
        s_qp = sem("q_done")
        s_qc = sem("q_copied")
        s_qtr = sem("q_transposed")
        s_qTe = counted("qT_copied", 1)
        s_qTst = counted("qT_stored", 16)
        s_qld = sem("q_loaded")
        s_qs = sem("q_shifted")
        s_qe = sem("q_exp")
        s_qn = sem("q_normed")
        s_qd = sem("q_dve")
        s_km = sem("kmax_dve")
        s_kmT = sem("kmax_transposed")
        s_kdg = sem("kmax_diagonal")
        s_kmB = sem("kmax_spread")
        s_ks = sem("k_shifted")
        s_ke = counted("k_exp", 1)
        s_ctx = counted("context_done", 1)
        s_ctT = sem("context_transposed")
        s_cmT = sem("context_turned")
        s_cm = sem("context_masked")
        s_cw = sem("context_wo_done")
        s_cwr = sem("context_wo_ready")
        s_ao = counted("attention_done", GT)
        s_b2 = sem("ffn_bias_added")
        s_xa = counted("x_attention_added", 1)
        s_up = sem("hidden_done")
        s_gel = counted("gelu_done", 2)
        s_fo = counted("ffn_done", 1)
        s_xf = counted("x_ffn_added", 1)
        s_gw = sem("graph_weights_loaded")
        s_dd = sem("dense_dve")
        s_hx = [sem(f"h_tile_loaded{k}") for k in range(SLOTS)]
        s_sc = sem("sums_scaled")
        s_dtr = counted("dense_transposed", SLOTS)
        s_dT = counted("dense_T_ready", 1)
        s_dy = counted("dense_product_done", 2)
        s_db = counted("dense_biased", 2)
        s_dt = sem("dense_tanh")
        s_hn = sem("h_new_ready")
        s_ew = sem("last_weights_loaded")
        s_er = sem("last_rows_loaded")
        s_zp = sem("x_and_transformer_added")
        s_ed = sem("last_dve")
        s_erow = sem("h2_rows_staged")
        s_etr = counted("h2_transposed", GT)
        s_eT = counted("h2T_ready", 1)
        s_emu = counted("mu_done", 1)
        s_emz = counted("mu_added", 1)
        s_exh = sem("last_xh_ready")
        s_ext = counted("last_xh_transposed", GT)
        s_exT = counted("last_xhT_ready", 1)
        s_elg = sem("gate_logits_done")
        s_elr = counted("gate_logits_read", 1)
        s_esb = sem("shared_bias_added")
        s_egx = sem("gates_shifted")
        s_ege = sem("gates_exp")
        s_e1 = sem("last_hidden1_done")
        s_e1a = counted("last_hidden1_ready", 1)
        s_e2 = sem("last_hidden2_done")
        s_e2a = counted("last_hidden2_ready", 1)
        s_eo = counted("experts_done", 1)
        s_ez = counted("row_combined", 1)

        block = ctx.enter_context(nc.Block())

        class Chain:

            def __init__(self, eng, s, base=0):
                self.eng, self.s, self.base, self.n = eng, s, base, 0

            def __call__(self, ins):
                ins.then_inc(self.s, 1)
                self.n += 1

            def wait(self):
                self.eng.wait_ge(self.s, self.base + self.n)

        def hold(eng, s, value):
            eng.wait_ge(s, value)
            eng.sem_inc(s_claim, 1)

        def inv_sqrt(dve, chain, variance, v, bits, y, t, between=lambda: None):
            chain(dve.tensor_scalar(v, variance, EPS, None, ALU.add))
            chain.wait()
            chain(dve.tensor_scalar(bits, v.bitcast(I32), 1, None, ALU.arith_shift_right))
            chain.wait()
            chain(dve.tensor_scalar(y.bitcast(I32), bits, -1.0, RSQRT_SEED, ALU.mult, ALU.add))
            for newton in range(3):
                if newton == 1:
                    between()
                chain.wait()
                chain(dve.scalar_tensor_tensor(t, y, -0.5, v, ALU.mult, ALU.mult))
                chain.wait()
                chain(dve.tensor_tensor(t, t, y, ALU.mult))
                chain.wait()
                chain(dve.scalar_tensor_tensor(y, t, 1.5, y, ALU.add, ALU.mult))

        def norm_stats(dve, chain, rows, between=lambda: None):
            for j in range(GT):
                chain(dve.bn_stats(stat[:, j, :], rows(j)))
            between()
            hold(dve, chain.s, chain.base + chain.n)
            for j in range(GT):
                chain(dve.bn_aggr(mv[:, j, :], stat[:, j, :]))
            between()
            chain.wait()
            inv_sqrt(dve, chain, mv[:, :, 1], var[:, :], seed[:, :], rstd[:, :], tmp[:, :], between)
            chain.wait()
        INV_STEPS = 3 + 9
        NORM_STEPS = 2 * GT + INV_STEPS
        LN0 = 2 * NT + INV_STEPS + 1

        def norm_rows(dve, j, rows):
            return dve.tensor_scalar(xh[:, j, :], rows, mv[:, j, 0:1], rstd[:, j:j + 1], ALU.subtract, ALU.mult)

        def transpose_rows(pe, dst, rows):
            for c in range(KC):
                ins = pe.transpose(dst[:, c * T:(c + 1) * T], rows[:, c * P:(c + 1) * P], ident[0:T, 0:T])
            return ins

        def columns(v):
            return v.rearrange("(c p) -> p c", p=P)

        def rows_of(w):
            return w.rearrange("(c p) n -> p c n", p=P)

        def flat_qT(t):
            return t[:, :, :, :].rearrange("p j c t -> p (j c t)")

        def start(eng, *sems):
            for s in sems:
                eng.sem_inc(s, START.pop(id(s)))

        def dense_tiles(eng, tile):
            tile(0, 0, True, False)
            with eng.Fori(0, (NT - 2) // SLOTS) as it:
                for j in range(1, SLOTS + 1):
                    tile(it * SLOTS + j, j, False, False)
            for t in range((NT - 2) // SLOTS * SLOTS + 1, NT):
                tile(t, t, False, t)

        offs, at = {}, 0
        for name, cols in (("mu", KC * D), ("sW1", KC * D), ("sW2", KC * P), ("sW3", D), ("eW1", NX * KC * P),
                           ("eW2", NX * EH2), ("eW3", NX * D), ("gW", KC * NX)):
            offs[name] = (at, at + cols)
            at += cols
        assert at <= 2 * KC * FF

        def last_w(name, c):
            a, b = offs[name]
            return wff[:, a:b].rearrange("p (c n) -> p c n", c=c)

        mu_w, sW1, sW2, gW = (last_w(n, KC) for n in ("mu", "sW1", "sW2", "gW"))
        sW3 = last_w("sW3", 1)[:, 0, :]
        eW1 = last_w("eW1", NX).rearrange("p e (c n) -> p e c n", c=KC)
        eW2, eW3 = last_w("eW2", NX), last_w("eW3", NX)
        e2T = acc[0:EH2 + 1, 0:2, 0:2 * T].rearrange("p a (b t) -> p a b t", t=T)

        def z_rows(gi):
            return kbuf[:, ds(gi * GT, GT), :]

        def over_rows(b):
            return b[:, :].unsqueeze(1).broadcast_to([T, GT, D])

        def e2T_of(e):
            return e2T[:, e // 2, e % 2, :]

        @block.sync
        def _(sp):
            for gi in range(NG):
                sp.dma_start(xres[:, gi * GT:(gi + 1) * GT, :], group_rows(io["x"], gi)).then_inc(s_x[gi], 16)
            sp.wait_ge(s_clr, 1)
            for m, name in enumerate(("src", "dst", "edge_type_400")):
                for ch, (at, end) in enumerate(CHUNKS):
                    n = min(SCH, (end - at) // EP)
                    sp.dma_start(step_rows[0:n, m, ch, :], io[name][at:at + n * EP].rearrange("(t p) -> t p", p=EP))\
                        .then_inc(s_tabl, 16)
                    if n < SCH:
                        sp.dma_start(step_rows[n:n + 1, m, ch, 0:end - at - n * EP],
                                     io[name][at + n * EP:end].rearrange("(o p) -> o p", o=1)).then_inc(s_tabl, 16)
            for t, lag in ((pair_a, 0), (pair_b, 1)):
                sp.dma_start(t, io["dst"][lag:lag + E - 1].rearrange("(p n) -> p n", p=PAIR_ROWS)).then_inc(s_pair, 16)
            sp.dma_start(res_b[:, :], io["L0_gnn_res"].partition_broadcast(T)).then_inc(s_par, 16)
            for gi in range(NG):
                sp.wait_ge(s_xr, gi + 1)
                sp.dma_start(group_rows(xn_d, gi), xres[:, gi * GT:(gi + 1) * GT, :]).then_inc(s_xn_st, 16)

            def load_qkv(lay):
                for m, name in enumerate(("Wq", "Wk", "Wv")):
                    sp.dma_start(wqkv[:, :, m * D:(m + 1) * D], rows_of(io[f"L0_mix_{name}"][lay])).then_inc(s_wqkv, 16)
                sp.dma_start(ln1p[:, 0, :], columns(io["L0_mix_ln1_g"][lay]),
                             allow_slow_non_contiguous=True).then_inc(s_wqkv, 16)
                sp.dma_start(ln1p[:, 1, :], columns(io["L0_mix_ln1_b"][lay]),
                             allow_slow_non_contiguous=True).then_inc(s_wqkv, 16)

            def load_ff(lay):
                sp.dma_start(wo[:, :, :], rows_of(io["L0_mix_Wo"][lay])).then_inc(s_wff, 16)
                sp.dma_start(w1, rows_of(io["L0_mix_W1"][lay])).then_inc(s_wff, 16)
                sp.dma_start(ln2p[:, 0, :], columns(io["L0_mix_ln2_g"][lay]),
                             allow_slow_non_contiguous=True).then_inc(s_wff, 16)
                sp.dma_start(ln2p[:, 1, :], columns(io["L0_mix_ln2_b"][lay]),
                             allow_slow_non_contiguous=True).then_inc(s_wff, 16)
                sp.dma_start(b1p[:, :], columns(io["L0_mix_b1"][lay]),
                             allow_slow_non_contiguous=True).then_inc(s_wff, 16)
                sp.dma_start(bo_b[:, :], io["L0_mix_bo"][lay].partition_broadcast(T)).then_inc(s_wff, 16)
                sp.dma_start(b2_b[:, :], io["L0_mix_b2"][lay].partition_broadcast(T)).then_inc(s_wff, 16)

            load_qkv(0)
            for lay in range(L):
                g, h = lay // 2, lay % 2
                sp.wait_ge(s_xr, NG * (lay + 1))
                load_ff(lay)

                def store_normed(gi):
                    for j in range(GT):
                        sp.wait_ge(s_hT, gi * GT + (j + 2 + lay * (2 * NT)))
                        sp.dma_start(hT_d[ds(gi, 1), :, j * KC * T:(j + 1) * KC * T].rearrange("o p n -> p (o n)"),
                                     hT[:, j, :, :].rearrange("p c t -> p (c t)")).then_inc(s_hst[j], 16)

                def load_normed(gi):
                    for j in range(GT):
                        sp.wait_ge(s_hst[j], gi * 16 + (32 + 16 * NG * lay))
                    sp.dma_start(flat_qT(hq), hT_d[ds(gi, 1)].rearrange("o p n -> p (o n)")).then_inc(s_hql, 16)
                with sp.Fori(0, NG - 1) as gi:
                    store_normed(gi)
                load_normed(0)
                store_normed(NG - 1)

                def store_qT(gi):
                    sp.wait_ge(s_qTe, gi * GT + (1 + GT + lay * NT))
                    sp.dma_start(qT_d[ds(gi, 1)].rearrange("o p n -> p (o n)"), flat_qT(hT)).then_inc(s_qTst, 16)
                with sp.Fori(0, NG - 1) as gi:
                    sp.wait_ge(s_qp, gi + (1 + lay * NG))
                    load_normed(gi + 1)
                    store_qT(gi)
                sp.wait_ge(s_qp, (lay + 1) * NG)
                sp.dma_start(w2, rows_of(io["L0_mix_W2"][lay])).then_inc(s_w2, 16)
                if h == 0:
                    load_qkv(lay + 1)
                else:
                    for m, name in enumerate(("W_in", "W_out", "W_loop")):
                        sp.dma_start(wg[:, m], rows_of(io[f"L0_gnn_{name}{g + 1}"])).then_inc(s_gw, 16)
                store_qT(NG - 1)
                sp.wait_ge(s_ctx, 1 + (lay + 1) * NG)
                if lay == L - 1:
                    for gi in range(NG):
                        sp.dma_start(kbuf[:, gi * GT:(gi + 1) * GT, :], group_rows(io["x"], gi)).then_inc(s_er, 16)
                with sp.Fori(0, NG) as gi:
                    sp.wait_ge(s_qTst, gi * 16 + (32 + 16 * NG * lay))
                    sp.wait_ge(s_ao, gi * GT + (GT + lay * NT))
                    sp.dma_start(flat_qT(qT), qT_d[ds(gi, 1)].rearrange("o p n -> p (o n)")).then_inc(s_qld, 16)
                if h == 1:
                    if g == 0:
                        sp.wait_ge(s_xn_st, 16 * NG)
                    else:
                        sp.wait_ge(s_h1_st, 16 * NG)
                    sp.dma_start(gb_b[:, :], io[f"L0_gnn_b{g + 1}"].partition_broadcast(T)).then_inc(s_gw, 16)
                    sp.wait_ge(s_tr, (lay + 1) * (2 * NT) + GT)

                    def load_h(it, n):
                        for k in range(n):
                            if not (isinstance(it, int) and it == 0):
                                sp.wait_ge(s_hn, it * SLOTS + (g * NT + k + 1 - SLOTS))
                            sp.dma_start(staged[k][2], (xn_d, h1_d)[g][ds(it * (SLOTS * T) + k * T, T), :])\
                                .then_inc(s_hx[k], 16)

                    def store_h1(gi):
                        sp.wait_ge(s_hn, gi * GT + GT)
                        sp.dma_start(group_rows(h1_d, gi), vbuf[:, ds(gi * GT, GT), :]).then_inc(s_h1_st, 16)
                    load_h(0, SLOTS)
                    load_h(1, SLOTS)
                    with sp.Fori(0, NG - 1) as it:
                        load_h(it + 2, SLOTS)
                        if g == 0:
                            store_h1(it)
                    for it in range(NG + 1, -(-NT // SLOTS)):
                        load_h(it, min(SLOTS, NT - it * SLOTS))
                    if g == 0:
                        store_h1(NG - 1)
                        load_qkv(lay + 1)
            for gi in range(NG):
                sp.wait_ge(s_ez, 1 + (gi + 1) * GT)
                sp.dma_start(group_rows(out, gi), kbuf[:, gi * GT:(gi + 1) * GT, :]).then_inc(s_out, 16)
            sp.wait_ge(s_out, 16 * NG)

        @block.gpsimd
        def _(pool):
            for ch in (1, 3):
                ins = pool.memset(step_rows[:, :, ch, :], 0)
            ins.then_inc(s_clr, 1)
            pool.memset(ones[:, :], 1.0)
            pool.memset(zrow[:, :], 0.0)
            pool.memset(ident[:, :], 0.0)
            pool.memset(quad_first, 0.0)
            pool.memset(xg[:, :, D:AW], 1.0)
            pool.iota(part_i, [[0, 1]], base=0, channel_multiplier=1)
            pool.iota(ramp_i, [[T, NT - 1]], base=T, channel_multiplier=0)
            for ch, (at, _end) in enumerate(CHUNKS):
                pool.iota(enum_i[:, ch, :], [[1, EP]], base=at, channel_multiplier=EP)
            pool.iota(iota_i, [[1, T]], base=0, channel_multiplier=0).then_inc(s_ppool, 1)
            pool.wait_ge(s_ppool, 1)
            pool.affine_select(out=ident[:, :], in_=ident[:, :], compare_op=ALU.not_equal, fill=1.0, base=0,
                               pattern=[[-1, P]], channel_multiplier=1)
            pool.affine_select(out=quad_first, in_=quad_first, compare_op=ALU.not_equal, fill=1.0, base=0,
                               pattern=[[-QUAD, SCH // QUAD], [0, QUAD]], channel_multiplier=1)
            pool.tensor_copy(iota_t[:, :], iota_i).then_inc(s_const, 1)
            pool.memset(acc[:, :, :], 0.0).then_inc(s_zero, 1)

            pool.wait_ge(s_tab, 1)
            for g in range(GL):
                rows, stored = ((xn_d, s_xn_st), (h1_d, s_h1_st))[g]
                pool.wait_ge(stored, 16 * NG)
                with pool.Fori(0, 2 * STEPS // (2 * RING)) as it:
                    for half in range(2):
                        s0 = it * (2 * RING) + (g * 2 * STEPS + half * RING)
                        pool.wait_ge(s_msg, s0 + 1)
                        pool.tensor_copy(idx_now[:, half], idx_tab[:, ds(it * (2 * RING) + half * RING, RING), :])\
                            .then_inc(s_idx, 1)
                        pool.wait_ge(s_idx, it * 2 + (g * 2 * STEPS // RING + half + 1))
                        for k in range(RING):
                            pool.wait_ge(s_seg, s0 + (k + 1))
                            pool.sem_inc(s_claim, 1)
                            pool.indirect_dma_start(
                                xg[:, k, 0:D], None, rows,
                                bass.IndirectOffsetOnAxis(ap=idx_now[:, half, k, 0:1], axis=0)).then_inc(s_edge[k], 16)
                            pool.indirect_dma_start(
                                rg[:, k, :], None, io[f"L0_gnn_rel{g + 1}"],
                                bass.IndirectOffsetOnAxis(ap=idx_now[:, half, k, 1:2], axis=0)).then_inc(s_edge[k], 16)
                hold(pool, s_seg, (g + 1) * (2 * STEPS) + RING)
                with pool.If(pool.value_load(unsorted_i[0:1, 0:1], min_val=0, max_val=1) == 1):
                    for half in range(2):
                        with pool.Fori(0, GHT) as i:
                            n = i + (g * 2 + half) * GHT
                            hold(pool, s_gadd, n * NT + 1)
                            for t, name in ((gsrc, "src"), (gtype, "edge_type_400"), (gdst, "dst")):
                                pool.dma_start(t, io[name][ds(i * T + half * SPLIT * T, T)].rearrange("(p o) -> p o", o=1),
                                               allow_slow_non_contiguous=True).then_inc(s_gidx, 16)
                            hold(pool, s_gidx, n * 48 + 48)
                            pool.indirect_dma_start(
                                xg[0:T, 0, 0:D], None, rows,
                                bass.IndirectOffsetOnAxis(ap=gsrc, axis=0)).then_inc(s_ggat, 16)
                            pool.indirect_dma_start(
                                rg[0:T, 0, :], None, io[f"L0_gnn_rel{g + 1}"],
                                bass.IndirectOffsetOnAxis(ap=gtype, axis=0)).then_inc(s_ggat, 16)

            pool.wait_ge(s_xr, NG * (L + 1))
            for t, src in (
                (mu_w, rows_of(io["L0_gnn_mu_w"])), (sW1, rows_of(io["L0_ffn_sW1"])), (sW2, rows_of(io["L0_ffn_sW2"])),
                (sW3, io["L0_ffn_sW3"]), (eW2, io["L0_ffn_eW2"].rearrange("e p n -> p e n")),
                (eW3[0:EH2], io["L0_ffn_eW3"].rearrange("e p n -> p e n")),
                (eW3[EH2:EH2 + 1], io["L0_ffn_eb3"].rearrange("(o e) n -> o e n", o=1)),
                (gW, rows_of(io["L0_ffn_gW"])), (sb1p, columns(io["L0_ffn_sb1"])),
                (sb2p, columns(io["L0_ffn_sb2"])), (eb1p, io["L0_ffn_eb1"].rearrange("e p -> p e")),
                (eb2p, io["L0_ffn_eb2"].rearrange("e p -> p e")),
                (bo_b[:, :], io["L0_gnn_mu_b"].partition_broadcast(T)),
                (b2_b[:, :], io["L0_ffn_sb3"].partition_broadcast(T)),
                (gateb[:, :], io["L0_ffn_gb"].partition_broadcast(T)),
            ):
                pool.dma_start(t, src, allow_slow_non_contiguous=True).then_inc(s_ew, 16)
            for e in range(NX):
                pool.dma_start(eW1[:, e], rows_of(io["L0_ffn_eW1"][e])).then_inc(s_ew, 16)
            pool.wait_ge(s_er, 16 * NG)
            pool.wait_ge(s_ew, 16 * LAST_LOADS)
            for gi in range(NG):
                z = z_rows(gi)
                pool.tensor_tensor(z, z, xres[:, gi * GT:(gi + 1) * GT, :], ALU.add).then_inc(s_zp, 1)
                pool.wait_ge(s_zp, 2 * gi + 1)
                pool.tensor_tensor(z, z, over_rows(bo_b), ALU.add).then_inc(s_zp, 1)
            for gi in range(NG):
                pool.wait_ge(s_exh, (gi + 1) * GT)
                pool.tensor_tensor(z_rows(gi), z_rows(gi), over_rows(b2_b), ALU.add).then_inc(s_esb, 1)

        @block.vector
        def _(dve):
            start(dve, s_gadd, s_msg, s_acc, s_xa, s_xf, s_db, s_emz, s_ez, s_elr)

            p = Chain(dve, s_pdve)
            dve.memset(lmask[:, :, :], 0.0)
            p(dve.memset(head_mask[:, :], 0.0))
            p.wait()
            for hd in range(P // DH):
                dve.memset(head_mask[hd * DH:(hd + 1) * DH, hd * DH:(hd + 1) * DH], 1.0)
            for e in range(1, NX):
                dve.memset(lmask[:, e, 0:e], 1.0)
            chain = Chain(dve, s_ln)
            for gi in range(NG):
                dve.wait_ge(s_x[gi], 16)
                for t in range(gi * GT, (gi + 1) * GT):
                    chain(dve.bn_stats(stat_all[:, t, :], xres[:, t, :]))
            chain.wait()
            for t in range(NT):
                chain(dve.bn_aggr(mv_all[:, t, :], stat_all[:, t, :]))
            chain.wait()
            inv_sqrt(dve, chain, mv_all[:, :, 1], var_all, seed_all, rstd_all, tmp_all)
            chain.wait()
            chain(dve.scalar_tensor_tensor(shift_all, mv_all[:, :, 0], -1.0, rstd_all, ALU.mult, ALU.mult))
            assert chain.n == LN0

            dve.wait_ge(s_const, 1)
            p(dve.tensor_copy(part[:, :], part_i))
            p(dve.tensor_copy(ramp, ramp_i))
            p(dve.tensor_copy(enum, enum_i))
            dve.wait_ge(s_tabl, 16 * 18)
            for m in (0, 2):
                dve.tensor_copy(step_rows_f[:, m], step_rows[:, m])
            p(dve.tensor_copy(step_rows_f[:, 1], step_rows[:, 1]))
            dve.wait_ge(s_pair, 2 * 16)
            p(dve.tensor_tensor(falls, pair_a, pair_b, ALU.is_gt))
            assert p.n == PD_ROWS
            p.wait()
            p(dve.tensor_reduce(nfall, falls, AX, ALU.add))
            dve.wait_ge(s_ppe, 1)
            p(dve.tensor_copy(first, ps_hid[0][0:SCH, 0:4]))
            p.wait()
            for ch in range(4):
                p(dve.tensor_scalar(reached, ramp, first[:, ch:ch + 1], None, ALU.is_le))
                p.wait()
                p(dve.tensor_reduce(tile_of[:, ch:ch + 1], reached, AX, ALU.add))
                p.wait()
                dve.tensor_scalar(spans[:, ch, :], step_rows_f[:, 1, ch, :], first[:, ch:ch + 1], float(T),
                                  ALU.subtract, ALU.is_ge)
            p(dve.tensor_scalar(base, tile_of, -float(T), None, ALU.mult))
            p.wait()
            p(dve.tensor_tensor(place, first, base, ALU.add))
            p(dve.tensor_reduce(bad, spans, AX, ALU.add))
            p.wait()
            p(dve.tensor_reduce(nspread, bad, AX, ALU.add))
            p(dve.tensor_scalar(tile_of[:, 2:4], tile_of[:, 2:4], float(NT), None, ALU.add))
            p.wait()
            assert p.n == PD_FALLS, p.n
            for ch in range(4):
                key = step_rows_f[:, 1, ch, :]
                p(dve.tensor_scalar(key, key, base[:, ch:ch + 1], None, ALU.add))
                p.wait()
                p(dve.tensor_scalar(dropped, key, float(T), -float(T), ALU.is_ge, ALU.mult))
                p.wait()
                p(dve.tensor_tensor(key, key, dropped, ALU.add))
                p.wait()
                if ch % 2:
                    p(dve.tensor_scalar(dropped, enum[:, ch, :], float(CHUNKS[ch][1]), FAR, ALU.is_ge, ALU.mult))
                    p.wait()
                    p(dve.tensor_tensor(key, key, dropped, ALU.add))
                    p.wait()
            dve.wait_ge(s_ppe, 2)
            p(dve.tensor_scalar(unsorted_f[:, :], ps_hid[1][0:EP, 0:1], 1.0, None, ALU.min))
            p.wait()
            p(dve.tensor_copy(unsorted_i[:, :], unsorted_f[0:1, :]))
            p.wait()
            p(dve.tensor_scalar(unsorted_f[:, :], unsorted_f[:, :], FAR, None, ALU.mult))
            p.wait()
            for m, row_f in ((0, tile_row), (1, place_row)):
                dve.wait_ge(s_ppe, 3 + m)
                p(dve.tensor_copy(row_f, (ps_tr, ps_kv0)[m][0:1, 0:2 * STEPS].rearrange("p (q s) -> p q s", s=QUAD)[:, :, 0]))
            p.wait()
            assert p.n == PD_KEYS, p.n
            p(dve.tensor_copy(row_tab[:, :, 0], tile_row))
            p(dve.tensor_scalar(tile_row, tile_row, 1.0, None, ALU.add))
            p.wait()
            for h in range(2):
                half_row = tile_row[:, h * QUADS:(h + 1) * QUADS]
                p(dve.tensor_scalar(row_tab[:, h * QUADS:(h + 1) * QUADS, 1], half_row, float(h * NT + NT - 1), None, ALU.min))
            for m, tab in ((0, idx_tab[:, :, 0]), (1, key_tab[:, :]), (2, idx_tab[:, :, 1])):
                dve.wait_ge(s_ppe, 5 + m)
                if m == 1:
                    p(dve.tensor_scalar(tab, ps_tab[m][0:EP, 0:2 * STEPS], unsorted_f[:, 0:1], None, ALU.add))
                else:
                    p(dve.tensor_copy(tab, ps_tab[m][0:EP, 0:2 * STEPS]))
            dve.wait_ge(s_ppe, 8)
            for m, op in enumerate((ALU.is_le, ALU.is_gt)):
                p(dve.tensor_scalar(in_tile[:, :, m], ps_kv1[0:T, 0:2 * QUADS], part[:, 0:1], None, op))
            p.wait()
            dve.sem_inc(s_tab, 1)

            dve.wait_ge(s_zero, 1)

            def edge_steps(h, lay, at, per, gi):
                s0 = lay * STEPS + gi * per + at
                slot0 = lay * (STEPS // RING) + gi * (per // RING) + at // RING
                t0 = h * STEPS + gi * per + at
                quad0 = lay * QUADS + gi * (per // QUAD) + at // QUAD
                quad_t0 = h * QUADS + gi * (per // QUAD) + at // QUAD
                done = [0]
                rows = []

                def add(q):
                    dve.wait_ge(s_seg, s0 + (QUAD * (q + 1) + RING))
                    for m in range(2):
                        dve.wait_ge(s_acc, (quad0 + q) * 2 + (m + 3))
                        a = acc[:, ds(rows[2 * q + m], 1), :].rearrange("p o n -> p (o n)")
                        dve.scalar_tensor_tensor(a, ps_seg[q % 2][0:T, 0:AW], in_tile[:, ds(quad_t0 + q, 1), m], a,
                                                 ALU.mult, ALU.add).then_inc(s_acc, 1)

                def go(n):
                    for _ in range(n):
                        k = done[0]
                        done[0] += 1
                        if k % RING == 0:
                            rows.extend(nc.values_load_multi_w_load_instructions(
                                row_tab[0:1, ds(quad_t0 + k // QUAD, RING // QUAD), :].rearrange("p q m -> p (q m)"),
                                engines=(mybir.EngineType.DVE,),
                                min_val=0, max_val=2 * NT - 1, skip_runtime_bounds_check_because="clamped above")[1])
                        dve.wait_ge(s_seg, s0 + (k + 1 + RING - QUAD))
                        dve.tensor_scalar(hot[:, k % QUAD, :], iota_t[:, :], key_tab[:, ds(t0 + k, 1)], None, ALU.is_equal)
                        dve.wait_ge(s_edge[k % RING], slot0 * 32 + 32 * (k // RING + 1))
                        m = xg[:, k % RING, 0:D]
                        dve.tensor_tensor(m, m, rg[:, k % RING, :], ALU.mult).then_inc(s_msg, 1)
                        if k % QUAD == QUAD - 2 and k >= QUAD:
                            add(k // QUAD - 1)

                def end():
                    assert done[0] == per, (done, per)
                    add(per // QUAD - 1)
                return go, end

            def row(gi, j):
                return xres[:, ds(gi * GT + j, 1), :].rearrange("p o d -> p (o d)")

            def stats_A(lay, gi, between=lambda: None):
                chain = Chain(dve, s_ln, (lay * (2 * NG) + gi) * NORM_STEPS + LN0)
                hold(dve, s_xr, lay * NG + gi + 1)
                norm_stats(dve, chain, lambda j: row(gi, j), between)

            stats_A(0, 0)
            hold(dve, s_xr, 1)
            with dve.Fori(0, GL) as g:
                with dve.Fori(0, 2) as h:
                    lay = g * 2 + h
                    dve.memset(kmax[:, :], -3.0e38).then_inc(s_km, 1)

                    def norm_A(gi, j):
                        dve.wait_ge(s_tr, lay * (2 * NT) + gi * GT + (j + 1))
                        norm_rows(dve, j, row(gi, j)).then_inc(s_xh, 1)

                    def group_A(gi, last):
                        tn = (lay * NG + gi) * GT
                        go, end = edge_steps(h, lay, 0, STEPS_A, gi)
                        km = Chain(dve, s_km, lay * KM_STEPS + gi * GT + 1)

                        def k_max(j):
                            km.wait()
                            dve.wait_ge(s_ev, tn + (j + 2))
                            k = kbuf[:, ds(gi * GT + j, 1), :].rearrange("p o d -> p (o d)")
                            km(dve.tensor_tensor(kmax[:, :], kmax[:, :], k, ALU.max))
                        beside = [0]

                        def between():
                            go(1)
                            if beside[0] in (1, 2):
                                k_max(beside[0] - 1)
                            beside[0] += 1
                        go(1)
                        if last:
                            for _ in range(3):
                                between()
                        else:
                            stats_A(lay, gi + 1, between)
                            for j in range(3):
                                norm_A(gi + 1, j)
                        k_max(2)
                        go(1)
                        if not last:
                            norm_A(gi + 1, 3)
                            norm_A(gi + 1, 4)
                        k_max(3)
                        go(2)
                        k_max(4)
                        go(STEPS_A - 7)
                        end()
                    for j in range(GT):
                        norm_A(0, j)
                    with dve.Fori(0, NG - 1) as gi:
                        group_A(gi, False)
                    group_A(NG - 1, True)

                    steps_0 = edge_steps(h, lay, AT_C, STEPS_C, 0)
                    km = Chain(dve, s_km, lay * KM_STEPS + NT + 1)
                    dve.wait_ge(s_kmT, lay + 1)
                    km(dve.tensor_reduce(kmaxT[:, :], ps_ctx[:, 0:KC * T].rearrange("p (c t) -> p c t", c=KC), AX, ALU.max))
                    km.wait()
                    for c in range(KC):
                        ins = dve.tensor_scalar(kdiag[:, c, :], ident[:, :], kmaxT[:, c:c + 1], None, ALU.mult)
                    ins.then_inc(s_kdg, 1)
                    steps_0[0](LEAD)
                    dve.wait_ge(s_kmB, lay + 1)
                    km(dve.memset(v_ones[:, :, :, P:P + 1], 1.0))
                    km(dve.tensor_copy(ksh[:, :], ps_ctx[0:T, 0:D]))
                    hold(dve, s_km, km.base + km.n)
                    def k_shift(gi):
                        k5 = kbuf[:, ds(gi * GT, GT), :]
                        dve.wait_ge(s_ke, lay * NG + gi + 1)
                        dve.tensor_tensor(xh[:, :, :], k5, ksh[:, :].unsqueeze(1).broadcast_to([T, GT, D]), ALU.subtract)\
                            .then_inc(s_ks, 1)

                    def mask_context():
                        dve.wait_ge(s_ctx, (lay + 1) * NG + 1)
                        sums = ps_ctx[:, 0:D + KC].rearrange("p (c n) -> p c n", c=KC)
                        km(dve.reciprocal(rsum[:, :], sums[:, :, P]))
                        km.wait()
                        for c in range(KC):
                            ins = dve.scalar_tensor_tensor(ctxm[:, c, :], sums[:, c, 0:P], rsum[:, c:c + 1],
                                                           head_mask[:, :], ALU.mult, ALU.mult)
                        ins.then_inc(s_cm, 1)

                    def group_C(gi, last, ahead=None):
                        grp = lay * NG + gi
                        go, end = ahead or edge_steps(h, lay, AT_C, STEPS_C, gi)
                        qd = Chain(dve, s_qd, grp * 3)
                        qh = qrow.rearrange("p j (h e) -> p (j h) e", e=DH)
                        qmb = qm[:, :].unsqueeze(2).broadcast_to([T, GT * HEADS, DH])
                        dve.wait_ge(s_qc, grp + 1)
                        qd(dve.tensor_reduce(qm[:, :], qh, AX, ALU.max))
                        if not ahead:
                            go(1)
                        qd.wait()
                        dve.tensor_tensor(qh, qh, qmb, ALU.subtract).then_inc(s_qs, 1)
                        go(1 if ahead else 2)
                        if not last:
                            k_shift(gi + 1)
                        dve.wait_ge(s_qe, grp + 1)
                        qd(dve.tensor_reduce(qm[:, :], qh, AX, ALU.add))
                        qd.wait()
                        qd(dve.reciprocal(qm[:, :], qm[:, :]))
                        go(1)
                        qd.wait()
                        dve.tensor_tensor(qh, qh, qmb, ALU.mult).then_inc(s_qn, 1)
                        go(STEPS_C - 4)
                        end()
                        if last:
                            mask_context()
                    k_shift(0)
                    group_C(0, False, steps_0)
                    with dve.Fori(0, NG - 2) as gi:
                        group_C(gi + 1, False)
                    group_C(NG - 1, True)
                    go, end = edge_steps(h, lay, AT_B0, STEPS_B0, 0)
                    go(2)
                    dve.wait_ge(s_ctT, lay + 1)
                    dve.tensor_copy(ctxT[:, :, :].rearrange("p c d -> p (c d)"), ps_tr[:, 0:D]).then_inc(s_cmT, 1)
                    go(1)
                    dve.wait_ge(s_cw, lay + 1)
                    dve.tensor_copy(cwo[:, :, :].rearrange("p c d -> p (c d)"), ps_ctx[:, :]).then_inc(s_cwr, 1)

                    hold(dve, s_wff, (lay + 1) * (7 * 16))

                    def add_attention(gi, j):
                        dve.wait_ge(s_ao, (lay * NG + gi) * GT + (GT + j + 1))
                        dve.tensor_tensor(row(gi, j), row(gi, j), ps_ao[j % 2][0:T, 0:D], ALU.add).then_inc(s_xa, 1)

                    def stats_B(gi, between=lambda: None, first=False):
                        chain = Chain(dve, s_ln, (lay * (2 * NG) + gi + NG) * NORM_STEPS + LN0)

                        def rows(j):
                            if first:
                                if j == 0:
                                    add_attention(gi, 0)
                                if j + 1 < GT:
                                    add_attention(gi, j + 1)
                                if j in (1, 2):
                                    go(1)
                                hold(dve, s_xa, (lay * NG + gi) * GT + (2 + j))
                            elif j == 0:
                                hold(dve, s_xa, (lay * NG + gi) * GT + (1 + GT))
                            return row(gi, j)
                        norm_stats(dve, chain, rows, between)

                    def norm_B(gi, j):
                        dve.wait_ge(s_tr, lay * (2 * NT) + gi * GT + (NT + j + 1))
                        norm_rows(dve, j, row(gi, j)).then_inc(s_xh, 1)

                    def add_b2(gi):
                        dve.wait_ge(s_xh, (lay * (2 * NG) + gi + (NG + 1)) * GT)
                        x5 = xres[:, ds(gi * GT, GT), :]
                        dve.tensor_tensor(x5, x5, b2_b[:, :].unsqueeze(1).broadcast_to([T, GT, D]), ALU.add).then_inc(s_b2, 1)

                    def add_ffn(gi, j):
                        if j == 0:
                            dve.wait_ge(s_b2, lay * NG + gi + 1)
                        dve.wait_ge(s_fo, (lay * NG + gi) * GT + (j + 2))
                        dve.tensor_tensor(row(gi, j), row(gi, j), ps_out[j % 2][0:T, 0:D], ALU.add).then_inc(s_xf, 1)

                    def group_B(gi, last):
                        go, end = edge_steps(h, lay, AT_B, STEPS_B, gi)
                        n = gi + 1
                        go(11)
                        add_ffn(gi, 0)
                        if not last:
                            for j in range(3):
                                add_attention(n, j)
                        go(5)
                        add_ffn(gi, 1)
                        if last:
                            go(1)
                            stats_A(lay + 1, 0, lambda: go(1))
                        else:
                            add_attention(n, 3)
                            add_attention(n, 4)
                            go(1)
                            stats_B(n, lambda: go(1))
                            for j in range(GT):
                                norm_B(n, j)
                        add_ffn(gi, 2)
                        go(2)
                        if not last:
                            add_b2(n)
                        go(2)
                        add_ffn(gi, 3)
                        end()
                        add_ffn(gi, 4)
                        dve.wait_ge(s_xf, (lay * NG + gi) * GT + (1 + GT))
                        dve.sem_inc(s_xr, 1)

                    rest = [2]

                    def between():
                        if rest[0]:
                            rest[0] -= 1
                            go(1)
                    stats_B(0, between, first=True)
                    for j in range(GT):
                        norm_B(0, j)
                    go(STEPS_B0 - 7)
                    add_b2(0)
                    end()
                    with dve.Fori(0, NG - 1) as gi:
                        group_B(gi, False)
                    group_B(NG - 1, True)

                hold(dve, s_acc, (g + 1) * (4 * QUADS) + 3)
                with dve.If(dve.value_load(unsorted_i[0:1, 0:1], min_val=0, max_val=1) == 1):
                    for half in range(2):
                        dve.tensor_scalar(gedge, part[:, 0:1], float(half * SPLIT * T), None, ALU.add).then_inc(s_gkey, 1)
                        with dve.Fori(0, GHT) as i:
                            n = (g * 2 + half) * GHT + i
                            gk = Chain(dve, s_gkey, n * 5 + (g * 2 + half + 1))
                            hold(dve, s_ggat, n * 32 + 32)
                            gk.wait()
                            gk(dve.tensor_scalar(gkey, gedge, float(HALF), float(N), ALU.is_ge, ALU.mult))
                            gk.wait()
                            gk(dve.tensor_tensor(gkey, gkey, gdst, ALU.add))
                            gk(dve.tensor_scalar(gedge, gedge, float(T), None, ALU.add))
                            gk.wait()
                            gk(dve.tensor_scalar(gkey, gkey, float(-half * N), None, ALU.add))
                            m = xg[0:T, 0, 0:D]
                            gk(dve.tensor_tensor(m, m, rg[0:T, 0, :], ALU.mult))
                            hold(dve, s_gkey, gk.base + gk.n)
                            with dve.Fori(0, NT) as d:
                                q = n * NT + d
                                hold(dve, s_gadd, q + 1)
                                dve.tensor_scalar(hot[0:T, 0, :], iota_t[0:T, :], gkey, None, ALU.is_equal).then_inc(s_ghot, 1)
                                dve.wait_ge(s_ghot, q + 1)
                                dve.tensor_scalar(gkey, gkey, float(-T), None, ALU.add)
                                dve.wait_ge(s_gseg, q + 1)
                                a = acc[:, ds(d + half * NT, 1), :].rearrange("p o n -> p (o n)")
                                dve.tensor_tensor(a, a, ps_seg[0][0:T, 0:AW], ALU.add).then_inc(s_gadd, 1)
                    hold(dve, s_gadd, (g + 1) * (GTILES * NT) + 1)
                dve.wait_ge(s_gw, (g + 1) * (4 * 16))
                dve.wait_ge(s_par, 16)
                dd = Chain(dve, s_dd, g * 3)
                deg = [acc[:, half * NT:(half + 1) * NT, D:AW].rearrange("p t o -> p (t o)") for half in range(2)]
                dd(dve.tensor_tensor(norm, deg[0], deg[1], ALU.add))
                dd.wait()
                dd(dve.tensor_scalar(norm, norm, 1.0, None, ALU.max))
                dd.wait()
                dd(dve.reciprocal(norm, norm))
                hold(dve, s_dd, dd.base + dd.n)

                def at_tile(b, t):
                    return b[:, ds(t, 1), :].rearrange("p o n -> p (o n)")

                def scale(t, j):
                    dve.wait_ge(s_dtr, g * NT + t + 1)
                    for half in range(2):
                        ins = dve.tensor_scalar(staged[j % SLOTS][half], at_tile(acc, t + half * NT)[:, 0:D],
                                                norm[:, ds(t, 1)], None, ALU.mult)
                    ins.then_inc(s_sc, 1)

                def update(t, j):
                    dve.wait_ge(s_dt, g * NT + t + 1)
                    v = at_tile(vbuf, t)
                    dve.scalar_tensor_tensor(v, v, res_b[:, 0:1], staged[j % SLOTS][2], ALU.mult, ALU.add).then_inc(s_hn, 1)

                def dense_tile(t, j, first, last):
                    if not last or last + 2 < NT:
                        scale(t + 2, j + 2)
                    dve.wait_ge(s_sc, g * NT + t + 1)
                    for half in range(2):
                        dve.tensor_scalar(at_tile(acc, t + half * NT), ones[0:T, 0:1].broadcast_to([T, AW]), 0.0, None,
                                          ALU.mult)
                    dve.wait_ge(s_dy, g * NT + t + 3)
                    dve.tensor_tensor(at_tile(vbuf, t), ps_out[j % 2][0:T, 0:D], gb_b[:, :], ALU.add).then_inc(s_db, 1)
                    if not first:
                        update(t - 1, j - 1)
                scale(0, 0)
                scale(1, 1)
                dense_tiles(dve, dense_tile)
                update(NT - 1, NT - 1)
                hold(dve, s_hn, (g + 1) * NT)

            dve.wait_ge(s_ew, 16 * LAST_LOADS)
            dve.memset(acc[EH2:EH2 + 1, 0:2, 0:2 * T], 1.0).then_inc(s_ed, 1)

            def z_row(t):
                return kbuf[:, ds(t, 1), :].rearrange("p o d -> p (o d)")

            def stage_h2(gi):
                dve.wait_ge(s_etr, gi * GT + GT)
                dve.tensor_copy(q5[:, :, :], vbuf[:, ds(gi * GT, GT), :]).then_inc(s_erow, 1)

            def group_z(gi, last):
                ed = Chain(dve, s_ed, gi * NORM_STEPS + 1)

                def stats(j):
                    hold(dve, s_emz, gi * GT + (j + 2))
                    ed(dve.bn_stats(stat[:, j, :], z_row(gi * GT + j)))
                dve.wait_ge(s_zp, gi * 2 + 2)
                for j in range(GT):
                    dve.wait_ge(s_emu, gi * GT + (j + 2))
                    z = z_row(gi * GT + j)
                    dve.tensor_tensor(z, z, ps_out[j % 2][0:T, 0:D], ALU.add).then_inc(s_emz, 1)
                    if j:
                        stats(j - 1)
                if not last:
                    stage_h2(gi + 1)
                stats(GT - 1)
                hold(dve, ed.s, ed.base + ed.n)
                for j in range(GT):
                    ed(dve.bn_aggr(mv[:, j, :], stat[:, j, :]))
                ed.wait()
                inv_sqrt(dve, ed, mv[:, :, 1], var[:, :], seed[:, :], rstd[:, :], tmp[:, :])
                hold(dve, ed.s, ed.base + ed.n)
                for j in range(GT):
                    dve.wait_ge(s_ext, gi * GT + (j + 1))
                    norm_rows(dve, j, z_row(gi * GT + j)).then_inc(s_exh, 1)

            def logits(gi):
                dve.wait_ge(s_elg, gi + 1)
                dve.tensor_tensor(lg[:, ds(gi * GT, GT), :], ps_seg[1][0:T, 0:GT * NX].rearrange("p (j e) -> p j e", e=NX),
                                  gateb[:, :].unsqueeze(1).broadcast_to([T, GT, NX]), ALU.add).then_inc(s_elr, 1)
            stage_h2(0)
            group_z(0, False)
            with dve.Fori(0, NG - 2) as it:
                group_z(it + 1, False)
                logits(it)
            group_z(NG - 1, True)
            logits(NG - 2)
            logits(NG - 1)
            ed = Chain(dve, s_ed, NG * NORM_STEPS + 1)

            def spread(v):
                return v.unsqueeze(2).broadcast_to([T, NT, NX])
            dve.wait_ge(s_elr, NG + 1)
            ed(dve.tensor_reduce(gone, lg, AX, ALU.max))
            ed.wait()
            dve.tensor_tensor(lg, lg, spread(gone), ALU.subtract).then_inc(s_egx, 1)
            dve.wait_ge(s_ege, 1)
            ed(dve.tensor_reduce(gone, lg, AX, ALU.add))
            ed.wait()
            ed(dve.reciprocal(gone, gone))
            ed.wait()
            ed(dve.tensor_tensor(gate, lg, spread(gone), ALU.mult))
            ed.wait()
            ed(dve.tensor_reduce(gone, gate, AX, ALU.max))
            ed.wait()
            dve.tensor_tensor(gex, gate, spread(gone), ALU.subtract).then_inc(s_egx, 1)
            g_own = gate.unsqueeze(3).broadcast_to([T, NT, NX, NX])
            g_oth = gate.unsqueeze(2).broadcast_to([T, NT, NX, NX])
            ed(dve.tensor_tensor(beat, g_oth, g_own, ALU.is_gt))
            ed(dve.tensor_tensor(beat2, g_oth, g_own, ALU.is_equal))
            ed.wait()
            ed(dve.tensor_tensor(beat2, beat2, lmask[:, :, :].unsqueeze(1).broadcast_to([T, NT, NX, NX]), ALU.mult))
            ed.wait()
            ed(dve.tensor_tensor(beat, beat, beat2, ALU.add))
            ed.wait()
            ed(dve.tensor_reduce(lg, beat, AX, ALU.add))
            ed.wait()
            ed(dve.tensor_scalar(lg, lg, 1.5, None, ALU.is_lt))
            ed.wait()
            dve.wait_ge(s_ege, 2)
            ed(dve.tensor_tensor(gate, gex, lg, ALU.mult))
            ed.wait()
            ed(dve.tensor_reduce(gone, gate, AX, ALU.add))
            ed.wait()
            ed(dve.reciprocal(gone, gone))
            ed.wait()
            ed(dve.tensor_tensor(gate, gate, spread(gone), ALU.mult))
            ed.wait()
            hold(dve, s_esb, NG)
            ED0 = ed.base + ed.n
            with dve.Fori(0, NT) as t:
                ed = Chain(dve, s_ed, t * NX + ED0)
                dve.wait_ge(s_eo, t + 2)
                z = z_row(t)
                ed(dve.tensor_tensor(z, z, ps_kv0[0:T, 0:D], ALU.add))
                for e in range(NX):
                    ed.wait()
                    o = (ps_kv0[0:T, D:2 * D], ps_kv1[0:T, 0:D], ps_kv1[0:T, D:2 * D], ps_seg[0][0:T, 0:D])[e]
                    ins = dve.scalar_tensor_tensor(z, o, gate[:, ds(t, 1), e], z, ALU.mult, ALU.add)
                    if e < NX - 1:
                        ed(ins)
                ins.then_inc(s_ez, 1)

        @block.scalar
        def _(act):
            start(act, s_hT, s_ev, s_qTe, s_gel, s_dT, s_eT, s_exT, s_e1a, s_e2a, s_ke, s_qTst, *s_hst)

            def copy(dst, src):
                return act.activation(dst, src, ACT.Identity)

            def dense_tanh(g, t):
                act.wait_ge(s_db, g * NT + t + 3)
                row = vbuf[:, ds(t, 1), :].rearrange("p o d -> p (o d)")
                act.activation(row, row, ACT.Tanh).then_inc(s_dt, 1)

            def norm_out(j, u, par, stored=None):
                act.wait_ge(s_tr, u + (GT + j + 1))
                if par is ln1p:
                    act.wait_ge(s_hst[j], stored * 16 + 16)
                for c in range(KC):
                    ins = act.activation(hT[:, j, c, :], ps_turn[j % 2][:, c * T:(c + 1) * T], ACT.Identity,
                                         bias=par[:, 1, c:c + 1], scale=par[:, 0, c:c + 1])
                ins.then_inc(s_hT, 1)

            act.wait_ge(s_ln, LN0)
            for t in range(NT):
                ins = act.activation(xres[:, t, :], xres[:, t, :], ACT.Identity, bias=shift_all[:, t:t + 1],
                                     scale=rstd_all[:, t:t + 1])
                if t % GT == GT - 1:
                    ins.then_inc(s_xr, 1)
            with act.Fori(0, GL) as g:
                with act.Fori(0, 2) as h:
                    lay = g * 2 + h
                    act.wait_ge(s_wqkv, (lay + 1) * (5 * 16))
                    def group_A(gi, last):
                        grp = lay * NG + gi
                        tn = grp * GT
                        u = lay * (2 * NT) + gi * GT
                        for j in range(GT):
                            if j + 1 < GT:
                                norm_out(j + 1, u, ln1p, grp)
                            act.wait_ge(s_mm, tn + (j + 1))
                            kv = ps_kv[j % 2]
                            copy(kbuf[:, ds(gi * GT + j, 1), :].rearrange("p o d -> p (o d)"), kv[0:T, 0:D])
                            copy(v_ones[:, ds(gi * GT + j, 1), :, 0:P].rearrange("p o c d -> p (o c) d"),
                                 kv[0:T, D:2 * D].rearrange("p (c d) -> p c d", c=KC)).then_inc(s_ev, 1)
                        if not last:
                            norm_out(0, u + GT, ln1p, grp + 1)
                    norm_out(0, lay * (2 * NT), ln1p, lay * NG)
                    with act.Fori(0, NG - 1) as gi:
                        group_A(gi, False)
                    group_A(NG - 1, True)
                    for j in range(GT):
                        act.wait_ge(s_hst[j], (lay + 1) * (NG * 16) + 16)
                    def k_exp(gi):
                        grp = lay * NG + gi
                        act.wait_ge(s_ks, grp + 1)
                        act.wait_ge(s_ctx, grp + 1)
                        act.activation(q5[:, :, :], xh[:, :, :], ACT.Exp, scale=SCALE).then_inc(s_ke, 1)

                    def group_C(gi, last):
                        grp = lay * NG + gi
                        act.wait_ge(s_qs, grp + 1)
                        act.activation(qrow, qrow, ACT.Exp, scale=SCALE).then_inc(s_qe, 1)
                        act.wait_ge(s_qTst, grp * 16 + 16)
                        for j in range(GT):
                            act.wait_ge(s_qtr, grp * GT + (j + 1))
                            copy(hT[:, j, :, :].rearrange("p c t -> p (c t)"), ps_out[j % 2][:, 0:KC * T]).then_inc(s_qTe, 1)
                        if not last:
                            q_rows(gi + 1)
                            k_exp(gi + 1)

                    def q_rows(gi):
                        act.wait_ge(s_qp, lay * NG + gi + 1)
                        for a, bank_a in enumerate(ps_q):
                            n = min(2, GT - 2 * a)
                            ins = copy(qrow[:, 2 * a:2 * a + n, :].rearrange("p j d -> p (j d)"), bank_a[0:T, 0:n * D])
                        ins.then_inc(s_qc, 1)
                    q_rows(0)
                    k_exp(0)
                    with act.Fori(0, NG - 1) as gi:
                        group_C(gi, False)
                    group_C(NG - 1, True)
                    act.wait_ge(s_wff, (lay + 1) * (7 * 16))
                    act.wait_ge(s_qTst, (lay + 1) * (NG * 16) + 16)
                    for j in range(GT):
                        norm_out(j, lay * (2 * NT) + NT, ln2p)

                    def gelu_group(gi):
                        tn = (lay * NG + gi) * GT
                        for j in range(GT):
                            for hf in range(2):
                                if hf == 0:
                                    act.wait_ge(s_fo, tn + (j if j else 1))
                                act.wait_ge(s_up, tn * 2 + (2 * j + hf + 1))
                                for f in range(FC // 2):
                                    ff = hf * (FC // 2) + f
                                    ins = act.activation(gT[:, j % 2, ff, :], ps_hid[hf][:, f * T:(f + 1) * T],
                                                         ACT.Gelu, bias=b1p[:, ff:ff + 1])
                                ins.then_inc(s_gel, 1)
                    with act.Fori(0, NG - 1) as gi:
                        gelu_group(gi)
                        for j in range(GT):
                            norm_out(j, lay * (2 * NT) + (gi + 1) * GT + NT, ln2p)
                    gelu_group(NG - 1)
                def dense_tile(t, j, first, last):
                    act.wait_ge(s_dtr, g * NT + t + (SLOTS + 1))
                    act.wait_ge(s_dy, g * NT + t + 1)
                    copy(gT[:, j % 2, 0:4, :].rearrange("p f t -> p (f t)"), ps_hid[0][:, 0:4 * T])
                    copy(gT[:, j % 2, 4:6, :].rearrange("p f t -> p (f t)"), ps_hid[1][:, 0:2 * T]).then_inc(s_dT, 1)
                    if not first:
                        dense_tanh(g, t - 1)
                dense_tiles(act, dense_tile)
                dense_tanh(g, NT - 1)

            act.wait_ge(s_ew, 16 * LAST_LOADS)
            act.wait_ge(s_ed, 1)

            def h2_T(gi):
                for j in range(GT):
                    act.wait_ge(s_etr, gi * GT + (GT + j + 1))
                    copy(hT[:, j, :, :].rearrange("p c t -> p (c t)"), ps_turn[j % 2][:, 0:KC * T]).then_inc(s_eT, 1)

            def z_T(gi):
                for j in range(GT):
                    act.wait_ge(s_ext, gi * GT + (GT + j + 1))
                    copy(gT[:, j % 2, 0:KC, :].rearrange("p c t -> p (c t)"), ps_hid[j % 2][:, 0:KC * T])
                    copy(hT_all[:, ds(gi * GT + j, 1), :].rearrange("p o n -> p (o n)"), ps_hid[j % 2][:, 0:KC * T])\
                        .then_inc(s_exT, 1)
            h2_T(0)
            with act.Fori(0, NG - 1) as gi:
                h2_T(gi + 1)
                z_T(gi)
            z_T(NG - 1)
            for m in range(2):
                act.wait_ge(s_egx, m + 1)
                gates = (lg, gex)[m]
                act.activation(gates, gates, ACT.Exp).then_inc(s_ege, 1)
            with act.Fori(0, NT) as t:
                act.wait_ge(s_e1, t + 1)
                for f in range(KC):
                    act.activation(gT[:, 0, f, :], ps_hid[0][:, f * T:(f + 1) * T], ACT.Relu, bias=sb1p[:, f:f + 1])
                for e in range(NX):
                    ins = act.activation(gT[:, 0, KC + e, :], ps_hid[1][:, e * T:(e + 1) * T], ACT.Relu, bias=eb1p[:, e:e + 1])
                ins.then_inc(s_e1a, 1)
                act.wait_ge(s_e2, t + 1)
                act.wait_ge(s_eo, t + 1)
                act.activation(gT[:, 1, 0, :], ps_tr[:, 0:T], ACT.Relu, bias=sb2p[:, 0:1])
                for e in range(NX):
                    ins = act.activation(e2T_of(e)[0:EH2], ps_ctx[0:EH2, e * T:(e + 1) * T], ACT.Relu, bias=eb2p[:, e:e + 1])
                ins.then_inc(s_e2a, 1)

        @block.tensor
        def _(pe):
            start(pe, s_seg, s_tr, s_ao, s_fo, s_dy, s_dtr, s_emu, s_ctx, s_etr, s_ext, s_eo)

            pe.wait_ge(s_const, 1)
            pe.wait_ge(s_pdve, PD_ROWS)
            pe.matmul(ps_hid[0][0:SCH, 0:4], quad_first, step_rows_f[:, 1, :, 0], start=True, stop=True).then_inc(s_ppe, 1)
            pe.wait_ge(s_pdve, PD_FALLS)
            pe.matmul(ps_hid[1][:, 0:1], ones[0:PAIR_ROWS, :], nfall, start=True, stop=False)
            pe.matmul(ps_hid[1][:, 0:1], ones[0:SCH, :], nspread, start=False, stop=True).then_inc(s_ppe, 1)
            for m, (bank_m, rows) in enumerate(((ps_tr, tile_of), (ps_kv0, place))):
                for ch in range(4):
                    ins = pe.transpose(bank_m[0:1, ch * SCH:(ch + 1) * SCH], rows[:, ch:ch + 1], ident[0:SCH, 0:SCH])
                ins.then_inc(s_ppe, 1)
            pe.wait_ge(s_pdve, PD_KEYS)
            for m in range(3):
                for ch in range(4):
                    ins = pe.transpose(ps_tab[m][0:EP, ch * SCH:(ch + 1) * SCH], step_rows_f[:, m, ch, :], ident[0:SCH, 0:SCH])
                ins.then_inc(s_ppe, 1)
            pe.matmul(ps_kv1[0:T, 0:2 * QUADS], ones[0:1, 0:T], place_row, start=True, stop=True).then_inc(s_ppe, 1)

            def edge_steps(lay, at, per, gi):
                s0 = lay * STEPS + gi * per + at
                quad0 = lay * QUADS + gi * (per // QUAD) + at // QUAD
                done = [0]

                def go(n):
                    for _ in range(n):
                        k = done[0]
                        done[0] += 1
                        q = k // QUAD
                        if k % QUAD == 0:
                            pe.wait_ge(s_acc, (quad0 + q) * 2 + 1)
                        pe.wait_ge(s_msg, s0 + (k + 2 + RING))
                        pe.matmul(ps_seg[q % 2][0:T, 0:AW], hot[:, k % QUAD, :], xg[:, k % RING, :],
                                  start=k % QUAD == 0, stop=k % QUAD == QUAD - 1).then_inc(s_seg, 1)
                return go

            def turn(j, u):
                pe.wait_ge(s_hT, u + (j if j else 1))
                pe.wait_ge(s_xh, u + (j + 1))
                transpose_rows(pe, ps_turn[j % 2], xh[:, j, :]).then_inc(s_tr, 1)

            with pe.Fori(0, GL) as g:
                with pe.Fori(0, 2) as h:
                    lay = g * 2 + h
                    pe.wait_ge(s_wqkv, (lay + 1) * (5 * 16))
                    def group_A(gi, last):
                        tn = (lay * NG + gi) * GT
                        u = lay * (2 * NT) + gi * GT
                        go = edge_steps(lay, 0, STEPS_A, gi)
                        for j in range(GT):
                            if j + 1 < GT:
                                turn(j + 1, u)
                            pe.wait_ge(s_hT, u + (j + 2))
                            pe.wait_ge(s_ev, tn + (j if j else 1))
                            for c in range(KC):
                                ins = pe.matmul(ps_kv[j % 2][0:T, :], hT[:, j, c, :], wqkv[:, c, D:], start=c == 0,
                                                stop=c == KC - 1)
                            ins.then_inc(s_mm, 1)
                            go(1)
                        if not last:
                            turn(0, u + GT)
                        go(STEPS_A - GT)
                    turn(0, lay * (2 * NT))
                    with pe.Fori(0, NG - 1) as gi:
                        group_A(gi, False)
                    group_A(NG - 1, True)
                    def q_group(gi, j, n):
                        if j == 0:
                            pe.wait_ge(s_hql, (lay * NG + gi) * 16 + 16)
                        for a in range(j, j + n):
                            for c in range(KC):
                                ins = pe.matmul(ps_q[a // 2][0:T, (a % 2) * D:(a % 2 + 1) * D], hq[:, a, c, :],
                                                wqkv[:, c, 0:D], start=c == 0, stop=c == KC - 1)
                        if j + n == GT:
                            ins.then_inc(s_qp, 1)
                    pe.wait_ge(s_km, lay * KM_STEPS + NT + 1)
                    transpose_rows(pe, ps_ctx, kmax[:, :]).then_inc(s_kmT, 1)
                    steps_0 = edge_steps(lay, AT_C, STEPS_C, 0)
                    q_group(0, 0, 2)
                    pe.wait_ge(s_kdg, lay + 1)
                    for c in range(KC):
                        ins = pe.matmul(ps_ctx[0:T, c * P:(c + 1) * P], ones[:, 0:T], kdiag[:, c, :], start=True, stop=True)
                    ins.then_inc(s_kmB, 1)
                    steps_0(LEAD)
                    q_group(0, 2, GT - 2)
                    pe.wait_ge(s_km, lay * KM_STEPS + NT + 4)
                    pe.matmul(ps_ctx[:, 0:D + KC], ones[0:1, :], zrow[:, :], start=True, stop=False, skip_group_check=True)
                    def group_C(gi, last, ahead=None):
                        tn = (lay * NG + gi) * GT
                        go = ahead or edge_steps(lay, AT_C, STEPS_C, gi)

                        def context(j):
                            for c in range(KC):
                                vj = v_ones[:, ds(gi * GT + j, 1), c, :].rearrange("p o d -> p (o d)")
                                ins = pe.matmul(ps_ctx[:, c * (P + 1):(c + 1) * (P + 1)], q5[:, j, c * P:(c + 1) * P], vj,
                                                start=False, stop=True, skip_group_check=True)
                            return ins
                        if not last:
                            pe.wait_ge(s_qc, lay * NG + gi + 1)
                        for j in range(0, GT, 2):
                            if not last:
                                q_group(gi + 1, j, min(2, GT - j))
                            if not ahead or j >= 2 * LEAD:
                                go(1)
                        pe.wait_ge(s_ke, lay * NG + gi + 2)
                        context(0)
                        go(1)
                        pe.wait_ge(s_qn, lay * NG + gi + 1)
                        for j in range(GT):
                            pe.wait_ge(s_qTe, tn + (j if j else 1))
                            transpose_rows(pe, ps_out[j % 2], qrow[:, j, :]).then_inc(s_qtr, 1)
                        go(STEPS_C - 4)
                        for j in range(1, GT):
                            ins = context(j)
                        ins.then_inc(s_ctx, 1)
                    group_C(0, False, steps_0)
                    with pe.Fori(0, NG - 2) as gi:
                        group_C(gi + 1, False)
                    group_C(NG - 1, True)
                    pe.wait_ge(s_wff, (lay + 1) * (7 * 16))
                    pe.wait_ge(s_cm, lay + 1)
                    for c in range(KC):
                        ins = pe.transpose(ps_tr[:, c * P:(c + 1) * P], ctxm[:, c, :], ident[:, :])
                    ins.then_inc(s_ctT, 1)
                    go = edge_steps(lay, AT_B0, STEPS_B0, 0)
                    go(2)
                    pe.wait_ge(s_cmT, lay + 1)
                    for c in range(KC):
                        ins = pe.matmul(ps_ctx[:, c * D:(c + 1) * D], ctxT[:, c, :], wo[:, c, :], start=True, stop=c > 0)
                        if c == 0:
                            pe.matmul(ps_ctx[:, 0:D], head_mask[0:1, :], bo_b[0:1, :], start=False, stop=True)
                    ins.then_inc(s_cw, 1)
                    go(1)
                    pe.wait_ge(s_w2, (lay + 1) * 16)
                    pe.wait_ge(s_cwr, lay + 1)

                    def attend(gi, j):
                        grp = lay * NG + gi
                        pe.wait_ge(s_qld, grp * 16 + 16)
                        pe.wait_ge(s_xa, grp * GT + (j if j else 1))
                        for c in range(KC):
                            ins = pe.matmul(ps_ao[j % 2][0:T, 0:D], qT[:, j, c, :], cwo[:, c, :], start=c == 0, stop=c == KC - 1)
                        ins.then_inc(s_ao, 1)

                    def turn_B(gi, j):
                        turn(j, lay * (2 * NT) + gi * GT + NT)

                    def group_B(gi, last):
                        tn = (lay * NG + gi) * GT
                        u = lay * (2 * NT) + gi * GT + NT
                        go = edge_steps(lay, AT_B, STEPS_B, gi)

                        def up(j):
                            for hf in range(2):
                                if hf == 0:
                                    pe.wait_ge(s_hT, u + (j + 2))
                                pe.wait_ge(s_gel, tn * 2 + (2 * j + hf + 1))
                                for f in range(FC // 2):
                                    ff = hf * (FC // 2) + f
                                    for c in range(KC):
                                        ins = pe.matmul(ps_hid[hf][:, f * T:(f + 1) * T], w1[:, c, ff * P:(ff + 1) * P],
                                                        hT[:, j, c, :], start=c == 0, stop=c == KC - 1)
                                ins.then_inc(s_up, 1)
                                go(2)

                        def down(j):
                            pe.wait_ge(s_xf, tn + (j if j else 1))
                            pe.wait_ge(s_gel, tn * 2 + (2 * j + 4))
                            for f in range(FC):
                                ins = pe.matmul(ps_out[j % 2][0:T, 0:D], gT[:, j % 2, f, :], w2[:, f, :],
                                                start=f == 0, stop=f == FC - 1)
                            ins.then_inc(s_fo, 1)
                        n = gi + 1
                        up(0)
                        for j in range(GT):
                            if j + 1 < GT:
                                up(j + 1)
                            if not last and j == 3:
                                turn_B(n, 0)
                                turn_B(n, 1)
                            if not last and j == 4:
                                turn_B(n, 2)
                                turn_B(n, 3)
                            down(j)
                            if not last and j == 0:
                                pe.wait_ge(s_hT, u + (GT + 1))
                                for a in range(3):
                                    attend(n, a)
                            if not last and j == 1:
                                attend(n, 3)
                                attend(n, 4)
                            if j < GT - 1:
                                go(1)
                        if not last:
                            turn_B(n, 4)

                    for j in range(GT):
                        attend(0, j)
                        if j >= 3:
                            go(1)
                    go(1)
                    for j in range(GT):
                        turn_B(0, j)
                    go(STEPS_B0 - 6)
                    with pe.Fori(0, NG - 1) as gi:
                        group_B(gi, False)
                    group_B(NG - 1, True)
                hold(pe, s_acc, (g + 1) * (4 * QUADS) + 3)
                with pe.If(pe.value_load(unsorted_i[0:1, 0:1], min_val=0, max_val=1) == 1):
                    with pe.Fori(0, GTILES * NT) as q:
                        pe.wait_ge(s_ghot, g * (GTILES * NT) + q + 1)
                        pe.matmul(ps_seg[0][0:T, 0:AW], hot[0:T, 0, :], xg[0:T, 0, :], start=True, stop=True).then_inc(s_gseg, 1)
                pe.wait_ge(s_gw, (g + 1) * (4 * 16))

                def turn_sums(t, j):
                    k = j % SLOTS
                    uses = len(range(k, NT, SLOTS))
                    pe.wait_ge(s_dT, g * NT + t + 1)
                    pe.wait_ge(s_sc, g * NT + t + 1)
                    pe.wait_ge(s_hx[k], g * (uses * 16) + (t - k) * (16 // SLOTS) + 16)
                    for m in range(2):
                        transpose_rows(pe, ps_hid[0][:, m * KC * T:(m + 1) * KC * T], staged[k][m])
                    transpose_rows(pe, ps_hid[1], staged[k][2]).then_inc(s_dtr, 1)

                def dense_tile(t, j, first, last):
                    pe.wait_ge(s_dT, g * NT + t + 2)
                    if not last or last + 1 < NT:
                        turn_sums(t + 1, j + 1)
                    pe.wait_ge(s_db, g * NT + t + 1)
                    for m in range(3):
                        for c in range(KC):
                            ins = pe.matmul(ps_out[j % 2][0:T, 0:D], gT[:, j % 2, m * KC + c, :], wg[:, m, c, :],
                                            start=m == 0 and c == 0, stop=m == 2 and c == KC - 1)
                    ins.then_inc(s_dy, 1)
                turn_sums(0, 0)
                dense_tiles(pe, dense_tile)

            pe.wait_ge(s_ew, 16 * LAST_LOADS)
            pe.wait_ge(s_hn, GL * NT)
            def mu_group(gi):
                dn = gi * GT

                def turn_h2(j):
                    pe.wait_ge(s_eT, dn + (j if j else 1))
                    pe.wait_ge(s_erow, gi + 1)
                    transpose_rows(pe, ps_turn[j % 2], q5[:, j, :]).then_inc(s_etr, 1)
                turn_h2(0)
                for j in range(GT):
                    if j + 1 < GT:
                        turn_h2(j + 1)
                    pe.wait_ge(s_eT, dn + (j + 2))
                    pe.wait_ge(s_emz, dn + (j if j else 1))
                    for c in range(KC):
                        ins = pe.matmul(ps_out[j % 2][0:T, 0:D], hT[:, j, c, :], mu_w[:, c, :], start=c == 0, stop=c == KC - 1)
                    ins.then_inc(s_emu, 1)

            def logit_group(gi):
                dn = gi * GT

                def turn_z(j):
                    pe.wait_ge(s_exT, dn + (j if j else 1))
                    pe.wait_ge(s_exh, dn + (j + 1))
                    transpose_rows(pe, ps_hid[j % 2], xh[:, j, :]).then_inc(s_ext, 1)
                turn_z(0)
                for j in range(GT):
                    if j + 1 < GT:
                        turn_z(j + 1)
                    if j == 0:
                        pe.wait_ge(s_elr, gi + 1)
                    pe.wait_ge(s_exT, dn + (j + 2))
                    for c in range(KC):
                        ins = pe.matmul(ps_seg[1][0:T, j * NX:(j + 1) * NX], gT[:, j % 2, c, :], gW[:, c, :], start=c == 0,
                                        stop=c == KC - 1)
                ins.then_inc(s_elg, 1)
            mu_group(0)
            with pe.Fori(0, NG - 1) as gi:
                mu_group(gi + 1)
                logit_group(gi)
            logit_group(NG - 1)

            def layer_1(t):
                x = hT_all[:, ds(t, 1), :].rearrange("p o (c t) -> p (o c) t", c=KC)
                pe.wait_ge(s_e1a, t + 1)
                for f in range(KC):
                    for c in range(KC):
                        pe.matmul(ps_hid[0][:, f * T:(f + 1) * T], sW1[:, c, f * P:(f + 1) * P], x[:, c, :],
                                  start=c == 0, stop=c == KC - 1)
                for e in range(NX):
                    for c in range(KC):
                        ins = pe.matmul(ps_hid[1][:, e * T:(e + 1) * T], eW1[:, e, c, :], x[:, c, :],
                                        start=c == 0, stop=c == KC - 1)
                ins.then_inc(s_e1, 1)

            def layer_2(t):
                pe.wait_ge(s_e2a, t + 1)
                pe.wait_ge(s_e1a, t + 2)
                for c in range(KC):
                    pe.matmul(ps_tr[:, 0:T], sW2[:, c, :], gT[:, 0, c, :], start=c == 0, stop=c == KC - 1)
                for e in range(NX):
                    ins = pe.matmul(ps_ctx[0:EH2, e * T:(e + 1) * T], eW2[:, e, :], gT[:, 0, KC + e, :], start=True, stop=True)
                ins.then_inc(s_e2, 1)

            def layer_3(t):
                pe.wait_ge(s_e2a, t + 2)
                pe.wait_ge(s_ez, t + 1)
                pe.matmul(ps_kv0[0:T, 0:D], gT[:, 1, 0, :], sW3, start=True, stop=True)
                for e in range(NX):
                    o = (ps_kv0[0:T, D:2 * D], ps_kv1[0:T, 0:D], ps_kv1[0:T, D:2 * D], ps_seg[0][0:T, 0:D])[e]
                    ins = pe.matmul(o, e2T_of(e), eW3[0:EH2 + 1, e, :], start=True, stop=True)
                ins.then_inc(s_eo, 1)
            layer_1(0)
            layer_2(0)
            with pe.Fori(0, NT - 1) as t:
                layer_1(t + 1)
                layer_3(t)
                layer_2(t + 1)
            layer_3(NT - 1)

        assert not START, "free buffers not handed out"


def kernel(**inputs):
    import concourse.bacc as bacc
    from concourse.bass_utils import run_bass_kernel_spmd

    nc = bacc.Bacc("TRN2", target_bir_lowering=False, num_devices=1)
    arrays, io = {}, {}
    for name, value in inputs.items():
        a = np.ascontiguousarray(value)
        arrays[name] = a
        io[name] = nc.dram_tensor(name, a.shape, mybir.dt.from_np(a.dtype), kind="ExternalInput").ap()
    out = nc.dram_tensor("out", inputs["x"].shape, F32, kind="ExternalOutput").ap()
    build(nc, io, out)
    return run_bass_kernel_spmd(nc, [arrays], core_ids=[0]).results[0]["out"]
```
